# Optimizing a Trainium2 kernel written in Bass

```python
import numpy as np
import jax
import jax.numpy as jnp

def _softmax(x, axis=-1):
    return jax.nn.softmax(x, axis=axis)

def _gelu(x):
    return jax.nn.gelu(x, approximate=True)

def _silu(x):
    return jax.nn.silu(x)

def _sigmoid(x):
    return jax.nn.sigmoid(x)

def _layernorm(x, axis=-1, eps=1e-05):
    m = jnp.mean(x, axis=axis, keepdims=True)
    v = jnp.var(x, axis=axis, keepdims=True)
    return (x - m) / jnp.sqrt(v + eps)

def _scatter_add(tgt, idx, src, axis=0):
    return tgt.at[idx].add(src)

def _segment_sum(src, seg, n):
    return jax.ops.segment_sum(src, seg, n)
kernel_name = 'mk_decoder_postln_d1_seqx_r8_5a9664'

def setup_inputs(seed: int=0):
    np.random.seed(seed)
    _w = jnp.asarray

    def _rec_inputs():
        import jax
        import jax.numpy as jnp
        _rk = jax.random.key(seed)
        x = -0.0002928 + 1 * jax.random.normal(jax.random.fold_in(_rk, 1), (64, 64, 128), jnp.float32)
        _lenS = 64 - jax.random.randint(jax.random.fold_in(_rk, 7), (64,), 0, max(1, 64 // 4) + 1, jnp.int32)
        _lenS2 = 64 - jax.random.randint(jax.random.fold_in(_rk, 8), (64,), 0, max(1, 64 // 4) + 1, jnp.int32)
        _ctx_1024P = jax.random.normal(jax.random.fold_in(_rk, 11), (64, 16, 128), jnp.float32)
        _ctx_1024c = jax.random.dirichlet(jax.random.fold_in(_rk, 511), 0.3 * jnp.ones((16,), jnp.float32), (64, 64))
        _ctx_1024t = jnp.einsum('bsk,bkd->bsd', _ctx_1024c, _ctx_1024P)
        _ctx_1024t = _ctx_1024t * jax.lax.rsqrt(jnp.mean(jnp.square(_ctx_1024t)) + 1e-12) * 0.953939
        ctx_1024 = -1.39393e-06 + 0.999914 * (_ctx_1024t + 0.3 * jax.random.normal(jax.random.fold_in(_rk, 611), (64, 64, 128), jnp.float32))
        return (x, ctx_1024)
    x, ctx_1024 = _rec_inputs()

    def _L0_attn_setup():
        import jax, jax.numpy as jnp
        import numpy as np
        DIM = 128
        HEADS = 8
        DIM_QK = 64
        MAX_POS = 10
        SCALE = DIM_QK ** (-0.5)
        key = jax.random.key(seed)
        ks = jax.random.split(key, 6)
        b, n = (4, 256)
        x = jax.random.normal(ks[0], (b, n, DIM), dtype=jnp.float32)
        mask = jnp.ones((b, n), dtype=bool)
        s = DIM ** (-0.5)
        W_qk = jax.random.normal(ks[1], (DIM, DIM_QK * HEADS * 2), dtype=jnp.float32) * s
        W_v = jax.random.normal(ks[2], (DIM, DIM), dtype=jnp.float32) * s
        W_out = jax.random.normal(ks[3], (DIM, DIM), dtype=jnp.float32) * s
        b_out = jnp.zeros((DIM,), dtype=jnp.float32)
        conv = jax.random.normal(ks[4], (HEADS, 2 * MAX_POS + 1), dtype=jnp.float32) * 0.02
        return {'x': x, 'mask': mask, 'W_qk': W_qk, 'W_v': W_v, 'W_out': W_out, 'b_out': b_out, 'conv': conv}
    _L0_attn_all = _L0_attn_setup()
    _L0_attn_in = {k: v for k, v in _L0_attn_all.items() if k in ('mask', 'W_qk', 'W_v', 'W_out', 'b_out', 'conv')}
    del _L0_attn_all

    def _L0_xattn_setup():
        import math
        import jax, jax.numpy as jnp
        import numpy as np
        B, S, H, NH = (2, 256, 128, 4)
        DH = H // NH

        def _mlstm_parallel(qh, kh, vh, ig, fg, eps=1e-06):
            b, nh, s, dh = qh.shape
            log_f = jax.nn.log_sigmoid(fg)
            pcs = jnp.pad(jnp.cumsum(log_f, axis=-1), ((0, 0), (0, 0), (1, 0)))
            mat = pcs[..., :, None] - pcs[..., None, :]
            ltr = jnp.tril(jnp.ones((s, s), dtype=bool))
            log_fg_matrix = jnp.where(ltr, mat[..., 1:, 1:], -jnp.inf)
            log_D = log_fg_matrix + ig[..., None, :]
            max_log_D = jnp.max(log_D, axis=-1, keepdims=True)
            D = jnp.exp(log_D - max_log_D)
            qk = jnp.einsum('bhsd,bhtd->bhst', qh, kh) / math.sqrt(dh)
            C = qk * D
            normalizer = jnp.maximum(jnp.abs(C.sum(axis=-1, keepdims=True)), jnp.exp(-max_log_D))
            Cn = C / (normalizer + eps)
            return jnp.einsum('bhst,bhtd->bhsd', Cn, vh)
        key = jax.random.key(seed)
        ks = jax.random.split(key, 8)
        gate_std = 1.0 / math.sqrt(3 * H)
        return {'q': jax.random.normal(ks[0], (B, S, H), jnp.float32), 'k': jax.random.normal(ks[1], (B, S, H), jnp.float32), 'v': jax.random.normal(ks[2], (B, S, H), jnp.float32), 'w_igate': jax.random.normal(ks[3], (NH, 3 * H), jnp.float32) * gate_std, 'b_igate': jax.random.normal(ks[4], (NH,), jnp.float32) * 0.1, 'w_fgate': jax.random.normal(ks[5], (NH, 3 * H), jnp.float32) * gate_std, 'b_fgate': jnp.linspace(3.4, 6.0, NH, dtype=jnp.float32), 'ln_weight': jnp.zeros((H,), jnp.float32)}
    _L0_xattn_all = _L0_xattn_setup()
    _L0_xattn_in = {k: v for k, v in _L0_xattn_all.items() if k in ('w_igate', 'b_igate', 'w_fgate', 'b_fgate', 'ln_weight')}
    del _L0_xattn_all

    def _L0_ffn_setup():
        import jax, jax.numpy as jnp
        import numpy as np
        H, F, E_SHARED, E_ROUTED, K = (128, 512, 1, 8, 2)

        def _expert(x, w_up, w_down):
            h = jax.nn.gelu(jnp.einsum('bsh,hf->bsf', x, w_up), approximate=False)
            return jnp.einsum('bsf,fh->bsh', h, w_down)
        key = jax.random.key(seed)
        ks = jax.random.split(key, 6)
        x = jax.random.normal(ks[0], (4, 256, H), dtype=jnp.float32)
        s = 0.02
        shared_up = jax.random.normal(ks[1], (E_SHARED, H, F), dtype=jnp.float32) * s
        shared_down = jax.random.normal(ks[2], (E_SHARED, F, H), dtype=jnp.float32) * s
        routed_up = jax.random.normal(ks[3], (E_ROUTED, H, F), dtype=jnp.float32) * s
        routed_down = jax.random.normal(ks[4], (E_ROUTED, F, H), dtype=jnp.float32) * s
        router_w = jax.random.normal(ks[5], (H, E_ROUTED), dtype=jnp.float32) * s
        return {'x': x, 'shared_up': shared_up, 'shared_down': shared_down, 'routed_up': routed_up, 'routed_down': routed_down, 'router_w': router_w}
    _L0_ffn_all = _L0_ffn_setup()
    _L0_ffn_in = {k: v for k, v in _L0_ffn_all.items() if k in ('shared_up', 'shared_down', 'routed_up', 'routed_down', 'router_w')}
    del _L0_ffn_all
    return {'x': x, 'ctx_1024': ctx_1024, 'L0_attn_mask': _L0_attn_in['mask'], 'L0_attn_W_qk': _L0_attn_in['W_qk'], 'L0_attn_W_v': _L0_attn_in['W_v'], 'L0_attn_W_out': _L0_attn_in['W_out'], 'L0_attn_b_out': _L0_attn_in['b_out'], 'L0_attn_conv': _L0_attn_in['conv'], 'L0_xattn_w_igate': _L0_xattn_in['w_igate'], 'L0_xattn_b_igate': _L0_xattn_in['b_igate'], 'L0_xattn_w_fgate': _L0_xattn_in['w_fgate'], 'L0_xattn_b_fgate': _L0_xattn_in['b_fgate'], 'L0_xattn_ln_weight': _L0_xattn_in['ln_weight'], 'L0_ffn_shared_up': _L0_ffn_in['shared_up'], 'L0_ffn_shared_down': _L0_ffn_in['shared_down'], 'L0_ffn_routed_up': _L0_ffn_in['routed_up'], 'L0_ffn_routed_down': _L0_ffn_in['routed_down'], 'L0_ffn_router_w': _L0_ffn_in['router_w']}

def reference(x, ctx_1024, L0_attn_mask, L0_attn_W_qk, L0_attn_W_v, L0_attn_W_out, L0_attn_b_out, L0_attn_conv, L0_xattn_w_igate, L0_xattn_b_igate, L0_xattn_w_fgate, L0_xattn_b_fgate, L0_xattn_ln_weight, L0_ffn_shared_up, L0_ffn_shared_down, L0_ffn_routed_up, L0_ffn_routed_down, L0_ffn_router_w):
    import jax
    import jax.numpy as jnp

    def _L0_attn_ref(x, mask, W_qk, W_v, W_out, b_out, conv):
        import jax, jax.numpy as jnp
        import numpy as np
        DIM = 128
        HEADS = 8
        DIM_QK = 64
        MAX_POS = 10
        SCALE = DIM_QK ** (-0.5)
        b, n, _ = x.shape
        h, dqk = (HEADS, DIM_QK)
        dv = DIM // h
        qk = x @ W_qk
        q, k = jnp.split(qk, 2, axis=-1)
        v = x @ W_v
        q = q.reshape(b, n, h, dqk).transpose(0, 2, 1, 3)
        k = k.reshape(b, n, h, dqk).transpose(0, 2, 1, 3)
        v = v.reshape(b, n, h, dv).transpose(0, 2, 1, 3)
        dots = jnp.einsum('bhid,bhjd->bhij', q, k) * SCALE
        seq = jnp.arange(n)
        dist = jnp.clip(seq[None, :] - seq[:, None], -MAX_POS, MAX_POS) + MAX_POS
        bias = conv[:, dist]
        attn = jax.nn.softmax(dots + bias[None], axis=-1)
        out = jnp.einsum('bhij,bhjd->bhid', attn, v)
        out = out.transpose(0, 2, 1, 3).reshape(b, n, h * dv)
        return out @ W_out + b_out

    def _L0_xattn_ref(q, k, v, w_igate, b_igate, w_fgate, b_fgate, ln_weight):
        import math
        import jax, jax.numpy as jnp
        import numpy as np
        B, S, H, NH = (2, 256, 128, 4)
        DH = H // NH

        def _mlstm_parallel(qh, kh, vh, ig, fg, eps=1e-06):
            b, nh, s, dh = qh.shape
            log_f = jax.nn.log_sigmoid(fg)
            pcs = jnp.pad(jnp.cumsum(log_f, axis=-1), ((0, 0), (0, 0), (1, 0)))
            mat = pcs[..., :, None] - pcs[..., None, :]
            ltr = jnp.tril(jnp.ones((s, s), dtype=bool))
            log_fg_matrix = jnp.where(ltr, mat[..., 1:, 1:], -jnp.inf)
            log_D = log_fg_matrix + ig[..., None, :]
            max_log_D = jnp.max(log_D, axis=-1, keepdims=True)
            D = jnp.exp(log_D - max_log_D)
            qk = jnp.einsum('bhsd,bhtd->bhst', qh, kh) / math.sqrt(dh)
            C = qk * D
            normalizer = jnp.maximum(jnp.abs(C.sum(axis=-1, keepdims=True)), jnp.exp(-max_log_D))
            Cn = C / (normalizer + eps)
            return jnp.einsum('bhst,bhtd->bhsd', Cn, vh)
        b, s, h = q.shape
        nh = b_igate.shape[0]
        dh = h // nh
        gin = jnp.concatenate([q, k, v], axis=-1)
        ig = jnp.einsum('bsd,hd->bhs', gin, w_igate) + b_igate[None, :, None]
        fg = jnp.einsum('bsd,hd->bhs', gin, w_fgate) + b_fgate[None, :, None]
        qh = q.reshape(b, s, nh, dh).transpose(0, 2, 1, 3)
        kh = k.reshape(b, s, nh, dh).transpose(0, 2, 1, 3)
        vh = v.reshape(b, s, nh, dh).transpose(0, 2, 1, 3)
        hst = _mlstm_parallel(qh, kh, vh, ig, fg)
        mean = hst.mean(axis=-1, keepdims=True)
        var = hst.var(axis=-1, keepdims=True)
        hn = (hst - mean) / jnp.sqrt(var + 1e-05)
        scale = (1.0 + ln_weight).reshape(nh, dh)
        hn = hn * scale[None, :, None, :]
        return hn.transpose(0, 2, 1, 3).reshape(b, s, h)

    def _L0_ffn_ref(x, shared_up, shared_down, routed_up, routed_down, router_w):
        import jax, jax.numpy as jnp
        import numpy as np
        H, F, E_SHARED, E_ROUTED, K = (128, 512, 1, 8, 2)

        def _expert(x, w_up, w_down):
            h = jax.nn.gelu(jnp.einsum('bsh,hf->bsf', x, w_up), approximate=False)
            return jnp.einsum('bsf,fh->bsh', h, w_down)
        shared_out = jnp.zeros_like(x)
        for i in range(E_SHARED):
            shared_out = shared_out + _expert(x, shared_up[i], shared_down[i])
        probs = jax.nn.softmax(jnp.einsum('bsh,he->bse', x, router_w), axis=-1)
        top_k_prob, top_k_idx = jax.lax.top_k(probs, K)
        onehot = jax.nn.one_hot(top_k_idx, E_ROUTED, dtype=x.dtype)
        gates = jnp.einsum('bsk,bske->bse', top_k_prob, onehot)
        routed_out = jnp.zeros_like(x)
        for e in range(E_ROUTED):
            y = _expert(x, routed_up[e], routed_down[e])
            routed_out = routed_out + gates[..., e:e + 1] * y
        return shared_out + routed_out + x
    x = _layernorm(x + _L0_attn_ref(x, L0_attn_mask, L0_attn_W_qk, L0_attn_W_v, L0_attn_W_out, L0_attn_b_out, L0_attn_conv), axis=-1)
    x = _layernorm(x + _L0_xattn_ref(x, ctx_1024, ctx_1024, L0_xattn_w_igate, L0_xattn_b_igate, L0_xattn_w_fgate, L0_xattn_b_fgate, L0_xattn_ln_weight), axis=-1)
    x = _layernorm(x + _L0_ffn_ref(x, L0_ffn_shared_up, L0_ffn_shared_down, L0_ffn_routed_up, L0_ffn_routed_down, L0_ffn_router_w), axis=-1)
    return x

_drawn_inputs = setup_inputs


def setup_inputs(seed=0):
    import zlib

    import numpy as np

    out = dict(_drawn_inputs(seed))
    spreads = {'L0_attn_b_out': (0.0, 0.1), 'L0_xattn_ln_weight': (0.0, 0.1)}
    factors = {'L0_attn_conv': 8.0,
     'L0_xattn_b_igate': 58.737,
     'L0_ffn_routed_up': 8.0,
     'L0_ffn_routed_down': 8.0,
     'L0_ffn_router_w': 8.0,
     'L0_ffn_shared_up': 3.49,
     'L0_ffn_shared_down': 3.404}
    for name, (base, spread) in spreads.items():
        noise = np.random.default_rng([zlib.crc32(name.encode()), seed]).standard_normal(out[name].shape)
        drawn = base * np.exp(spread * noise) if base else spread * noise
        out[name] = jnp.asarray(drawn.astype(out[name].dtype))
    for name, factor in factors.items():
        out[name] = (out[name] * factor).astype(out[name].dtype)
    return out
```

```python
import concourse.bass as bass
from concourse import mybir
from contextlib import ExitStack

F32 = mybir.dt.float32
BF16 = mybir.dt.bfloat16
I32 = mybir.dt.int32
ALU = mybir.AluOpType
ACT = mybir.ActivationFunctionType
AX = mybir.AxisListType

P = 128
B, S, D = 64, 64, 128
NT = B * S // P
GT = 4
NG = NT // GT
W = GT * P
H, DQ = 8, 64
DV = D // H
MAXPOS = 10
NH, DH = 4, 32
FF, E = 512, 8
FC = FF // P
SLOT_TILES = 2 * NT + E
ROW = D + 4
GATE, DEST = D, D + 1
DUMP = 9
BIG = 1e30
LN_EPS = 1e-5


class Steps:

    def __init__(self, eng, sem):
        self.eng, self.sem, self.base, self.n = eng, sem, 0, 0

    def __call__(self, ins):
        self.n += 1
        ins.then_inc(self.sem, 1)
        self.eng.wait_ge(self.sem, self.base + self.n)

    def start(self, base):
        self.base, self.n = base, 0


def pause(eng, sem, value, passed):
    eng.wait_ge(sem, value)
    eng.sem_inc(passed, 1)


def spread(ap, shape):
    return ap.unsqueeze(len(shape) - 1).broadcast_to(shape)


def decoder_layer(nc, x, ctx_in, w_qk, w_v, w_out, b_out, conv, w_ig, b_ig, w_fg, b_fg, ln_w,
                  sh_up, sh_down, ro_up, ro_down, router_w, out):
    es = ExitStack()

    def sb(name, shape, dt=F32):
        return es.enter_context(nc.sbuf_tensor(name, shape, dt))

    def sem(name):
        return es.enter_context(nc.semaphore(name))

    bank = [es.enter_context(nc.psum_tensor(f"bank{n}", [P, 512], F32)) for n in range(8)]

    x_tok = x.rearrange("(t a) s d -> (a s) t d", a=2)
    ctx_tok = ctx_in.rearrange("(t a) s d -> (a s) t d", a=2)
    out_tok = out.rearrange("(t a) s d -> (a s) t d", a=2)
    conv_pad = nc.dram_tensor("conv_pad", (H, S, P), F32, kind="Internal").ap()
    slots = nc.dram_tensor("slots", (SLOT_TILES * P, ROW), F32, kind="Internal").ap()
    routed = nc.dram_tensor("routed", (2 * B * S + DUMP * P, D), F32, kind="Internal").ap()

    tok = sb("tok", [P, NT, D])
    x2T = sb("x2T", [P, NT * P])
    wup = sb("wup", [P, E * FF])
    wdn = sb("wdn", [P, E * FC * D])
    sup = sb("sup", [P, FF])
    sdn = sb("sdn", [P, FC, D])
    ident = sb("ident", [P, P])
    identb = sb("identb", [P, P], BF16)
    onesb = sb("onesb", [P, P], BF16)
    trib = sb("trib", [P, P], BF16)
    causal = sb("causal", [P, NH * S], BF16)
    eps = sb("eps", [P, 1])
    ones_row = sb("ones_row", [1, P])
    bout = sb("bout", [1, D])
    wqk = sb("wqk", [P, 2 * H * DQ])
    wqkT = sb("wqkT", [P, H, P])
    wv = sb("wv", [P, D])
    wo = sb("wo", [P, D])
    pairw = sb("pairw", [P, H, D])
    cpad = sb("cpad", [H, P])
    cin = sb("cin", [H, 2 * MAXPOS + 1])
    bias = sb("bias", [P, H, S])
    gw = sb("gw", [2 * NH, 3 * D])
    gwT = sb("gwT", [P, 3, 2 * NH])
    wgx = sb("wgx", [P, 36])
    wgc = sb("wgc", [P, 36])
    bi = sb("bi", [NH, 1])
    bf = sb("bf", [NH, 1])
    lnw = sb("lnw", [P, D])
    rw = sb("rw", [P, E])
    xs = sb("xs", [P, GT, D])
    xT = sb("xT", [P, W])
    z = sb("z", [P, H, W])
    prob = sb("prob", [P, GT, H * S])
    negmax = sb("negmax", [P, GT, H])
    probT = sb("probT", [P, GT * P])
    vblk = sb("vblk", [P, GT * 8, 2, DV + 1])
    rden = sb("rden", [P, GT, H])
    o = sb("o", [P, D])
    oT = sb("oT", [P, P])
    res = sb("res", [P, GT, D])
    stats = sb("stats", [P, GT, 6])
    mv = sb("mv", [P, GT, 2])
    lnv = sb("lnv", [P, GT])
    rstd = sb("rstd", [P, GT])
    cs = sb("cs", [P, GT, D])
    x1T = sb("x1T", [P, W])
    cT = sb("cT", [P, W])
    qblk = sb("qblk", [P, 2 * GT, NH, S])
    vmask = sb("vmask", [P, GT, 2, NH, DH + 1])
    fpre = sb("fpre", [NH, W])
    fabs = sb("fabs", [NH, W])
    fexp = sb("fexp", [NH, W])
    flog = sb("flog", [NH, W])
    logf = sb("logf", [NH, W])
    cumf = sb("cumf", [NH, W])
    amax = sb("amax", [NH, W])
    seqm = sb("seqm", [NH, W])
    seqn = sb("seqn", [NH, W])
    emx = sb("emx", [NH, W])
    mrow = sb("mrow", [NH, W])
    al = sb("al", [36, W])
    rh = sb("rh", [36, 2 * GT, NH, S])
    nhot = sb("nhot", [NH, NH, S])
    decay = sb("decay", [P, 2, NH * S])
    cmat = sb("cmat", [P, 2, NH * S])
    floor = sb("floor", [P, GT, NH])
    nrm = sb("nrm", [P, GT, NH])
    hst = sb("hst", [P, GT * NH, DH])
    hmu = sb("hmu", [P, GT * NH])
    hsq = sb("hsq", [P, GT * NH, DH])
    hva = sb("hva", [P, GT * NH])
    hln = sb("hln", [P, GT * NH])
    hrs = sb("hrs", [P, GT * NH])
    lg = sb("lg", [P, NT, E])
    m8 = sb("m8", [P, NT])
    cand = sb("cand", [P, NT, E])
    hot = [sb(f"hot{k}", [P, NT, E]) for k in range(2)]
    hotb = sb("hotb", [P, NT, E], BF16)
    gate = [sb(f"gate{k}", [P, NT]) for k in range(2)]
    io_e = sb("io_e", [P, E])
    io_128 = sb("io_128", [P, NT])
    io_tau = sb("io_tau", [1, SLOT_TILES])
    tote = sb("tote", [P, E, NT])
    cume = sb("cume", [P, E, NT])
    segm = sb("segm", [P, E, NT])
    one8 = sb("one8", [P, E])
    ntile = sb("ntile", [P, E])
    ctile = sb("ctile", [P, E])
    gt = sb("gt", [P, E, NT])
    sl = sb("sl", [P, NT, E])
    slot = [sb(f"slot{k}", [P, NT], I32) for k in range(2)]
    slotf = sb("slotf", [P, NT])
    dest = sb("dest", [P, 2, NT], I32)
    tcmp = sb("tcmp", [1, SLOT_TILES, E])
    texp = sb("texp", [1, SLOT_TILES])
    texpi = sb("texpi", [1, SLOT_TILES], I32)
    prefill = sb("prefill", [P, DUMP, ROW])
    stg = [sb(f"stg{n}", [P, ROW]) for n in range(4)]
    idx = [sb(f"idx{n}", [P, 1], I32) for n in range(4)]
    shT = z[:, :, :].rearrange("p (a c) w -> p a c w", a=2)
    NX = 8
    qflat = qblk[:, :, :, :].rearrange("p n h s -> p (n h s)")
    xr = [qflat[:, n * ROW:(n + 1) * ROW] for n in range(NX)]
    yr = [qflat[:, NX * ROW + n * D:NX * ROW + (n + 1) * D] for n in range(4)]
    xrT = cT[:, 0:2 * P].rearrange("p (a d) -> p a d", a=2)
    hh = prob[:, 0:2, :]
    hT = prob[:, 2:4, :]
    y0, y1, fin = (x2T[:, n * 2 * W:(n + 1) * 2 * W].rearrange("p (a k d) -> p a k d", a=2, k=GT) for n in range(3))

    names = """ld_tok ld_wqk ld_conv ld_cpad ld_bias ld_small ld_gw ld_wup ld_wdn ld_sh st_cpad cpad_ok
    const_p const_v wqkT_ps wqkT_ok pw_ps pw_ok gwT_ps gw_ok vsteps bias_ok
    xs_ok xT_ps xT_ok z_ps z_ok s_ps v_ps v_ok logit_ok exp_ok pT_ps pT_ok av_ps o_ok oT_ps oT_ok
    pr_ps res_ok stat_ok mv_ok lnv_ok rstd_ok x1_ok asteps
    xs1_ok cs_ok x1T_ps x1T_ok cT_ps cT_ok g_ps fpre_ok fabs_ok fexp_ok flog_ok igsteps al_ok rh_ok
    mrow_ok emx_ok en_ps floor_ok qblk_ok vmask_ok dd_ps decay_ok c_ok u_ps h_ok hsteps hsq_ok hva_ok
    hln_ok hrs_ok res1_ok mv1_ok lnv1_ok rstd1_ok x2_ok bsteps
    xs2_ok x2T_ps x2T_ok x2Ts_ok lg_ps lg_ok lmax_ok lexp_ok rsteps hotb_ok rank_ps slot_ok texp_ok
    stage_ok scat0 scat1 scat2 scat3 pre_ok shu_ps sh_ok shd_ps base_ok
    xr_ps xrT_ok up_ps hh_ok hT_ps hT_ok y_ps y_ok
    passed_pool passed_dve passed_pe fsteps mv2_ok lnv2_ok rstd2_ok fin_ok st_out""".split()
    s = {n: sem(n) for n in names}
    ld_xr = [sem(f"ld_xr{n}") for n in range(NX)]
    sc_y = [sem(f"sc_y{n}") for n in range(4)]
    ld_y0 = [sem(f"ld_y0_{n}") for n in range(2)]
    ld_y1 = [sem(f"ld_y1_{n}") for n in range(2)]
    scat = [s[f"scat{n}"] for n in range(4)]
    st_o = [sem(f"st_o{n}") for n in range(2)]

    def g4(t):
        return bass.ds(t, GT)

    block = es.enter_context(nc.Block())

    @block.sync
    def _(sp):
        sp.dma_start(wqk[:, :], w_qk).then_inc(s["ld_wqk"], 16)
        sp.dma_start(xs[:, :, :], x_tok[:, 0:GT, :]).then_inc(s["xs_ok"], 16)
        sp.dma_start(cin[:, :], conv).then_inc(s["ld_conv"], 16)
        sp.dma_start(tok[:, :, :], x_tok).then_inc(s["ld_tok"], 16)
        sp.dma_start(gw[0:NH, :], w_ig).then_inc(s["ld_gw"], 16)
        sp.dma_start(gw[NH:2 * NH, :], w_fg).then_inc(s["ld_gw"], 16)
        sp.wait_ge(s["cpad_ok"], 3)
        sp.dma_start(conv_pad, cpad[:, :].unsqueeze(1).broadcast_to([H, S, P])).then_inc(s["st_cpad"], 16)
        sp.wait_ge(s["st_cpad"], 16)
        for a in range(2):
            src = bass.AP(tensor=conv_pad.tensor, offset=S - 1, ap=[[P - 1, S], [S * P, H], [1, S]])
            sp.dma_start(bias[a * S:(a + 1) * S, :, :], src).then_inc(s["ld_bias"], 16)
        sp.wait_ge(s["pre_ok"], 1)
        for n in range(SLOT_TILES // DUMP):
            sp.dma_start(slots[n * DUMP * P:(n + 1) * DUMP * P, :].rearrange("(b p) r -> p b r", p=P),
                         prefill[:, :, :]).then_inc(s["st_out"], 16)
        with sp.Fori(1, NG) as g:
            sp.wait_ge(s["xT_ps"], g)
            sp.dma_start(xs[:, :, :], x_tok[:, g4(g * GT), :]).then_inc(s["xs_ok"], 16)
        def stage_b(g, first):
            if not first:
                sp.wait_ge(s["x1T_ps"], g)
                sp.wait_ge(s["cT_ps"], g)
                sp.wait_ge(s["vmask_ok"], g)
            sp.wait_ge(s["x1_ok"], GT * g + GT)
            sp.dma_start(xs[:, :, :], tok[:, g4(g * GT), :]).then_inc(s["xs1_ok"], 16)
            sp.dma_start(cs[:, :, :], ctx_tok[:, g4(g * GT), :]).then_inc(s["cs_ok"], 16)
        sp.wait_ge(s["xT_ps"], NG)
        stage_b(0, True)
        with sp.Fori(1, NG) as g:
            stage_b(g, False)
        sp.wait_ge(s["x1T_ps"], NG)
        sp.wait_ge(s["x2_ok"], GT)
        sp.dma_start(xs[:, :, :], tok[:, 0:GT, :]).then_inc(s["xs2_ok"], 16)
        with sp.Fori(1, NG) as g:
            sp.wait_ge(s["x2_ok"], GT * g + GT)
            sp.wait_ge(s["x2T_ps"], g)
            sp.dma_start(xs[:, :, :], tok[:, g4(g * GT), :]).then_inc(s["xs2_ok"], 16)
        for n in range(4):
            sp.wait_ge(scat[n], 16 * 2 * NT // 4)
        def load_slots(t, n):
            sp.dma_start(xr[n][:, :], slots[bass.ds(t * P, P), :]).then_inc(ld_xr[n], 16)
        for n in range(NX):
            load_slots(n, n)
        with sp.Fori(1, SLOT_TILES // NX) as i:
            for n in range(NX):
                sp.wait_ge(sc_y[n % 4], 16 * (2 * i - 1 + n // 4))
                load_slots(i * NX + n, n)
        for n in range(4):
            sp.wait_ge(sc_y[n], 16 * SLOT_TILES // 4)
        def final(g, n, first):
            if not first:
                sp.wait_ge(s["fin_ok"], g - 1)
            sp.dma_start(y0[:, n], routed[bass.ds(g * W, W), :].rearrange("(t p) d -> p t d", p=P)).then_inc(ld_y0[n], 16)
            sp.dma_start(y1[:, n], routed[bass.ds(g * W + B * S, W), :].rearrange("(t p) d -> p t d", p=P)).then_inc(ld_y1[n], 16)
        final(0, 0, True)
        final(1, 1, True)
        with sp.Fori(1, NG // 2) as i:
            for n in range(2):
                final(2 * i + n, n, False)

    @block.gpsimd
    def _(pool):
        st = Steps(pool, s["const_p"])
        st(pool.memset(ident[:, :], 0.0))
        st(pool.affine_select(out=ident[:, :], in_=ident[:, :], compare_op=ALU.not_equal, fill=1.0,
                              base=0, pattern=[[-1, P]], channel_multiplier=1))
        st(pool.tensor_copy(identb[:, :], ident[:, :]))
        st(pool.memset(causal[:, :], 0.0))
        for a in range(2):
            v = causal[a * S:(a + 1) * S, :].rearrange("p (h s) -> p h s", h=NH)
            st(pool.affine_select(out=v, in_=v, compare_op=ALU.is_ge, fill=-BIG, base=0,
                                  pattern=[[0, NH], [1, S]], channel_multiplier=-1))
        st(pool.memset(trib[:, :], 1.0))
        st(pool.affine_select(out=trib[:, :], in_=trib[:, :], compare_op=ALU.is_gt, fill=0.0, base=0,
                              pattern=[[1, P]], channel_multiplier=-1))
        st(pool.memset(rh[:, :, :, :], 0.0))
        st(pool.memset(rh[0:NH, :, :, :], 1.0))
        v = rh[0:NH, :, :, :]
        st(pool.affine_select(out=v, in_=v, compare_op=ALU.is_equal, fill=0.0, base=0,
                              pattern=[[0, 2 * GT], [1, NH], [0, S]], channel_multiplier=-1))
        st(pool.memset(nhot[:, :, :], -1.0))
        st(pool.affine_select(out=nhot[:, :, :], in_=nhot[:, :, :], compare_op=ALU.is_equal, fill=0.0,
                              base=0, pattern=[[1, NH], [0, S]], channel_multiplier=-1))
        st(pool.iota(io_e[:, :], [[-1, E]], base=E, channel_multiplier=0, allow_small_or_imprecise_dtypes=True))
        st(pool.iota(io_128[:, :], [[P, NT]], base=0, channel_multiplier=0, allow_small_or_imprecise_dtypes=True))
        st(pool.iota(io_tau[:, :], [[1, SLOT_TILES]], base=0, channel_multiplier=0, allow_small_or_imprecise_dtypes=True))
        st(pool.iota(dest[:, :, :], [[B * S, 2], [P, NT]], base=0, channel_multiplier=1))
        st(pool.memset(prefill[:, :, :], 0.0))
        pool.iota(prefill[:, :, :].bitcast(I32)[:, :, DEST], [[P, DUMP]], base=2 * B * S,
                  channel_multiplier=1).then_inc(s["pre_ok"], 1)
        pool.wait_ge(s["st_out"], 16 * (SLOT_TILES // DUMP))
        with pool.Fori(0, NT // 2) as i:
            for n in range(4):
                pause(pool, s["stage_ok"], 4 * i + n + 1, s["passed_pool"])
                pool.indirect_dma_start(slots, bass.IndirectOffsetOnAxis(ap=idx[n][:, 0:1], axis=0),
                                        stg[n][:, :], None).then_inc(scat[n], 16)
        with pool.Fori(0, SLOT_TILES // NX) as i:
            for n in range(NX):
                pause(pool, s["y_ok"], NX * i + n + 1, s["passed_pool"])
                pool.indirect_dma_start(routed, bass.IndirectOffsetOnAxis(ap=xr[n][:, :].bitcast(I32)[:, DEST:DEST + 1], axis=0),
                                        yr[n % 4][:, :], None).then_inc(sc_y[n % 4], 16)

    @block.scalar
    def _(act):
        for n, (dst, src) in enumerate(((wv[:, :], w_v), (wo[:, :], w_out),
                                        (bout[:, :], b_out.rearrange("(a n) -> a n", a=1)),
                                        (bi[:, :], b_ig.rearrange("(n a) -> n a", a=1)),
                                        (bf[:, :], b_fg.rearrange("(n a) -> n a", a=1)),
                                        (rw[:, :], router_w),
                                        (lnw[:, :], bass.AP(tensor=ln_w.tensor, offset=0, ap=[[0, P], [1, D]])))):
            act.dma_start(dst, src).then_inc(s["ld_small"], 16)
        act.dma_start(sup[:, :], sh_up[0]).then_inc(s["ld_sh"], 16)
        act.dma_start(sdn[:, :, :], sh_down[0].rearrange("(c p) h -> p c h", p=P)).then_inc(s["ld_sh"], 16)
        act.dma_start(wup[:, :].rearrange("p (e f) -> p e f", e=E), ro_up.rearrange("e h f -> h e f")).then_inc(s["ld_wup"], 16)
        act.dma_start(wdn[:, :].rearrange("p (e c h) -> p e c h", e=E, c=FC),
                      ro_down.rearrange("e (c p) h -> p e c h", p=P)).then_inc(s["ld_wdn"], 16)

        def x_evac(g):
            act.wait_ge(s["xT_ps"], g + 1)
            act.activation(xT[:, :], bank[7][:, :], ACT.Copy).then_inc(s["xT_ok"], 1)

        def z_evac(g, h):
            act.wait_ge(s["z_ps"], H * g + h + 1)
            act.activation(z[:, h, :], bank[4 + h % 2][:, :], ACT.Copy).then_inc(s["z_ok"], 1)

        def exps(g, k):
            act.wait_ge(s["logit_ok"], GT * g + k + 1)
            act.activation(prob[:, k, :], prob[:, k, :], ACT.Exp).then_inc(s["exp_ok"], 1)

        def pT_evac(g, k):
            act.wait_ge(s["pT_ps"], GT * g + k + 1)
            act.activation(probT[:, :], bank[6][:, :], ACT.Copy).then_inc(s["pT_ok"], 1)

        def oT_evac(g, k):
            act.wait_ge(s["oT_ps"], GT * g + k + 1)
            act.activation(oT[:, :], bank[k][:, 136:136 + P], ACT.Copy).then_inc(s["oT_ok"], 1)

        def rsqrt(mv_sem, need, src, ln_out, ln_sem, r_out, r_sem, count, scale=1.0):
            act.wait_ge(mv_sem, need)
            act.activation(ln_out, src, ACT.Ln, bias=eps[:, 0:1], scale=scale).then_inc(ln_sem, 1)
            act.wait_ge(ln_sem, count)
            act.activation(r_out, ln_out, ACT.Exp, scale=-0.5).then_inc(r_sem, 1)

        def group_a(g, more):
            exps(g, 0)
            for half in range(2):
                act.wait_ge(s["v_ps"], g + 1)
                r = slice(half * S, half * S + S)
                act.activation(vblk[r, :, half, 0:DV], bank[7][r, :].rearrange("p (n d) -> p n d", d=DV),
                               ACT.Copy).then_inc(s["v_ok"], 1)
            if more:
                x_evac(g + 1)
            act.wait_ge(s["s_ps"], GT * g + GT)
            for k in range(GT):
                pT_evac(g, k)
                if more:
                    z_evac(g + 1, 2 * k)
                if k + 1 < GT:
                    exps(g, k + 1)
                if more:
                    z_evac(g + 1, 2 * k + 1)
                oT_evac(g, k)
            rsqrt(s["mv_ok"], GT * g + GT, mv[:, :, 1], lnv[:, :], s["lnv_ok"], rstd[:, :], s["rstd_ok"], g + 1)

        act.wait_ge(s["wqkT_ps"], 1)
        act.activation(wqkT[:, 0:4, :], bank[0][:, :].rearrange("p (a b) -> p a b", a=4), ACT.Copy).then_inc(s["wqkT_ok"], 1)
        act.activation(wqkT[:, 4:8, :], bank[1][:, :].rearrange("p (a b) -> p a b", a=4), ACT.Copy).then_inc(s["wqkT_ok"], 1)
        act.wait_ge(s["pw_ps"], 1)
        for a in range(2):
            act.activation(pairw[:, a:H:2, :], bank[2 + a][:, :].rearrange("p (a b) -> p a b", a=4),
                           ACT.Copy, scale=DQ ** -0.5).then_inc(s["pw_ok"], 1)
        x_evac(0)
        for h in range(H):
            z_evac(0, h)
        act.wait_ge(s["const_v"], 1)
        with act.Fori(0, NG - 1) as g:
            group_a(g, True)
        group_a(NG - 1, False)

        def group_b(g):
            act.wait_ge(s["x1T_ps"], g + 1)
            act.activation(x1T[:, :], bank[0][:, :], ACT.Copy).then_inc(s["x1T_ok"], 1)
            act.wait_ge(s["cT_ps"], g + 1)
            act.activation(cT[:, :], bank[1][:, :], ACT.Copy).then_inc(s["cT_ok"], 1)
            act.wait_ge(s["g_ps"], g + 1)
            act.activation(fpre[:, :], bank[2][32:32 + NH, :], ACT.Identity, bias=bf[:, 0:1]).then_inc(s["fpre_ok"], 1)
            act.wait_ge(s["fpre_ok"], g + 1)
            act.activation(fabs[:, :], fpre[:, :], ACT.Abs).then_inc(s["fabs_ok"], 1)
            act.wait_ge(s["fabs_ok"], g + 1)
            act.activation(fexp[:, :], fabs[:, :], ACT.Exp, scale=-1.0).then_inc(s["fexp_ok"], 1)
            act.wait_ge(s["fexp_ok"], g + 1)
            act.activation(flog[:, :], fexp[:, :], ACT.Ln, bias=1.0).then_inc(s["flog_ok"], 1)
            for h in range(NH):
                r = slice(h * DH, (h + 1) * DH)
                act.activation(qblk[r, :, h, :], bank[0][r, :].rearrange("p (n s) -> p n s", s=S),
                               ACT.Copy).then_inc(s["qblk_ok"], 1)
            act.wait_ge(s["mrow_ok"], g + 1)
            act.activation(emx[:, :], mrow[:, :], ACT.Exp, scale=-1.0).then_inc(s["emx_ok"], 1)
            for k in range(GT):
                if k == 0:
                    act.wait_ge(s["en_ps"], g + 1)
                    act.activation(floor[:, :, :], bank[7][:, 0:GT * NH].rearrange("p (a b) -> p a b", a=GT),
                                   ACT.Copy).then_inc(s["floor_ok"], 1)
                act.wait_ge(s["dd_ps"], GT * g + k + 1)
                act.activation(decay[:, k % 2, :], bank[3 + k % 2][:, 256:512], ACT.Exp).then_inc(s["decay_ok"], 1)
            act.wait_ge(s["h_ok"], g + 1)
            act.activation(hsq[:, :, :], hst[:, :, :], ACT.Square).then_inc(s["hsq_ok"], 1)
            rsqrt(s["hva_ok"], g + 1, hva[:, :], hln[:, :], s["hln_ok"], hrs[:, :], s["hrs_ok"], g + 1, scale=1.0 / DH)
            rsqrt(s["mv1_ok"], GT * g + GT, mv[:, :, 1], lnv[:, :], s["lnv1_ok"], rstd[:, :], s["rstd1_ok"], g + 1)
        with act.Fori(0, NG) as g:
            group_b(g)
        with act.Fori(0, NG) as g:
            act.wait_ge(s["x2T_ps"], g + 1)
            act.activation(xT[:, :], bank[0][:, :], ACT.Copy).then_inc(s["x2Ts_ok"], 1)
        act.wait_ge(s["lmax_ok"], 1)
        act.activation(lg[:, :, :], lg[:, :, :], ACT.Exp).then_inc(s["lexp_ok"], 1)
        with act.Fori(0, NG // 2) as i:
            for a in range(2):
                g = 2 * i + a
                for c in range(FC):
                    act.wait_ge(s["shu_ps"], FC * g + c + 1)
                    act.activation(shT[:, a, c, :], bank[c % 2][:, :], ACT.Gelu).then_inc(s["sh_ok"], 1)
        def gelu(t, n):
            act.wait_ge(s["up_ps"], t + 1)
            act.activation(hh[:, n % 2, :], bank[2 + n % 2][:, :], ACT.Gelu).then_inc(s["hh_ok"], 1)
        with act.Fori(0, SLOT_TILES // 2) as i:
            for n in range(2):
                gelu(2 * i + n, n)
        def last_a(g, n):
            rsqrt(s["mv2_ok"], GT * g + GT, mv[:, :, 1], lnv[:, :], s["lnv2_ok"], rstd[:, :], s["rstd2_ok"], g + 1)
            act.wait_ge(s["fin_ok"], g + 1)
            act.dma_start(out_tok[:, g4(g * GT), :], fin[:, n]).then_inc(st_o[n], 16)
        with act.Fori(0, NG // 2) as i:
            for n in range(2):
                last_a(2 * i + n, n)
        for n in range(2):
            act.wait_ge(st_o[n], 16 * NG // 2)

    @block.tensor
    def _(pe):
        mm = pe.matmul
        pe.wait_ge(s["const_p"], 3)
        pe.wait_ge(s["ld_wqk"], 16)
        for c in range(H):
            m = pe.transpose(bank[c // 4][:, (c % 4) * P:(c % 4 + 1) * P], wqk[:, c * P:(c + 1) * P], ident[:, :])
        m.then_inc(s["wqkT_ps"], 1)
        pe.wait_ge(s["ld_gw"], 32)
        for c in range(3):
            m = pe.transpose(bank[6][:, 8 * c:8 * c + 8], gw[:, c * D:(c + 1) * D], ident[0:8, 0:8])
        m.then_inc(s["gwT_ps"], 1)

        def x_turn(g):
            pe.wait_ge(s["xs_ok"], 16 * (g + 1))
            for k in range(GT):
                m = pe.transpose(bank[7][:, k * P:(k + 1) * P], xs[:, k, :], ident[:, :])
            m.then_inc(s["xT_ps"], 1)
        x_turn(0)
        pe.wait_ge(s["wqkT_ok"], 2)
        for a in range(2):
            for j in range(4):
                r = slice(a * DQ, (a + 1) * DQ)
                m = mm(bank[2 + a][:, j * P:(j + 1) * P], wqkT[r, 4 + j, :], wqkT[r, j, :], start=True, stop=True)
        m.then_inc(s["pw_ps"], 1)
        pe.wait_ge(s["pw_ok"], 2)
        pe.wait_ge(s["xT_ok"], 1)

        def z_mm(g, h, early=False):
            if not (early and h < 2):
                pe.wait_ge(s["z_ok"], H * g + h - 1)
            mm(bank[4 + h % 2][:, :], pairw[:, h, :], xT[:, :], start=True, stop=True).then_inc(s["z_ps"], 1)
        for h in range(H):
            z_mm(0, h, True)
        pe.wait_ge(s["ld_small"], 16 * 7)
        pe.wait_ge(s["const_v"], 1)

        def proj(g, k):
            pe.wait_ge(s["oT_ok"], GT * g + k + 1)
            mm(bank[k][:, 264:264 + D], oT[:, :], wo[:, :], start=True, stop=False)
            mm(bank[k][:, 264:264 + D], ones_row[:, :], bout[:, :], start=False, stop=True).then_inc(s["pr_ps"], 1)

        def group_a(g, more):
            pe.wait_ge(s["z_ok"], H * g + H)
            for k in range(GT):
                pe.wait_ge(s["res_ok"], GT * g + k + 1)
                for a in range(2):
                    q = slice(k * P + a * S, k * P + a * S + S)
                    m = mm(bank[k][a * S:(a + 1) * S, :], xT[:, q], z[:, :, q], start=True, stop=True)
                m.then_inc(s["s_ps"], 1)
            for k in range(GT):
                for a in range(2):
                    for half in range(2):
                        m = mm(bank[7][half * S:(half + 1) * S, k * P + a * 64:k * P + a * 64 + 64],
                               xT[:, k * P + a * S:k * P + a * S + S],
                               wv[:, :].rearrange("p (j e d) -> p e j d", e=2, d=DV)[:, half],
                               start=True, stop=True)
            m.then_inc(s["v_ps"], 1)
            if more:
                pe.wait_ge(s["v_ok"], 2 * g + 2)
                x_turn(g + 1)
            for k in range(GT):
                pe.wait_ge(s["exp_ok"], GT * g + k + 1)
                pe.wait_ge(s["pT_ok"], GT * g + k + 1)
                for j in range(4):
                    m = pe.transpose(bank[6][:, j * P:(j + 1) * P], prob[:, k, j * P:(j + 1) * P], ident[:, :])
                m.then_inc(s["pT_ps"], 1)
                if k:
                    proj(g, k - 1)
                if more:
                    if k == 0:
                        pe.wait_ge(s["xT_ok"], g + 2)
                    z_mm(g + 1, 2 * k)
                pe.wait_ge(s["pT_ok"], GT * g + k + 2)
                if k == 0:
                    pe.wait_ge(s["v_ok"], 2 * g + 2)
                for j in range(4):
                    for a in range(2):
                        m = mm(bank[k][a * S:(a + 1) * S, j * 34:j * 34 + 34],
                               probT[:, j * P + a * S:j * P + a * S + S],
                               vblk[:, k * 8 + a * 4 + j, :, :], start=True, stop=True)
                m.then_inc(s["av_ps"], 1)
                if more:
                    z_mm(g + 1, 2 * k + 1)
                pe.wait_ge(s["o_ok"], GT * g + k + 1)
                pe.transpose(bank[k][:, 136:136 + P], o[:, :], ident[:, :]).then_inc(s["oT_ps"], 1)
            proj(g, GT - 1)
        with pe.Fori(0, NG - 1) as g:
            group_a(g, True)
        group_a(NG - 1, False)
        pe.wait_ge(s["res_ok"], NT + GT)

        def group_b(g, first):
            pe.wait_ge(s["xs1_ok"], 16 * (g + 1))
            if not first:
                pe.wait_ge(s["x1T_ok"], g)
                pe.wait_ge(s["qblk_ok"], NH * g)
                pe.wait_ge(s["cT_ok"], g)
            for k in range(GT):
                m = pe.transpose(bank[0][:, k * P:(k + 1) * P], xs[:, k, :], ident[:, :])
            m.then_inc(s["x1T_ps"], 1)
            pe.wait_ge(s["cs_ok"], 16 * (g + 1))
            for k in range(GT):
                m = pe.transpose(bank[1][:, k * P:(k + 1) * P], cs[:, k, :], ident[:, :])
            m.then_inc(s["cT_ps"], 1)
            pe.wait_ge(s["x1T_ok"], g + 1)
            pe.wait_ge(s["cT_ok"], g + 1)
            if not first:
                pe.wait_ge(s["fpre_ok"], g)
                pe.wait_ge(s["al_ok"], g)
            mm(bank[2][0:36, :], wgx[:, :], x1T[:, :], start=True, stop=False)
            mm(bank[2][0:36, :], wgc[:, :], cT[:, :], start=False, stop=True).then_inc(s["g_ps"], 1)

            def qk(k):
                t = GT * g + k
                if not (first and k < 2):
                    pe.wait_ge(s["c_ok"], t - 1)
                if k == 0:
                    pe.wait_ge(s["qblk_ok"], NH * g + NH)
                bk = bank[3 + k % 2]
                for a in range(2):
                    m = mm(bk[a * S:(a + 1) * S, 0:256], cT[:, k * P + a * S:k * P + a * S + S],
                           qblk[:, 2 * k + a, :, :], start=True, stop=True)
                if k == 0:
                    pe.wait_ge(s["al_ok"], g + 1)
                    pause(pe, s["rh_ok"], g + 1, s["passed_pe"])
                for a in range(2):
                    mm(bk[a * S:(a + 1) * S, 256:512], al[:, k * P + a * S:k * P + a * S + S],
                       rh[:, 2 * k + a, :, :], start=True, stop=False, skip_group_check=True)
                mm(bk[:, 256:512], identb[:, :], causal[:, :], start=False, stop=True,
                   skip_group_check=True).then_inc(s["dd_ps"], 1)

            def av(k):
                pe.wait_ge(s["c_ok"], GT * g + k + 1)
                if k == 0:
                    pe.wait_ge(s["vmask_ok"], g + 1)
                    if not first:
                        pe.wait_ge(s["h_ok"], g)
                for h in range(NH):
                    for a in range(2):
                        c = (k % 2) * 132 + h * 33
                        m = mm(bank[5 + k // 2][a * S:(a + 1) * S, c:c + 33],
                               cmat[:, k % 2, h * S:(h + 1) * S],
                               vmask[:, k, a, h, :], start=True, stop=True)
                m.then_inc(s["u_ps"], 1)
            qk(0)
            pe.wait_ge(s["emx_ok"], g + 1)
            if not first:
                pe.wait_ge(s["floor_ok"], g)
            pe.sem_inc(s["passed_pe"], 1)
            for k in range(GT):
                m = pe.transpose(bank[7][:, k * NH:(k + 1) * NH], emx[:, k * P:(k + 1) * P], ident[0:NH, 0:NH])
            m.then_inc(s["en_ps"], 1)
            for k in range(1, GT):
                qk(k)
                av(k - 1)
            av(GT - 1)
        pe.wait_ge(s["const_p"], 17)
        pe.wait_ge(s["gw_ok"], 1)
        group_b(0, True)
        with pe.Fori(1, NG) as g:
            group_b(g, False)

        def group_r(g, first):
            pe.wait_ge(s["xs2_ok"], 16 * (g + 1))
            if not first:
                pe.wait_ge(s["x2Ts_ok"], g)
                pe.wait_ge(s["x2T_ok"], g)
            for k in range(GT):
                m = pe.transpose(bank[0][:, k * P:(k + 1) * P], xs[:, k, :], ident[:, :])
            m.then_inc(s["x2T_ps"], 1)
            pe.wait_ge(s["x2Ts_ok"], g + 1)
            if not first:
                pe.wait_ge(s["lg_ok"], g)
            for k in range(GT):
                m = mm(bank[1][:, k * E:(k + 1) * E], xT[:, k * P:(k + 1) * P], rw[:, :], start=True, stop=True)
            m.then_inc(s["lg_ps"], 1)
        group_r(0, True)
        with pe.Fori(1, NG) as g:
            group_r(g, False)
        pe.wait_ge(s["x2T_ok"], NG)
        pe.wait_ge(s["lg_ok"], NG)
        pe.wait_ge(s["hotb_ok"], 1)
        hb = hotb[:, :, :].rearrange("p t e -> p (t e)")
        mm(bank[6][:, 0:256], trib[:, :], hb, start=True, stop=True)
        mm(bank[6][:, 256:512], onesb[:, :], hb, start=True, stop=True).then_inc(s["rank_ps"], 1)
        pe.wait_ge(s["ld_sh"], 32)

        def sh_up_mm(g, first=False):
            for c in range(FC):
                if not (first and c < 2):
                    pe.wait_ge(s["sh_ok"], FC * g + c - 1)
                mm(bank[c % 2][:, :], sup[:, c * P:(c + 1) * P], x2T[:, bass.ds(g * W, W)],
                   start=True, stop=True).then_inc(s["shu_ps"], 1)

        def sh_down_mm(g, a, first=False):
            pe.wait_ge(s["sh_ok"], FC * g + FC)
            if not first:
                pe.wait_ge(s["base_ok"], g)
            for k in range(GT):
                for c in range(FC):
                    m = mm(bank[4 + a][:, k * D:(k + 1) * D], shT[:, a, c, k * P:(k + 1) * P], sdn[:, c, :],
                           start=(c == 0), stop=(c == FC - 1))
            m.then_inc(s["shd_ps"], 1)
        sh_up_mm(0, True)
        sh_up_mm(1)
        sh_down_mm(0, 0, True)
        with pe.Fori(1, NG // 2) as i:
            sh_up_mm(2 * i)
            sh_down_mm(2 * i - 1, 1)
            sh_up_mm(2 * i + 1)
            sh_down_mm(2 * i, 0)
        sh_down_mm(NG - 1, 1)
        pe.wait_ge(s["base_ok"], NG + 1)
        pe.wait_ge(s["texp_ok"], 1)
        pe.wait_ge(s["ld_wup"], 16)
        pe.wait_ge(s["ld_wdn"], 16)
        pe.wait_ge(s["rsteps"], 1)

        def expert(t):
            return pe.value_load(texpi[0:1, bass.ds(t, 1)], min_val=0, max_val=E - 1)

        def turn(t, n, i):
            pe.wait_ge(ld_xr[n % NX], 16 * (i + 1))
            if not (isinstance(t, int) and t < 2):
                pe.wait_ge(s["xrT_ok"], t - 1)
            pe.transpose(bank[n % 2][:, 0:P], xr[n % NX][:, 0:D], ident[:, :]).then_inc(s["xr_ps"], 1)

        def up(t, n):
            e = expert(t)
            pe.wait_ge(s["xrT_ok"], t + 1)
            if not (isinstance(t, int) and t < 2):
                pe.wait_ge(s["hh_ok"], t - 1)
            mm(bank[2 + n % 2][:, :], xrT[:, n % 2, :], wup[:, bass.ds(e * FF, FF)],
               start=True, stop=True).then_inc(s["up_ps"], 1)

        def turn_h(t, n):
            pe.wait_ge(s["hh_ok"], t + 1)
            if not (isinstance(t, int) and t < 2):
                pe.wait_ge(s["hT_ok"], t - 1)
            for c in range(FC):
                m = pe.transpose(bank[4 + n % 2][:, c * P:(c + 1) * P], hh[:, n % 2, c * P:(c + 1) * P], ident[:, :])
            m.then_inc(s["hT_ps"], 1)

        def down(t, n):
            e = expert(t)
            pe.wait_ge(s["hT_ok"], t + 1)
            if not (isinstance(t, int) and t < 2):
                pe.wait_ge(s["y_ok"], t - 1)
            for c in range(FC):
                m = mm(bank[6 + n % 2][:, 0:D], hT[:, n % 2, c * P:(c + 1) * P],
                       wdn[:, bass.ds(e * (FC * D) + c * D, D)], start=(c == 0), stop=(c == FC - 1))
            m.then_inc(s["y_ps"], 1)

        def step(t, n, i, lo=True, hi=True):
            if hi:
                turn(t, n, i)
            if (not isinstance(t, int)) or (t >= 1 and t - 1 < SLOT_TILES):
                up(t - 1, n - 1)
            if (not isinstance(t, int)) or (t >= 2 and t - 2 < SLOT_TILES):
                turn_h(t - 2, n - 2)
            if (not isinstance(t, int)) or (t >= 3 and t - 3 < SLOT_TILES):
                down(t - 3, n - 3)
        for t in range(NX):
            step(t, t, 0)
        with pe.Fori(1, SLOT_TILES // NX) as i:
            for n in range(NX):
                step(i * NX + n, n, i)
        for t in range(SLOT_TILES, SLOT_TILES + 3):
            step(t, t, 0, hi=False)

    @block.vector
    def _(dve):
        tt, tsc, stt = dve.tensor_tensor, dve.tensor_scalar, dve.scalar_tensor_tensor
        dve.sem_inc(s["res_ok"], GT)
        dve.sem_inc(s["pT_ok"], 1)
        dve.sem_inc(s["base_ok"], 1)
        st = Steps(dve, s["vsteps"])
        dve.wait_ge(s["ld_conv"], 16)
        lo = S - 1 - MAXPOS
        nn = 2 * MAXPOS + 1
        dve.tensor_copy(cpad[:, lo:lo + nn], cin[:, :]).then_inc(s["cpad_ok"], 1)
        dve.tensor_copy(cpad[:, 0:lo], cin[:, 0:1].broadcast_to([H, lo])).then_inc(s["cpad_ok"], 1)
        dve.tensor_copy(cpad[:, lo + nn:P], cin[:, nn - 1:nn].broadcast_to([H, P - lo - nn])).then_inc(s["cpad_ok"], 1)
        st(dve.memset(eps[:, :], LN_EPS))
        st(dve.memset(ones_row[:, :], 1.0))
        st(dve.memset(onesb[:, :], 1.0))
        st(dve.memset(one8[:, :], 1.0))
        st(dve.memset(vblk[:, :, :, :], 0.0))
        st(dve.memset(vblk[0:S, :, 0, DV:DV + 1], 1.0))
        st(dve.memset(vblk[S:P, :, 1, DV:DV + 1], 1.0))
        st(dve.memset(qblk[:, :, :, :], 0.0))
        st(dve.memset(vmask[:, :, :, :, :], 0.0))
        st(dve.memset(vmask[0:S, :, 0, :, DH:DH + 1], 1.0))
        st(dve.memset(vmask[S:P, :, 1, :, DH:DH + 1], 1.0))
        st(dve.memset(al[:, :], 0.0))
        st(dve.memset(al[32:36, :], 1.0))
        st(dve.memset(seqm[:, :], 1.0))
        st(dve.memset(seqm[:, :].rearrange("p (n s) -> p n s", s=S)[:, :, 0], 0.0))
        st(tsc(seqn[:, :], seqm[:, :], 1.0, BIG, ALU.subtract, ALU.mult))
        st(dve.memset(segm[:, :, :], 1.0))
        st(dve.memset(segm[:, :, 0], 0.0))
        for n in range(4):
            st(dve.memset(stg[n][:, :], 0.0))
        st(dve.memset(wgx[:, :], 0.0))
        st(dve.memset(wgc[:, :], 0.0))
        dve.wait_ge(s["ld_small"], 16 * 7)
        dve.sem_inc(s["const_v"], 1)
        st(tsc(lnw[:, :], lnw[:, :], 1.0, None, ALU.add))
        dve.wait_ge(s["gwT_ps"], 1)
        st(dve.tensor_copy(gwT[:, :, :], bank[6][:, 0:24].rearrange("p (a b) -> p a b", a=3)))
        st(dve.tensor_copy(wgx[:, 0:4], gwT[:, 0, 0:4]))
        st(dve.tensor_copy(wgx[:, 32:36], gwT[:, 0, 4:8]))
        st(tt(wgc[:, 0:4], gwT[:, 1, 0:4], gwT[:, 2, 0:4], ALU.add))
        st(tt(wgc[:, 32:36], gwT[:, 1, 4:8], gwT[:, 2, 4:8], ALU.add))
        dve.sem_inc(s["gw_ok"], 1)
        dve.wait_ge(s["ld_bias"], 32)
        dve.wait_ge(s["ld_tok"], 16)

        def layernorm(g, mv_sem, rstd_sem, src, dst, done):
            dve.wait_ge(rstd_sem, g + 1)
            for k in range(GT):
                tsc(dst[:, k, :], src[:, k, :], mv[:, k, 0:1], rstd[:, k:k + 1],
                    ALU.subtract, ALU.mult).then_inc(done, 1)

        def scores(g, k, st):
            dve.wait_ge(s["s_ps"], GT * g + k + 1)
            p3 = prob[:, k, :].rearrange("p (h j) -> p h j", h=H)
            st(tt(prob[:, k, :], bank[k][:, :], bias[:, :, :].rearrange("p h j -> p (h j)"), ALU.add))
            st(dve.tensor_reduce(negmax[:, k, :], p3, AX.X, ALU.max))
            tt(p3, p3, spread(negmax[:, k, :], [P, H, S]), ALU.subtract).then_inc(s["logit_ok"], 1)

        def head_out(g, k, st):
            dve.wait_ge(s["av_ps"], GT * g + k + 1)
            u = bank[k][:, 0:136].rearrange("p (h d) -> p h d", h=H)
            st(dve.reciprocal(rden[:, k, :], u[:, :, DV]))
            tt(o[:, :].rearrange("p (h d) -> p h d", h=H), u[:, :, 0:DV],
               spread(rden[:, k, :], [P, H, DV]), ALU.mult).then_inc(s["o_ok"], 1)

        def residual(g, k):
            dve.wait_ge(s["pr_ps"], GT * g + k + 1)
            tt(res[:, k, :], bank[k][:, 264:264 + D], tok[:, g * GT + k, :], ALU.add).then_inc(s["res_ok"], 1)
            dve.wait_ge(s["res_ok"], GT * g + k + 1 + GT)
            dve.bn_stats(stats[:, k, :], res[:, k, :]).then_inc(s["stat_ok"], 1)
            pause(dve, s["stat_ok"], GT * g + k + 1, s["passed_dve"])
            dve.bn_aggr(mv[:, k, :], stats[:, k, :]).then_inc(s["mv_ok"], 1)

        ast = Steps(dve, s["asteps"])
        A_STEPS = 3 * GT
        def group_a(g):
            ast.start(g * A_STEPS)
            scores(g, 0, ast)
            scores(g, 1, ast)
            scores(g, 2, ast)
            head_out(g, 0, ast)
            scores(g, 3, ast)
            residual(g, 0)
            for k in range(1, GT):
                head_out(g, k, ast)
                residual(g, k)
            assert ast.n == A_STEPS
            layernorm(g, s["mv_ok"], s["rstd_ok"], res, tok[:, g4(g * GT), :], s["x1_ok"])
        with dve.Fori(0, NG) as g:
            group_a(g)

        dve.wait_ge(s["const_p"], 17)
        ist = Steps(dve, s["igsteps"])
        bst = Steps(dve, s["bsteps"])
        I_STEPS, B_STEPS = 3, 15

        def group_b(g):
            ist.start(g * I_STEPS)
            bst.start(g * B_STEPS)
            dve.wait_ge(s["cs_ok"], 16 * (g + 1))
            for a in range(2):
                r = slice(a * S, (a + 1) * S)
                m = dve.tensor_copy(vmask[r, :, a, :, 0:DH], cs[r, :, :].rearrange("p k (h d) -> p k h d", h=NH))
                if a == 0:
                    bst(m)
            m.then_inc(s["vmask_ok"], 1)
            dve.wait_ge(s["flog_ok"], g + 1)
            ist(stt(logf[:, :], fpre[:, :], 0.0, flog[:, :], ALU.min, ALU.subtract))
            ist(dve.tensor_tensor_scan(cumf[:, :], seqm[:, :], logf[:, :], 0.0, ALU.mult, ALU.add))
            dve.wait_ge(s["g_ps"], g + 1)
            stt(al[0:NH, :], bank[2][0:NH, :], bi[:, 0:1], cumf[:, :], ALU.add, ALU.subtract).then_inc(s["al_ok"], 1)
            dve.wait_ge(s["al_ok"], g + 1)
            ist(dve.tensor_tensor_scan(amax[:, :], seqn[:, :], al[0:NH, :], -BIG, ALU.add, ALU.max))
            tt(rh[32:36, :, :, :], nhot[:, :, :].unsqueeze(1).broadcast_to([NH, 2 * GT, NH, S]),
               amax[:, :].rearrange("p (n s) -> p n s", s=S).unsqueeze(2).broadcast_to([NH, 2 * GT, NH, S]),
               ALU.mult).then_inc(s["rh_ok"], 1)
            tt(mrow[:, :], cumf[:, :], amax[:, :], ALU.add).then_inc(s["mrow_ok"], 1)
            assert ist.n == I_STEPS
            for k in range(GT):
                dve.wait_ge(s["decay_ok"], GT * g + k + 1)
                stt(cmat[:, k % 2, :], bank[3 + k % 2][:, 0:256], DH ** -0.5, decay[:, k % 2, :],
                    ALU.mult, ALU.mult).then_inc(s["c_ok"], 1)
                if k % 2 == 0 and k:
                    cell(g, k // 2 - 1)
            cell(g, 1)
            bst(dve.tensor_reduce(hmu[:, :], hst[:, :, :], AX.X, ALU.add))
            bst(tsc(hmu[:, :], hmu[:, :], 1.0 / DH, None, ALU.mult))
            tt(hst[:, :, :], hst[:, :, :], spread(hmu[:, :], [P, GT * NH, DH]), ALU.subtract).then_inc(s["h_ok"], 1)
            dve.wait_ge(s["hsq_ok"], g + 1)
            dve.tensor_reduce(hva[:, :], hsq[:, :, :], AX.X, ALU.add).then_inc(s["hva_ok"], 1)
            dve.wait_ge(s["hrs_ok"], g + 1)
            bst(tt(hst[:, :, :], hst[:, :, :], spread(hrs[:, :], [P, GT * NH, DH]), ALU.mult))
            h3 = hst[:, :, :].rearrange("p (k h) d -> p k (h d)", k=GT)
            bst(tt(h3, h3, lnw[:, :].unsqueeze(1).broadcast_to([P, GT, D]), ALU.mult))
            tt(res[:, :, :], h3, tok[:, g4(g * GT), :], ALU.add).then_inc(s["res1_ok"], 1)
            dve.wait_ge(s["res1_ok"], g + 1)
            for k in range(GT):
                m = dve.bn_stats(stats[:, k, :], res[:, k, :])
            bst(m)
            dve.sem_inc(s["passed_dve"], 1)
            for k in range(GT):
                dve.bn_aggr(mv[:, k, :], stats[:, k, :]).then_inc(s["mv1_ok"], 1)
            assert bst.n == B_STEPS, bst.n
            layernorm(g, s["mv1_ok"], s["rstd1_ok"], res, tok[:, g4(g * GT), :], s["x2_ok"])

        def cell(g, j):
            dve.wait_ge(s["u_ps"], GT * g + 2 * j + 2)
            dve.wait_ge(s["floor_ok"], g + 1)
            u = bank[5 + j][:, 0:264].rearrange("p (n d) -> p n d", d=DH + 1)
            nv = nrm[:, 2 * j:2 * j + 2, :].rearrange("p k h -> p (k h)")
            bst(dve.tensor_reduce(nv, u[:, :, DH:DH + 1], AX.X, ALU.max, apply_absolute_value=True))
            bst(tt(nv, nv, floor[:, 2 * j:2 * j + 2, :].rearrange("p k h -> p (k h)"), ALU.max))
            bst(tsc(nv, nv, 1e-6, None, ALU.add))
            bst(dve.reciprocal(nv, nv))
            m = tt(hst[:, 8 * j:8 * j + 8, :], u[:, :, 0:DH], spread(nv, [P, 8, DH]), ALU.mult)
            if j == 1:
                bst(m)
        with dve.Fori(0, NG) as g:
            group_b(g)

        with dve.Fori(0, NG) as g:
            pause(dve, s["x2Ts_ok"], g + 1, s["passed_dve"])
            dve.tensor_copy(x2T[:, bass.ds(g * W, W)], xT[:, :]).then_inc(s["x2T_ok"], 1)
            pause(dve, s["lg_ps"], g + 1, s["passed_dve"])
            dve.tensor_copy(lg[:, g4(g * GT), :], bank[1][:, 0:GT * E].rearrange("p (k e) -> p k e", k=GT)).then_inc(s["lg_ok"], 1)
        r = Steps(dve, s["rsteps"])
        dve.wait_ge(s["lg_ok"], NG)
        full = [P, NT, E]
        r(dve.tensor_reduce(m8[:, :], lg[:, :, :], AX.X, ALU.max))
        tt(lg[:, :, :], lg[:, :, :], spread(m8[:, :], full), ALU.subtract).then_inc(s["lmax_ok"], 1)
        dve.wait_ge(s["lexp_ok"], 1)
        r(dve.tensor_reduce(m8[:, :], lg[:, :, :], AX.X, ALU.add))
        r(dve.reciprocal(m8[:, :], m8[:, :]))
        r(tt(lg[:, :, :], lg[:, :, :], spread(m8[:, :], full), ALU.mult))
        for k in range(2):
            r(dve.tensor_reduce(gate[k][:, :], lg[:, :, :], AX.X, ALU.max))
            r(tt(cand[:, :, :], lg[:, :, :], spread(gate[k][:, :], full), ALU.is_equal))
            r(tt(cand[:, :, :], cand[:, :, :], io_e[:, :].unsqueeze(1).broadcast_to(full), ALU.mult))
            r(dve.tensor_reduce(m8[:, :], cand[:, :, :], AX.X, ALU.max))
            r(tt(hot[k][:, :, :], cand[:, :, :], spread(m8[:, :], full), ALU.is_equal))
            if k == 0:
                r(stt(lg[:, :, :], hot[0][:, :, :], -2.0, lg[:, :, :], ALU.mult, ALU.add))
        tt(hotb[:, :, :], hot[0][:, :, :], hot[1][:, :, :], ALU.add).then_inc(s["hotb_ok"], 1)
        dve.wait_ge(s["rank_ps"], 1)
        r(dve.tensor_copy(tote[:, :, :], bank[6][:, 256:512].rearrange("p (t e) -> p e t", e=E)))
        fl = lambda a: a[:, :, :].rearrange("p e t -> p (e t)")
        r(dve.tensor_tensor_scan(fl(cume), fl(segm), fl(tote), 0.0, ALU.mult, ALU.add))
        r(tt(gt[:, :, :], spread(cume[:, :, NT - 1], [P, E, NT]), io_128[:, :].unsqueeze(1).broadcast_to([P, E, NT]), ALU.is_gt))
        r(dve.tensor_reduce(ntile[:, :], gt[:, :, :], AX.X, ALU.add))
        r(dve.tensor_tensor_scan(ctile[:, :], one8[:, :], ntile[:, :], 0.0, ALU.mult, ALU.add))
        r(tt(cume[:, :, :], cume[:, :, :], tote[:, :, :], ALU.subtract))
        r(tt(sl[:, :, :], bank[6][:, 0:256].rearrange("p (t e) -> p t e", e=E), cume[:, :, :].rearrange("p e t -> p t e"), ALU.add))
        r(tt(ntile[:, :], ctile[:, :], ntile[:, :], ALU.subtract))
        r(stt(sl[:, :, :], ntile[:, :].unsqueeze(1).broadcast_to(full), float(P), sl[:, :, :], ALU.mult, ALU.add))
        for k in range(2):
            r(tt(cand[:, :, :], sl[:, :, :], hot[k][:, :, :], ALU.mult))
            r(dve.tensor_reduce(slotf[:, :], cand[:, :, :], AX.X, ALU.add))
            r(dve.tensor_copy(slot[k][:, :], slotf[:, :]))
        r(tt(tcmp[:, :, :], ctile[0:1, :].unsqueeze(1).broadcast_to([1, SLOT_TILES, E]),
             spread(io_tau[:, :], [1, SLOT_TILES, E]), ALU.is_le))
        r(dve.tensor_reduce(texp[:, :], tcmp[:, :, :], AX.X, ALU.add))
        r(tsc(texp[:, :], texp[:, :], float(E - 1), None, ALU.min))
        dve.tensor_copy(texpi[:, :], texp[:, :]).then_inc(s["texp_ok"], 1)

        def stage(i, n, t, k, first):
            if not first:
                pause(dve, scat[n], 16 * i, s["passed_dve"])
            dve.tensor_copy(stg[n][:, 0:D], tok[:, t, :])
            dve.tensor_copy(stg[n][:, GATE:GATE + 1], gate[k][:, bass.ds(t, 1)])
            dve.tensor_copy(stg[n][:, :].bitcast(I32)[:, DEST:DEST + 1], dest[:, k, bass.ds(t, 1)])
            dve.tensor_copy(idx[n][:, :], slot[k][:, bass.ds(t, 1)]).then_inc(s["stage_ok"], 1)

        def two_groups(i, first):
            for a in range(2):
                g = 2 * i + a
                for n in range(2 * GT):
                    stage(2 * g + n // 4, n % 4, g * GT + n // 2, n % 2, first and a == 0 and n < 4)
                dve.wait_ge(s["shd_ps"], g + 1)
                dve.wait_ge(s["stage_ok"], 2 * GT * (g + 1))
                tg = tok[:, g4(g * GT), :]
                stt(tg, tg, 2.0, bank[4 + a][:, :].rearrange("p (k d) -> p k d", k=GT),
                    ALU.mult, ALU.add).then_inc(s["base_ok"], 1)
        two_groups(0, True)
        with dve.Fori(1, NG // 2) as i:
            two_groups(i, False)

        def x_out(t, n):
            dve.wait_ge(s["xr_ps"], t + 1)
            dve.tensor_copy(xrT[:, n % 2, :], bank[n % 2][:, 0:P]).then_inc(s["xrT_ok"], 1)

        def h_out(t, n):
            dve.wait_ge(s["hT_ps"], t + 1)
            dve.tensor_copy(hT[:, n % 2, :], bank[4 + n % 2][:, :]).then_inc(s["hT_ok"], 1)

        def y_out(t, n, times):
            dve.wait_ge(s["y_ps"], t + 1)
            if not (isinstance(t, int) and t < 4):
                dve.wait_ge(sc_y[n % 4], 16 * times)
            tsc(yr[n % 4][:, :], bank[6 + n % 2][:, 0:D], xr[n % NX][:, GATE:GATE + 1], None,
                ALU.mult).then_inc(s["y_ok"], 1)

        def step(t, n, i):
            known = isinstance(t, int)
            if not known or t < SLOT_TILES:
                x_out(t, n)
            if not known or (t >= 2 and t - 2 < SLOT_TILES):
                h_out(t - 2, n - 2)
            if not known or (t >= 3 and t - 3 < SLOT_TILES):
                y_out(t - 3, n - 3, (t - 3) // 4 if known else 2 * i + (n - 3) // 4)
        for t in range(NX):
            step(t, t, 0)
        with dve.Fori(1, SLOT_TILES // NX) as i:
            for n in range(NX):
                step(i * NX + n, n, i)
        for t in range(SLOT_TILES, SLOT_TILES + 3):
            step(t, t, 0)

        fst = Steps(dve, s["fsteps"])
        F_STEPS = 3

        def last(g, n, i, first):
            fst.start(g * F_STEPS)
            dve.wait_ge(ld_y0[n], 16 * (i + 1))
            dve.wait_ge(ld_y1[n], 16 * (i + 1))
            if not first:
                dve.wait_ge(st_o[n], 16 * i)
            if not (first and n == 0):
                dve.wait_ge(s["fin_ok"], g)
            fst(tt(res[:, :, :], y0[:, n], tok[:, g4(g * GT), :], ALU.add))
            fst(tt(res[:, :, :], res[:, :, :], y1[:, n], ALU.add))
            for k in range(GT):
                m = dve.bn_stats(stats[:, k, :], res[:, k, :])
            fst(m)
            dve.sem_inc(s["passed_dve"], 1)
            for k in range(GT):
                dve.bn_aggr(mv[:, k, :], stats[:, k, :]).then_inc(s["mv2_ok"], 1)
            dve.wait_ge(s["rstd2_ok"], g + 1)
            for k in range(GT):
                m = tsc(fin[:, n, k, :], res[:, k, :], mv[:, k, 0:1], rstd[:, k:k + 1], ALU.subtract, ALU.mult)
            m.then_inc(s["fin_ok"], 1)
        for n in range(2):
            last(n, n, 0, True)
        with dve.Fori(1, NG // 2) as i:
            for n in range(2):
                last(2 * i + n, n, i, False)

    es.close()


_INS = ['x', 'ctx_1024', 'L0_attn_W_qk', 'L0_attn_W_v', 'L0_attn_W_out', 'L0_attn_b_out', 'L0_attn_conv',
        'L0_xattn_w_igate', 'L0_xattn_b_igate', 'L0_xattn_w_fgate', 'L0_xattn_b_fgate', 'L0_xattn_ln_weight',
        'L0_ffn_shared_up', 'L0_ffn_shared_down', 'L0_ffn_routed_up', 'L0_ffn_routed_down', 'L0_ffn_router_w']


def kernel(**inputs):
    import numpy as _np
    import concourse.bacc as _bacc
    from concourse import mybir as _mybir
    from concourse.bass_utils import run_bass_kernel_spmd as _run

    nc = _bacc.Bacc("TRN2", target_bir_lowering=False, num_devices=1)
    arrays, args = {}, []
    for name in _INS:
        a = _np.ascontiguousarray(inputs[name])
        arrays[f"in_{name}"] = a
        args.append(nc.dram_tensor(f"in_{name}", a.shape, _mybir.dt.from_np(a.dtype), kind="ExternalInput").ap())
    out = nc.dram_tensor("out_x", (64, 64, 128), _mybir.dt.float32, kind="ExternalOutput").ap()
    decoder_layer(nc, *args, out)
    r = _run(nc, [arrays], core_ids=[0])
    return r.results[0]["out_x"]
```

```python
import concourse.bass as bass
from concourse import mybir
from contextlib import ExitStack

F32 = mybir.dt.float32
BF16 = mybir.dt.bfloat16
I32 = mybir.dt.int32
ALU = mybir.AluOpType
ACT = mybir.ActivationFunctionType
AX = mybir.AxisListType

P = 128
B, S, D = 64, 64, 128
NT = B * S // P
GT = 4
NG = NT // GT
W = GT * P
H, DQ = 8, 64
DV = D // H
MAXPOS = 10
NH, DH = 4, 32
FF, E = 512, 8
FC = FF // P
SLOT_TILES = 2 * NT + E
ROW = D + 4
GATE, DEST = D, D + 1
DUMP = 9
BIG = 1e30
LN_EPS = 1e-5
N_CONST, N_TABLES = 14, 18


class Steps:

    def __init__(self, eng, sem):
        self.eng, self.sem, self.base, self.n = eng, sem, 0, 0

    def __call__(self, ins):
        self.n += 1
        ins.then_inc(self.sem, 1)
        self.eng.wait_ge(self.sem, self.base + self.n)

    def start(self, base):
        self.base, self.n = base, 0


def pause(eng, sem, value, passed):
    eng.wait_ge(sem, value)
    eng.sem_inc(passed, 1)


def spread(ap, shape):
    return ap.unsqueeze(len(shape) - 1).broadcast_to(shape)


def decoder_layer(nc, x, ctx_in, w_qk, w_v, w_out, b_out, conv, w_ig, b_ig, w_fg, b_fg, ln_w,
                  sh_up, sh_down, ro_up, ro_down, router_w, out):
    es = ExitStack()

    def sb(name, shape, dt=F32):
        return es.enter_context(nc.sbuf_tensor(name, shape, dt))

    def sem(name):
        return es.enter_context(nc.semaphore(name))

    bank = [es.enter_context(nc.psum_tensor(f"bank{n}", [P, 512], F32)) for n in range(8)]

    x_tok = x.rearrange("(t a) s d -> (a s) t d", a=2)
    ctx_tok = ctx_in.rearrange("(t a) s d -> (a s) t d", a=2)
    out_tok = out.rearrange("(t a) s d -> (a s) t d", a=2)
    conv_pad = nc.dram_tensor("conv_pad", (H, S, P), F32, kind="Internal").ap()
    slots = nc.dram_tensor("slots", (SLOT_TILES * P, ROW), F32, kind="Internal").ap()
    routed = nc.dram_tensor("routed", (2 * B * S + DUMP * P, D), F32, kind="Internal").ap()

    tok = sb("tok", [P, NT, D])
    x2T = sb("x2T", [P, NT * P])
    wup = sb("wup", [P, E * FF])
    wdn = sb("wdn", [P, E * FC * D])
    sup = sb("sup", [P, FF])
    sdn = sb("sdn", [P, FC, D])
    ident = sb("ident", [P, P])
    identb = sb("identb", [P, P], BF16)
    onesb = sb("onesb", [P, P], BF16)
    trib = sb("trib", [P, P], BF16)
    causal = sb("causal", [P, NH * S], BF16)
    eps = sb("eps", [P, 1])
    bout = sb("bout", [P, D])
    wv = sb("wv", [P, D])
    wo = sb("wo", [P, D])
    pairw = sb("pairw", [P, H, D])
    cpad = sb("cpad", [H, P])
    cin = sb("cin", [H, 2 * MAXPOS + 1])
    bias = sb("bias", [P, H, S])
    gw = sb("gw", [2 * NH, 3 * D])
    gwT = sb("gwT", [P, 3, 2 * NH])
    GR = 2 * GT * NH
    wg = [sb(f"wg{n}", [P, 2 * GT, 2 * GR]) for n in range(2)]
    bi = sb("bi", [GR, 1])
    bf = sb("bf", [GR, 1])
    lnw = sb("lnw", [P, D])
    rw = sb("rw", [P, E])
    xs = sb("xs", [P, GT, D])
    xT = sb("xT", [P, W])
    z = sb("z", [P, H, W])
    prob = sb("prob", [P, GT, H * S])
    wqk = prob[:, 0:2, :].rearrange("p a b -> p (a b)")
    wqkT = prob[:, 2:4, :].rearrange("p a (b c) -> p (a b) c", c=P)
    negmax = sb("negmax", [P, GT, H])
    probT = sb("probT", [P, GT * P])
    vblk = sb("vblk", [P, GT * 8, 2, DV + 1])
    rden = sb("rden", [P, GT, H])
    o = sb("o", [P, D])
    oT = sb("oT", [P, P])
    res = sb("res", [P, GT, D])
    stats = sb("stats", [P, GT, 6])
    mv = sb("mv", [P, GT, 2])
    lnv = sb("lnv", [P, GT])
    rstd = sb("rstd", [P, GT])
    cs = sb("cs", [P, GT, D])
    x1T = sb("x1T", [P, W])
    cT = [sb(f"cT{n}", [P, W]) for n in range(2)]
    qblk = [sb(f"qblk{n}", [P, 2 * GT, NH, S]) for n in range(2)]
    vmask = [sb(f"vmask{n}", [P, GT, 2, NH, DH + 1]) for n in range(2)]
    fpre = sb("fpre", [GR, S])
    ipre = sb("ipre", [GR, S])
    flog = sb("flog", [GR, S])
    logf = sb("logf", [GR, S])
    cumf = sb("cumf", [GR, S])
    arow = sb("arow", [GR, S])
    amax = sb("amax", [GR, S])
    one_s = sb("one_s", [GR, S])
    zero_s = sb("zero_s", [GR, S])
    emx = sb("emx", [GR, S])
    mrow = sb("mrow", [GR, S])
    al = [sb(f"al{n}", [2 * GR, S]) for n in range(2)]
    rh = [sb(f"rh{n}", [2 * GR, 2 * GT, NH, S]) for n in range(2)]
    nhot = sb("nhot", [GR, GR])
    decay = sb("decay", [P, 2, NH * S])
    cmat = sb("cmat", [P, 2, NH * S])
    floor = [sb(f"floor{n}", [P, GT, NH]) for n in range(2)]
    nrm = sb("nrm", [P, GT, NH])
    hst = sb("hst", [P, GT * NH, DH])
    hmu = sb("hmu", [P, GT * NH])
    hsq = sb("hsq", [P, GT * NH, DH])
    hlw = sb("hlw", [P, GT * NH, DH])
    x2s = sb("x2s", [P, GT, D])
    hva = sb("hva", [P, GT * NH])
    hln = sb("hln", [P, GT * NH])
    hrs = sb("hrs", [P, GT * NH])
    resf = [z[:, n, :].rearrange("p (k d) -> p k d", k=GT) for n in range(2)]
    sumf = [z[:, 2 + n, :].rearrange("p (k d) -> p k d", k=GT) for n in range(2)]
    mvf = [sb(f"mvf{n}", [P, GT, 2]) for n in range(2)]
    rstdf = [sb(f"rstdf{n}", [P, GT]) for n in range(2)]
    shift = [sb(f"shift{n}", [P, GT]) for n in range(2)]
    lg = sb("lg", [P, NT, E])
    m8 = sb("m8", [P, NT])
    cand = sb("cand", [P, NT, E])
    hot = [sb(f"hot{k}", [P, NT, E]) for k in range(2)]
    hotb = sb("hotb", [P, NT, E], BF16)
    gate = [sb(f"gate{k}", [P, NT]) for k in range(2)]
    io_e = sb("io_e", [P, E])
    io_128 = sb("io_128", [P, NT])
    io_tau = sb("io_tau", [1, SLOT_TILES])
    tote = sb("tote", [P, E, NT])
    cume = sb("cume", [P, E, NT])
    segm = sb("segm", [P, E, NT])
    one8 = sb("one8", [P, E])
    ntile = sb("ntile", [P, E])
    ctile = sb("ctile", [P, E])
    gt = sb("gt", [P, E, NT])
    sl = sb("sl", [P, NT, E])
    slot = [sb(f"slot{k}", [P, NT], I32) for k in range(2)]
    slotf = sb("slotf", [P, NT])
    dest = sb("dest", [P, 2, NT], I32)
    tcmp = sb("tcmp", [1, SLOT_TILES, E])
    texp = sb("texp", [1, SLOT_TILES])
    texpi = sb("texpi", [1, SLOT_TILES], I32)
    prefill = sb("prefill", [P, DUMP, ROW])
    stg = [sb(f"stg{n}", [P, ROW]) for n in range(4)]
    idx = [sb(f"idx{n}", [P, 1], I32) for n in range(4)]
    shT = z[:, :, :].rearrange("p (a c) w -> p a c w", a=2)
    NX = 8
    qflat = qblk[0][:, :, :, :].rearrange("p n h s -> p (n h s)")
    xr = [qflat[:, n * ROW:(n + 1) * ROW] for n in range(NX)]
    yr = [qflat[:, NX * ROW + n * D:NX * ROW + (n + 1) * D] for n in range(4)]
    xrT = cT[0][:, 0:2 * P].rearrange("p (a d) -> p a d", a=2)
    hh = prob[:, 0:2, :]
    hT = prob[:, 2:4, :]
    y0, y1, fin = (x2T[:, n * 2 * W:(n + 1) * 2 * W].rearrange("p (a k d) -> p a k d", a=2, k=GT) for n in range(3))

    names = """ld_tok ld_wqk ld_conv ld_cpad ld_bias ld_small ld_gw ld_wup ld_wdn ld_sh st_cpad cpad_ok
    const_p const_v wqkT_ps wqkT_ok pw_ps pw_ok gwT_ps gw_ok vsteps bias_ok
    xs_ok xT_ps xT_ok z_ps z_ok s_ps v_ps v_ok logit_ok exp_ok pT_ps pT_ok av_ps o_ok oT_ps oT_ok
    pr_ps res_ok stat_ok mv_ok lnv_ok rstd_ok x1_ok asteps
    xs1_ok cs_ok x1T_ps x1T_ok cT_ps cT_ok g_ps fpre_ok fabs_ok fexp_ok flog_ok igsteps al_ok rh_ok
    mrow_ok emx_ok en_ps floor_ok qblk_ok vmask_ok dd_ps decay_ok c_ok u_ps h_ok hsteps hsq_ok hva_ok
    hln_ok hrs_ok res1_ok mv1_ok lnv1_ok rstd1_ok x2_ok bsteps
    xs2_ok x2T_ps x2T_ok x2Ts_ok lg_ps lg_ok lmax_ok lexp_ok tokb_ok lnd_ok fl_ps hlw_ok tk_ok x2e_ok presum_ok shift_ok rsteps hotb_ok rank_ps slot_ok texp_ok
    stage_ok scat0 scat1 scat2 scat3 pre_ok shu_ps sh_ok shd_ps base_ok
    xr_ps xrT_ok up_ps hh_ok hT_ps hT_ok y_ps y_ok
    passed_pool passed_dve passed_pe fsteps mv2_ok lnv2_ok rstd2_ok fin_ok st_out""".split()
    s = {n: sem(n) for n in names}
    ld_xr = [sem(f"ld_xr{n}") for n in range(NX)]
    sc_y = [sem(f"sc_y{n}") for n in range(4)]
    ld_y0 = [sem(f"ld_y0_{n}") for n in range(2)]
    ld_y1 = [sem(f"ld_y1_{n}") for n in range(2)]
    scat = [s[f"scat{n}"] for n in range(4)]
    st_o = [sem(f"st_o{n}") for n in range(2)]

    def g4(t):
        return bass.ds(t, GT)

    block = es.enter_context(nc.Block())

    @block.sync
    def _(sp):
        sp.dma_start(wqk, w_qk).then_inc(s["ld_wqk"], 16)
        sp.dma_start(xs[:, :, :], x_tok[:, 0:GT, :]).then_inc(s["xs_ok"], 16)
        sp.dma_start(cin[:, :], conv).then_inc(s["ld_conv"], 16)
        sp.wait_ge(s["cpad_ok"], 3)
        sp.dma_start(conv_pad, cpad[:, :].unsqueeze(1).broadcast_to([H, S, P])).then_inc(s["st_cpad"], 16)
        sp.wait_ge(s["st_cpad"], 16)
        for a in range(2):
            src = bass.AP(tensor=conv_pad.tensor, offset=S - 1, ap=[[P - 1, S], [S * P, H], [1, S]])
            sp.dma_start(bias[a * S:(a + 1) * S, :, :], src).then_inc(s["ld_bias"], 16)
        sp.dma_start(tok[:, :, :], x_tok).then_inc(s["ld_tok"], 16)
        sp.dma_start(gw[0:NH, :], w_ig).then_inc(s["ld_gw"], 16)
        sp.dma_start(gw[NH:2 * NH, :], w_fg).then_inc(s["ld_gw"], 16)
        with sp.Fori(1, NG) as g:
            sp.wait_ge(s["xT_ps"], g)
            sp.dma_start(xs[:, :, :], x_tok[:, g4(g * GT), :]).then_inc(s["xs_ok"], 16)
        sp.wait_ge(s["pre_ok"], 1)
        for n in range(SLOT_TILES // DUMP):
            sp.dma_start(slots[n * DUMP * P:(n + 1) * DUMP * P, :].rearrange("(b p) r -> p b r", p=P),
                         prefill[:, :, :]).then_inc(s["st_out"], 16)
        sp.dma_start(sup[:, :], sh_up[0]).then_inc(s["ld_sh"], 16)
        sp.dma_start(sdn[:, :, :], sh_down[0].rearrange("(c p) h -> p c h", p=P)).then_inc(s["ld_sh"], 16)
        sp.dma_start(wup[:, :].rearrange("p (e f) -> p e f", e=E), ro_up.rearrange("e h f -> h e f")).then_inc(s["ld_wup"], 16)
        sp.dma_start(wdn[:, :].rearrange("p (e c h) -> p e c h", e=E, c=FC),
                     ro_down.rearrange("e (c p) h -> p e c h", p=P)).then_inc(s["ld_wdn"], 16)

        def stage_b(g, q, first):
            if not first:
                sp.wait_ge(s["x1T_ps"], g)
                sp.wait_ge(s["cT_ps"], g)
            sp.wait_ge(s["x1_ok"], GT * g + GT)
            sp.dma_start(xs[:, :, :], tok[:, g4(g * GT), :]).then_inc(s["xs1_ok"], 16)
            sp.dma_start(cs[:, :, :], ctx_tok[:, g4(g * GT), :]).then_inc(s["cs_ok"], 16)
            if not (isinstance(g, int) and g < 2):
                sp.wait_ge(s["u_ps"], GT * (g - 1))
            for a in range(2):
                r = slice(a * S, (a + 1) * S)
                for k in range(GT):
                    sp.dma_start(vmask[q][r, k, a, :, 0:DH],
                                 ctx_in[bass.ds(2 * GT * g + 2 * k + a, 1), :, :].rearrange("a s (h d) -> (a s) h d", h=NH))\
                      .then_inc(s["vmask_ok"], 16)

        def keep_x2(g):
            sp.wait_ge(s["x2_ok"], GT * g + GT)
            sp.dma_start(tok[:, g4(g * GT), :], x2s[:, :, :]).then_inc(s["tk_ok"], 16)
        sp.wait_ge(s["xT_ps"], NG)
        sp.wait_ge(s["const_v"], 1)
        stage_b(0, 0, True)
        stage_b(1, 1, False)
        keep_x2(0)
        with sp.Fori(0, (NG - 2) // 2) as i:
            for n in range(2):
                stage_b(2 * i + 2 + n, n, False)
                keep_x2(2 * i + 1 + n)
        keep_x2(NG - 1)
        for n in range(4):
            sp.wait_ge(scat[n], 16 * 2 * NT // 4)
        def load_slots(t, n):
            sp.dma_start(xr[n][:, :], slots[bass.ds(t * P, P), :]).then_inc(ld_xr[n], 16)
        for n in range(NX):
            load_slots(n, n)
        with sp.Fori(1, SLOT_TILES // NX) as i:
            for n in range(NX):
                sp.wait_ge(sc_y[n % 4], 16 * (2 * i - 1 + n // 4))
                load_slots(i * NX + n, n)
        for n in range(4):
            sp.wait_ge(sc_y[n], 16 * SLOT_TILES // 4)
        def final(g, n, first):
            if not first:
                sp.wait_ge(s["stat_ok"], NT + g - 1)
            sp.dma_start(y0[:, n], routed[bass.ds(g * W, W), :].rearrange("(t p) d -> p t d", p=P)).then_inc(ld_y0[n], 16)
            sp.dma_start(y1[:, n], routed[bass.ds(g * W + B * S, W), :].rearrange("(t p) d -> p t d", p=P)).then_inc(ld_y1[n], 16)
        final(0, 0, True)
        final(1, 1, True)
        with sp.Fori(1, NG // 2) as i:
            for n in range(2):
                final(2 * i + n, n, False)

    @block.gpsimd
    def _(pool):
        st = Steps(pool, s["const_p"])
        st(pool.memset(ident[:, :], 0.0))
        st(pool.affine_select(out=ident[:, :], in_=ident[:, :], compare_op=ALU.not_equal, fill=1.0,
                              base=0, pattern=[[-1, P]], channel_multiplier=1))
        st(pool.tensor_copy(identb[:, :], ident[:, :]))
        st(pool.memset(causal[:, :], 0.0))
        for a in range(2):
            v = causal[a * S:(a + 1) * S, :].rearrange("p (h s) -> p h s", h=NH)
            st(pool.affine_select(out=v, in_=v, compare_op=ALU.is_ge, fill=-BIG, base=0,
                                  pattern=[[0, NH], [1, S]], channel_multiplier=-1))
        st(pool.memset(trib[:, :], 1.0))
        st(pool.affine_select(out=trib[:, :], in_=trib[:, :], compare_op=ALU.is_gt, fill=0.0, base=0,
                              pattern=[[1, P]], channel_multiplier=-1))
        for q in range(2):
            v = rh[q][GR:2 * GR, :, :, :]
            st(pool.memset(v, 1.0))
            st(pool.affine_select(out=v, in_=v, compare_op=ALU.is_equal, fill=0.0, base=0,
                                  pattern=[[NH, 2 * GT], [1, NH], [0, S]], channel_multiplier=-1))
        st(pool.memset(nhot[:, :], -1.0))
        st(pool.affine_select(out=nhot[:, :], in_=nhot[:, :], compare_op=ALU.is_equal, fill=0.0,
                              base=0, pattern=[[1, GR]], channel_multiplier=-1))
        st(pool.iota(io_e[:, :], [[-1, E]], base=E, channel_multiplier=0, allow_small_or_imprecise_dtypes=True))
        st(pool.iota(io_128[:, :], [[P, NT]], base=0, channel_multiplier=0, allow_small_or_imprecise_dtypes=True))
        st(pool.iota(io_tau[:, :], [[1, SLOT_TILES]], base=0, channel_multiplier=0, allow_small_or_imprecise_dtypes=True))
        st(pool.iota(dest[:, :, :], [[B * S, 2], [P, NT]], base=0, channel_multiplier=1))
        st(pool.memset(prefill[:, :, :], 0.0))
        pool.iota(prefill[:, :, :].bitcast(I32)[:, :, DEST], [[P, DUMP]], base=2 * B * S,
                  channel_multiplier=1).then_inc(s["pre_ok"], 1)
        pool.wait_ge(s["ld_tok"], 16)
        pool.wait_ge(s["ld_small"], 16 * 7)
        pool.tensor_tensor(tok[:, :, :], tok[:, :, :], bout[:, :].unsqueeze(1).broadcast_to([P, NT, D]), ALU.add)\
            .then_inc(s["tokb_ok"], 1)

        def maxima(g, q):
            if not (isinstance(g, int) and g < 2):
                pool.wait_ge(s["dd_ps"], GT * (g - 1))
            pool.wait_ge(s["mrow_ok"], g + 1)
            pool.tensor_tensor(rh[q][0:GR, :, :, :].rearrange("r j h s -> r (j h) s"),
                               spread(nhot[:, :], [GR, GR, S]),
                               amax[:, :].unsqueeze(1).broadcast_to([GR, GR, S]), ALU.mult).then_inc(s["rh_ok"], 1)

        def weighted(g):
            pool.wait_ge(s["h_ok"], g + 1)
            pool.tensor_tensor(hlw[:, :, :].rearrange("p (k h) d -> p k (h d)", k=GT),
                               hst[:, :, :].rearrange("p (k h) d -> p k (h d)", k=GT),
                               lnw[:, :].unsqueeze(1).broadcast_to([P, GT, D]), ALU.mult).then_inc(s["hlw_ok"], 1)
        maxima(0, 0)
        maxima(1, 1)
        weighted(0)
        with pool.Fori(0, (NG - 2) // 2) as i:
            for n in range(2):
                maxima(2 * i + 2 + n, n)
                weighted(2 * i + 1 + n)
        weighted(NG - 1)
        pool.wait_ge(s["st_out"], 16 * (SLOT_TILES // DUMP))
        with pool.Fori(0, NT // 2) as i:
            for n in range(4):
                pause(pool, s["stage_ok"], 4 * i + n + 1, s["passed_pool"])
                pool.indirect_dma_start(slots, bass.IndirectOffsetOnAxis(ap=idx[n][:, 0:1], axis=0),
                                        stg[n][:, :], None).then_inc(scat[n], 16)
        with pool.Fori(0, SLOT_TILES // NX) as i:
            for n in range(NX):
                pause(pool, s["y_ok"], NX * i + n + 1, s["passed_pool"])
                pool.indirect_dma_start(routed, bass.IndirectOffsetOnAxis(ap=xr[n][:, :].bitcast(I32)[:, DEST:DEST + 1], axis=0),
                                        yr[n % 4][:, :], None).then_inc(sc_y[n % 4], 16)

        def presum(g, n, i, first):
            pool.wait_ge(ld_y0[n], 16 * (i + 1))
            if not first:
                pool.wait_ge(s["stat_ok"], NT + g - 1)
            pool.tensor_tensor(sumf[n], y0[:, n], tok[:, g4(g * GT), :], ALU.add).then_inc(s["presum_ok"], 1)
        for n in range(2):
            presum(n, n, 0, True)
        with pool.Fori(1, NG // 2) as i:
            for n in range(2):
                presum(2 * i + n, n, i, False)

    @block.scalar
    def _(act):
        for n, (dst, src) in enumerate(((wv[:, :], w_v), (wo[:, :], w_out),
                                        (bout[:, :], bass.AP(tensor=b_out.tensor, offset=0, ap=[[0, P], [1, D]])),
                                        (bi[:, :], bass.AP(tensor=b_ig.tensor, offset=0, ap=[[0, 2 * GT], [1, NH], [1, 1]])),
                                        (bf[:, :], bass.AP(tensor=b_fg.tensor, offset=0, ap=[[0, 2 * GT], [1, NH], [1, 1]])),
                                        (rw[:, :], router_w),
                                        (lnw[:, :], bass.AP(tensor=ln_w.tensor, offset=0, ap=[[0, P], [1, D]])))):
            act.dma_start(dst, src).then_inc(s["ld_small"], 16)
        def x_evac(g):
            act.wait_ge(s["xT_ps"], g + 1)
            act.activation(xT[:, :], bank[7][:, :], ACT.Copy).then_inc(s["xT_ok"], 1)

        def z_evac(g, h):
            act.wait_ge(s["z_ps"], H * g + h + 1)
            act.activation(z[:, h, :], bank[4 + h % 2][:, :], ACT.Copy).then_inc(s["z_ok"], 1)

        def exps(g, k):
            act.wait_ge(s["logit_ok"], GT * g + k + 1)
            act.activation(prob[:, k, :], prob[:, k, :], ACT.Exp).then_inc(s["exp_ok"], 1)

        def pT_evac(g, k):
            act.wait_ge(s["pT_ps"], GT * g + k + 1)
            act.activation(probT[:, :], bank[6][:, :], ACT.Copy).then_inc(s["pT_ok"], 1)

        def oT_evac(g, k):
            act.wait_ge(s["oT_ps"], GT * g + k + 1)
            act.activation(oT[:, :], bank[k][:, 136:136 + P], ACT.Copy).then_inc(s["oT_ok"], 1)

        def rsqrt(mv_sem, need, src, ln_out, ln_sem, r_out, r_sem, count, scale=1.0):
            act.wait_ge(mv_sem, need)
            act.activation(ln_out, src, ACT.Ln, bias=eps[:, 0:1], scale=scale).then_inc(ln_sem, 1)
            act.wait_ge(ln_sem, count)
            act.activation(r_out, ln_out, ACT.Exp, scale=-0.5).then_inc(r_sem, 1)

        def group_a(g, more):
            exps(g, 0)
            for half in range(2):
                act.wait_ge(s["v_ps"], g + 1)
                r = slice(half * S, half * S + S)
                act.activation(vblk[r, :, half, 0:DV], bank[7][r, :].rearrange("p (n d) -> p n d", d=DV),
                               ACT.Copy).then_inc(s["v_ok"], 1)
            if more:
                x_evac(g + 1)
            act.wait_ge(s["s_ps"], GT * g + GT)
            for k in range(GT):
                pT_evac(g, k)
                if k:
                    oT_evac(g, k - 1)
                if more:
                    z_evac(g + 1, 2 * k)
                if k + 1 < GT:
                    exps(g, k + 1)
                if more:
                    z_evac(g + 1, 2 * k + 1)
            oT_evac(g, GT - 1)
            rsqrt(s["mv_ok"], GT * g + GT, mv[:, :, 1], lnv[:, :], s["lnv_ok"], rstd[:, :], s["rstd_ok"], g + 1)

        act.preload_act_table_set("natural_log_exp_and_others")
        act.wait_ge(s["wqkT_ps"], 1)
        act.activation(wqkT[:, 0:4, :], bank[0][:, :].rearrange("p (a b) -> p a b", a=4), ACT.Copy).then_inc(s["wqkT_ok"], 1)
        act.activation(wqkT[:, 4:8, :], bank[1][:, :].rearrange("p (a b) -> p a b", a=4), ACT.Copy).then_inc(s["wqkT_ok"], 1)
        act.wait_ge(s["pw_ps"], 1)
        for a in range(2):
            act.activation(pairw[:, a:H:2, :], bank[2 + a][:, :].rearrange("p (a b) -> p a b", a=4),
                           ACT.Copy, scale=DQ ** -0.5).then_inc(s["pw_ok"], 1)
        x_evac(0)
        for h in range(H):
            z_evac(0, h)
        act.wait_ge(s["const_v"], 1)
        with act.Fori(0, NG - 1) as g:
            group_a(g, True)
        group_a(NG - 1, False)

        def x2_evac(g):
            act.wait_ge(s["x2T_ps"], g + 1)
            act.activation(xT[:, :], bank[0][:, :], ACT.Copy).then_inc(s["x2Ts_ok"], 1)
            act.activation(x2T[:, bass.ds(g * W, W)], bank[0][:, :], ACT.Copy).then_inc(s["x2e_ok"], 1)

        def front_turn(g, q):
            act.wait_ge(s["x1T_ps"], g + 1)
            act.activation(x1T[:, :], bank[0][:, :], ACT.Copy).then_inc(s["x1T_ok"], 1)
            act.wait_ge(s["cT_ps"], g + 1)
            act.activation(cT[q][:, :], bank[1][:, :], ACT.Copy).then_inc(s["cT_ok"], 1)
            for h in range(NH):
                r = slice(h * DH, (h + 1) * DH)
                act.activation(qblk[q][r, :, h, :], bank[0][r, :].rearrange("p (n s) -> p n s", s=S),
                               ACT.Copy).then_inc(s["qblk_ok"], 1)

        def front_gates(g):
            act.wait_ge(s["g_ps"], g + 1)
            act.activation(fpre[:, :], bank[2][0:GR, 0:S], ACT.Identity, bias=bf[:, 0:1]).then_inc(s["fpre_ok"], 1)
            act.activation(ipre[:, :], bank[2][GR:2 * GR, 0:S], ACT.Identity, bias=bi[:, 0:1])
            act.wait_ge(s["fpre_ok"], g + 1)
            act.activation(flog[:, :], fpre[:, :], ACT.Abs).then_inc(s["fabs_ok"], 1)
            act.wait_ge(s["fabs_ok"], g + 1)
            act.activation(flog[:, :], flog[:, :], ACT.Exp, scale=-1.0).then_inc(s["fexp_ok"], 1)
            act.wait_ge(s["fexp_ok"], g + 1)
            act.activation(flog[:, :], flog[:, :], ACT.Ln, bias=1.0).then_inc(s["flog_ok"], 1)

        def front_floor(g, q):
            act.wait_ge(s["fl_ps"], g + 1)
            for a in range(2):
                r = slice(a * S, (a + 1) * S)
                act.activation(floor[q][r, :, :], bank[7][r, 0:GR].rearrange("p (k a h) -> p a k h", a=2, h=NH)[:, a],
                               ACT.Copy).then_inc(s["floor_ok"], 1)

        def front_emx(g):
            act.wait_ge(s["mrow_ok"], g + 1)
            act.activation(emx[:, :], mrow[:, :], ACT.Exp, scale=-1.0).then_inc(s["emx_ok"], 1)

        def decays(g, k):
            act.wait_ge(s["dd_ps"], GT * g + k + 1)
            act.activation(decay[:, k % 2, :], bank[3 + k % 2][:, 256:512], ACT.Exp).then_inc(s["decay_ok"], 1)

        def group_b(g, q, before, after):
            if before:
                x2_evac(g - 1)
            if after:
                front_turn(g + 1, 1 - q)
            decays(g, 0)
            decays(g, 1)
            if after:
                front_gates(g + 1)
            decays(g, 2)
            decays(g, 3)
            if after:
                front_emx(g + 1)
                front_floor(g + 1, 1 - q)
            act.wait_ge(s["h_ok"], g + 1)
            act.activation(hsq[:, :, :], hst[:, :, :], ACT.Square).then_inc(s["hsq_ok"], 1)
            rsqrt(s["hva_ok"], g + 1, hva[:, :], hln[:, :], s["hln_ok"], hrs[:, :], s["hrs_ok"], g + 1, scale=1.0 / DH)
            rsqrt(s["mv1_ok"], GT * g + GT, mv[:, :, 1], lnv[:, :], s["lnv1_ok"], rstd[:, :], s["rstd1_ok"], g + 1)
        front_turn(0, 0)
        front_gates(0)
        front_emx(0)
        front_floor(0, 0)
        group_b(0, 0, False, True)
        with act.Fori(0, (NG - 2) // 2) as i:
            for n in range(2):
                group_b(2 * i + 1 + n, 1 - n, True, True)
        group_b(NG - 1, 1, True, False)
        x2_evac(NG - 1)
        act.wait_ge(s["lmax_ok"], 1)
        act.activation(lg[:, :, :], lg[:, :, :], ACT.Exp).then_inc(s["lexp_ok"], 1)
        with act.Fori(0, NG // 2) as i:
            for a in range(2):
                g = 2 * i + a
                for c in range(FC):
                    act.wait_ge(s["shu_ps"], FC * g + c + 1)
                    act.activation(shT[:, a, c, :], bank[c % 2][:, :], ACT.Gelu).then_inc(s["sh_ok"], 1)
        def gelu(t, n):
            act.wait_ge(s["up_ps"], t + 1)
            act.activation(hh[:, n % 2, :], bank[2 + n % 2][:, :], ACT.Gelu).then_inc(s["hh_ok"], 1)
        with act.Fori(0, SLOT_TILES // 2) as i:
            for n in range(2):
                gelu(2 * i + n, n)
        act.preload_act_table_set("natural_log_exp_and_others")
        def last_a(g, n, i, first):
            act.wait_ge(s["mv2_ok"], GT * g + GT)
            act.activation(lnv[:, :], mvf[n][:, :, 1], ACT.Ln, bias=eps[:, 0:1]).then_inc(s["lnv2_ok"], 1)
            act.wait_ge(s["lnv2_ok"], g + 1)
            act.activation(rstdf[n][:, :], lnv[:, :], ACT.Exp, scale=-0.5).then_inc(s["rstd2_ok"], 1)
            if not first:
                act.wait_ge(st_o[n], 16 * i)
            act.wait_ge(s["shift_ok"], g + 1)
            for k in range(GT):
                m = act.activation(fin[:, n, k, :], resf[n][:, k, :], ACT.Identity, scale=rstdf[n][:, k:k + 1],
                                   bias=shift[n][:, k:k + 1])
            m.then_inc(s["fin_ok"], 1)
            act.wait_ge(s["fin_ok"], g + 1)
            act.dma_start(out_tok[:, g4(g * GT), :], fin[:, n]).then_inc(st_o[n], 16)
        for n in range(2):
            last_a(n, n, 0, True)
        with act.Fori(1, NG // 2) as i:
            for n in range(2):
                last_a(2 * i + n, n, i, False)
        for n in range(2):
            act.wait_ge(st_o[n], 16 * NG // 2)

    @block.tensor
    def _(pe):
        mm = pe.matmul
        pe.wait_ge(s["const_p"], 3)
        pe.wait_ge(s["ld_wqk"], 16)
        for c in range(H):
            m = pe.transpose(bank[c // 4][:, (c % 4) * P:(c % 4 + 1) * P], wqk[:, c * P:(c + 1) * P], ident[:, :])
        m.then_inc(s["wqkT_ps"], 1)
        pe.wait_ge(s["ld_gw"], 32)
        for c in range(3):
            m = pe.transpose(bank[6][:, 8 * c:8 * c + 8], gw[:, c * D:(c + 1) * D], ident[0:8, 0:8])
        m.then_inc(s["gwT_ps"], 1)

        def x_turn(g):
            pe.wait_ge(s["xs_ok"], 16 * (g + 1))
            for k in range(GT):
                m = pe.transpose(bank[7][:, k * P:(k + 1) * P], xs[:, k, :], ident[:, :])
            m.then_inc(s["xT_ps"], 1)
        x_turn(0)
        pe.wait_ge(s["wqkT_ok"], 2)
        for a in range(2):
            for j in range(4):
                r = slice(a * DQ, (a + 1) * DQ)
                m = mm(bank[2 + a][:, j * P:(j + 1) * P], wqkT[r, 4 + j, :], wqkT[r, j, :], start=True, stop=True)
        m.then_inc(s["pw_ps"], 1)
        pe.wait_ge(s["pw_ok"], 2)
        pe.wait_ge(s["xT_ok"], 1)

        def z_mm(g, h, early=False):
            if not (early and h < 2):
                pe.wait_ge(s["z_ok"], H * g + h - 1)
            mm(bank[4 + h % 2][:, :], pairw[:, h, :], xT[:, :], start=True, stop=True).then_inc(s["z_ps"], 1)
        for h in range(H):
            z_mm(0, h, True)
        pe.wait_ge(s["ld_small"], 16 * 7)
        pe.wait_ge(s["const_v"], 1)

        def proj(g, k):
            pe.wait_ge(s["oT_ok"], GT * g + k + 1)
            mm(bank[k][:, 264:264 + D], oT[:, :], wo[:, :], start=True, stop=True).then_inc(s["pr_ps"], 1)

        def out_turn(g, k):
            pe.wait_ge(s["o_ok"], GT * g + k + 1)
            pe.transpose(bank[k][:, 136:136 + P], o[:, :], ident[:, :]).then_inc(s["oT_ps"], 1)

        def group_a(g, more):
            pe.wait_ge(s["z_ok"], H * g + H)
            for k in range(GT):
                pe.wait_ge(s["res_ok"], GT * g + k + 1)
                for a in range(2):
                    q = slice(k * P + a * S, k * P + a * S + S)
                    m = mm(bank[k][a * S:(a + 1) * S, :], xT[:, q], z[:, :, q], start=True, stop=True)
                m.then_inc(s["s_ps"], 1)
            for k in range(GT):
                for a in range(2):
                    for half in range(2):
                        m = mm(bank[7][half * S:(half + 1) * S, k * P + a * 64:k * P + a * 64 + 64],
                               xT[:, k * P + a * S:k * P + a * S + S],
                               wv[:, :].rearrange("p (j e d) -> p e j d", e=2, d=DV)[:, half],
                               start=True, stop=True)
            m.then_inc(s["v_ps"], 1)
            if more:
                pe.wait_ge(s["v_ok"], 2 * g + 2)
                x_turn(g + 1)
            for k in range(GT):
                pe.wait_ge(s["exp_ok"], GT * g + k + 1)
                pe.wait_ge(s["pT_ok"], GT * g + k + 1)
                for j in range(4):
                    m = pe.transpose(bank[6][:, j * P:(j + 1) * P], prob[:, k, j * P:(j + 1) * P], ident[:, :])
                m.then_inc(s["pT_ps"], 1)
                if k:
                    out_turn(g, k - 1)
                if more:
                    if k == 0:
                        pe.wait_ge(s["xT_ok"], g + 2)
                    z_mm(g + 1, 2 * k)
                pe.wait_ge(s["pT_ok"], GT * g + k + 2)
                if k == 0:
                    pe.wait_ge(s["v_ok"], 2 * g + 2)
                for j in range(4):
                    for a in range(2):
                        m = mm(bank[k][a * S:(a + 1) * S, j * 34:j * 34 + 34],
                               probT[:, j * P + a * S:j * P + a * S + S],
                               vblk[:, k * 8 + a * 4 + j, :, :], start=True, stop=True)
                m.then_inc(s["av_ps"], 1)
                if k:
                    proj(g, k - 1)
                if more:
                    z_mm(g + 1, 2 * k + 1)
            out_turn(g, GT - 1)
            proj(g, GT - 1)
        with pe.Fori(0, NG - 1) as g:
            group_a(g, True)
        group_a(NG - 1, False)
        pe.wait_ge(s["res_ok"], NT + GT)

        def front_turn(g, first=False):
            pe.wait_ge(s["xs1_ok"], 16 * (g + 1))
            if not first:
                pe.wait_ge(s["qblk_ok"], NH * g)
                pe.wait_ge(s["cT_ok"], g)
            for k in range(GT):
                m = pe.transpose(bank[0][:, k * P:(k + 1) * P], xs[:, k, :], ident[:, :])
            m.then_inc(s["x1T_ps"], 1)
            pe.wait_ge(s["cs_ok"], 16 * (g + 1))
            for k in range(GT):
                m = pe.transpose(bank[1][:, k * P:(k + 1) * P], cs[:, k, :], ident[:, :])
            m.then_inc(s["cT_ps"], 1)

        def front_gates(g, q):
            pe.wait_ge(s["x1T_ok"], g + 1)
            pe.wait_ge(s["cT_ok"], g + 1)
            for j in range(2 * GT):
                for n, src in enumerate((x1T, cT[q])):
                    m = mm(bank[2][0:2 * GR, 0:S], wg[n][:, j, :], src[:, j * S:(j + 1) * S],
                           start=(j == 0 and n == 0), stop=(j == 2 * GT - 1 and n == 1))
            m.then_inc(s["g_ps"], 1)

        def front_floor(g):
            pause(pe, s["emx_ok"], g + 1, s["passed_pe"])
            for a in range(2):
                m = mm(bank[7][a * S:(a + 1) * S, 0:GR], emx[:, :], ident[0:GR, 0:GR], start=True, stop=True)
            m.then_inc(s["fl_ps"], 1)

        def qk(g, q, k, first):
            t = GT * g + k
            if not (first and k < 2):
                pe.wait_ge(s["c_ok"], t - 1)
            if k == 0:
                pe.wait_ge(s["qblk_ok"], NH * g + NH)
                pe.wait_ge(s["al_ok"], g + 1)
                pe.wait_ge(s["rh_ok"], g + 1)
            bk = bank[3 + k % 2]
            for a in range(2):
                mm(bk[a * S:(a + 1) * S, 0:256], cT[q][:, k * P + a * S:k * P + a * S + S],
                   qblk[q][:, 2 * k + a, :, :], start=True, stop=True)
            for a in range(2):
                mm(bk[a * S:(a + 1) * S, 256:512], al[q][:, :], rh[q][:, 2 * k + a, :, :],
                   start=True, stop=False, skip_group_check=True)
            mm(bk[:, 256:512], identb[:, :], causal[:, :], start=False, stop=True,
               skip_group_check=True).then_inc(s["dd_ps"], 1)

        def av(g, q, k, first):
            pe.wait_ge(s["c_ok"], GT * g + k + 1)
            if k == 0:
                pe.wait_ge(s["vmask_ok"], 16 * 2 * GT * (g + 1))
                if not first:
                    pe.wait_ge(s["h_ok"], g)
            for h in range(NH):
                for a in range(2):
                    c = (k % 2) * 132 + h * 33
                    m = mm(bank[5 + k // 2][a * S:(a + 1) * S, c:c + 33],
                           cmat[:, k % 2, h * S:(h + 1) * S],
                           vmask[q][:, k, a, h, :], start=True, stop=True)
            m.then_inc(s["u_ps"], 1)

        def x2_turn(g):
            pe.wait_ge(s["qblk_ok"], NH * min(g + 2, NG) if isinstance(g, int) else NH * (g + 2))
            pe.wait_ge(s["x2_ok"], GT * g + GT)
            for k in range(GT):
                m = pe.transpose(bank[0][:, k * P:(k + 1) * P], x2s[:, k, :], ident[:, :])
            m.then_inc(s["x2T_ps"], 1)

        def router(g, first=False):
            pe.wait_ge(s["x2Ts_ok"], g + 1)
            if not first:
                pe.wait_ge(s["lg_ok"], g)
            for k in range(GT):
                m = mm(bank[1][:, k * E:(k + 1) * E], xT[:, k * P:(k + 1) * P], rw[:, :], start=True, stop=True)
            m.then_inc(s["lg_ps"], 1)

        def group_b(g, q, before, after, first=False, early=False):
            if before:
                x2_turn(g - 1)
            if after:
                if before:
                    pe.wait_ge(s["x2e_ok"], g)
                    if not early:
                        pe.wait_ge(s["lg_ok"], g - 1)
                front_turn(g + 1)
                front_gates(g + 1, 1 - q)
            if before:
                router(g - 1, early)
            qk(g, q, 0, first)
            for k in range(1, GT):
                qk(g, q, k, first)
                av(g, q, k - 1, first)
            av(g, q, GT - 1, first)
            if after:
                front_floor(g + 1)
        pe.wait_ge(s["const_p"], N_CONST)
        pe.wait_ge(s["gw_ok"], 1)
        front_turn(0, True)
        front_gates(0, 0)
        front_floor(0)
        group_b(0, 0, False, True, True)
        group_b(1, 1, True, True, False, True)
        with pe.Fori(0, (NG - 4) // 2) as i:
            for n in range(2):
                group_b(2 * i + 2 + n, n, True, True)
        group_b(NG - 2, 0, True, True)
        group_b(NG - 1, 1, True, False)
        x2_turn(NG - 1)
        router(NG - 1)
        pe.wait_ge(s["lg_ok"], NG)
        pe.wait_ge(s["x2e_ok"], NG)
        def ranks():
            pe.wait_ge(s["hotb_ok"], 1)
            hb = hotb[:, :, :].rearrange("p t e -> p (t e)")
            mm(bank[6][:, 0:256], trib[:, :], hb, start=True, stop=True)
            mm(bank[6][:, 256:512], onesb[:, :], hb, start=True, stop=True).then_inc(s["rank_ps"], 1)
        pe.wait_ge(s["ld_sh"], 32)

        def sh_up_mm(g, first=False):
            for c in range(FC):
                if not (first and c < 2):
                    pe.wait_ge(s["sh_ok"], FC * g + c - 1)
                mm(bank[c % 2][:, :], sup[:, c * P:(c + 1) * P], x2T[:, bass.ds(g * W, W)],
                   start=True, stop=True).then_inc(s["shu_ps"], 1)

        def sh_down_mm(g, a, first=False):
            pe.wait_ge(s["sh_ok"], FC * g + FC)
            if not first:
                pe.wait_ge(s["base_ok"], g)
            for k in range(GT):
                for c in range(FC):
                    m = mm(bank[4 + a][:, k * D:(k + 1) * D], shT[:, a, c, k * P:(k + 1) * P], sdn[:, c, :],
                           start=(c == 0), stop=(c == FC - 1))
            m.then_inc(s["shd_ps"], 1)
        sh_up_mm(0, True)
        ranks()
        sh_up_mm(1)
        sh_down_mm(0, 0, True)
        with pe.Fori(1, NG // 2) as i:
            sh_up_mm(2 * i)
            sh_down_mm(2 * i - 1, 1)
            sh_up_mm(2 * i + 1)
            sh_down_mm(2 * i, 0)
        sh_down_mm(NG - 1, 1)
        pe.wait_ge(s["base_ok"], NG + 1)
        pe.wait_ge(s["texp_ok"], 1)
        pe.wait_ge(s["ld_wup"], 16)
        pe.wait_ge(s["ld_wdn"], 16)
        pe.wait_ge(s["rsteps"], 1)

        def expert(t):
            return pe.value_load(texpi[0:1, bass.ds(t, 1)], min_val=0, max_val=E - 1)

        def turn(t, n, i):
            pe.wait_ge(ld_xr[n % NX], 16 * (i + 1))
            if not (isinstance(t, int) and t < 2):
                pe.wait_ge(s["xrT_ok"], t - 1)
            pe.transpose(bank[n % 2][:, 0:P], xr[n % NX][:, 0:D], ident[:, :]).then_inc(s["xr_ps"], 1)

        def up(t, n):
            e = expert(t)
            pe.wait_ge(s["xrT_ok"], t + 1)
            if not (isinstance(t, int) and t < 2):
                pe.wait_ge(s["hh_ok"], t - 1)
            mm(bank[2 + n % 2][:, :], xrT[:, n % 2, :], wup[:, bass.ds(e * FF, FF)],
               start=True, stop=True).then_inc(s["up_ps"], 1)

        def turn_h(t, n):
            pe.wait_ge(s["hh_ok"], t + 1)
            if not (isinstance(t, int) and t < 2):
                pe.wait_ge(s["hT_ok"], t - 1)
            for c in range(FC):
                m = pe.transpose(bank[4 + n % 2][:, c * P:(c + 1) * P], hh[:, n % 2, c * P:(c + 1) * P], ident[:, :])
            m.then_inc(s["hT_ps"], 1)

        def down(t, n):
            e = expert(t)
            pe.wait_ge(s["hT_ok"], t + 1)
            if not (isinstance(t, int) and t < 2):
                pe.wait_ge(s["y_ok"], t - 1)
            for c in range(FC):
                m = mm(bank[6 + n % 2][:, 0:D], hT[:, n % 2, c * P:(c + 1) * P],
                       wdn[:, bass.ds(e * (FC * D) + c * D, D)], start=(c == 0), stop=(c == FC - 1))
            m.then_inc(s["y_ps"], 1)

        def step(t, n, i, lo=True, hi=True):
            if hi:
                turn(t, n, i)
            if (not isinstance(t, int)) or (t >= 1 and t - 1 < SLOT_TILES):
                up(t - 1, n - 1)
            if (not isinstance(t, int)) or (t >= 2 and t - 2 < SLOT_TILES):
                turn_h(t - 2, n - 2)
            if (not isinstance(t, int)) or (t >= 3 and t - 3 < SLOT_TILES):
                down(t - 3, n - 3)
        for t in range(NX):
            step(t, t, 0)
        with pe.Fori(1, SLOT_TILES // NX) as i:
            for n in range(NX):
                step(i * NX + n, n, i)
        for t in range(SLOT_TILES, SLOT_TILES + 3):
            step(t, t, 0, hi=False)

    @block.vector
    def _(dve):
        tt, tsc, stt = dve.tensor_tensor, dve.tensor_scalar, dve.scalar_tensor_tensor
        dve.sem_inc(s["res_ok"], GT)
        dve.sem_inc(s["pT_ok"], 1)
        dve.sem_inc(s["base_ok"], 1)
        st = Steps(dve, s["vsteps"])
        dve.wait_ge(s["ld_conv"], 16)
        lo = S - 1 - MAXPOS
        nn = 2 * MAXPOS + 1
        dve.tensor_copy(cpad[:, lo:lo + nn], cin[:, :]).then_inc(s["cpad_ok"], 1)
        dve.tensor_copy(cpad[:, 0:lo], cin[:, 0:1].broadcast_to([H, lo])).then_inc(s["cpad_ok"], 1)
        dve.tensor_copy(cpad[:, lo + nn:P], cin[:, nn - 1:nn].broadcast_to([H, P - lo - nn])).then_inc(s["cpad_ok"], 1)
        st(dve.memset(eps[:, :], LN_EPS))
        st(dve.memset(onesb[:, :], 1.0))
        st(dve.memset(one8[:, :], 1.0))
        st(dve.memset(vblk[:, :, :, :], 0.0))
        st(dve.memset(vblk[0:S, :, 0, DV:DV + 1], 1.0))
        st(dve.memset(vblk[S:P, :, 1, DV:DV + 1], 1.0))
        for q in range(2):
            st(dve.memset(qblk[q][:, :, :, :], 0.0))
            st(dve.memset(vmask[q][:, :, :, :, :], 0.0))
            st(dve.memset(vmask[q][0:S, :, 0, :, DH:DH + 1], 1.0))
            st(dve.memset(vmask[q][S:P, :, 1, :, DH:DH + 1], 1.0))
            st(dve.memset(al[q][0:GR, :], 1.0))
        st(dve.memset(one_s[:, :], 1.0))
        st(dve.memset(zero_s[:, :], 0.0))
        st(dve.memset(segm[:, :, :], 1.0))
        st(dve.memset(segm[:, :, 0], 0.0))
        for n in range(4):
            st(dve.memset(stg[n][:, :], 0.0))
        for n in range(2):
            st(dve.memset(wg[n][:, :, :], 0.0))
        dve.wait_ge(s["ld_small"], 16 * 7)
        dve.sem_inc(s["const_v"], 1)
        st(tsc(lnw[:, :], lnw[:, :], 1.0, None, ALU.add))
        dve.wait_ge(s["gwT_ps"], 1)
        st(dve.tensor_copy(gwT[:, :, :], bank[6][:, 0:24].rearrange("p (a b) -> p a b", a=3)))
        st(tt(gwT[:, 1, :], gwT[:, 1, :], gwT[:, 2, :], ALU.add))
        for n in range(2):
            for rows, cols in ((0, NH), (GR, 0)):
                w0 = wg[n][:, 0, rows:rows + NH]
                dst = bass.AP(tensor=w0.tensor, offset=w0.offset, ap=[list(w0.ap[0]), [2 * GR + NH, 2 * GT], [1, NH]])
                st(dve.tensor_copy(dst, gwT[:, n, cols:cols + NH].unsqueeze(1).broadcast_to([P, 2 * GT, NH])))
        dve.sem_inc(s["gw_ok"], 1)
        dve.wait_ge(s["ld_bias"], 32)
        dve.wait_ge(s["tokb_ok"], 1)

        def layernorm(g, mv_sem, rstd_sem, src, dst, done):
            dve.wait_ge(rstd_sem, g + 1)
            for k in range(GT):
                tsc(dst[:, k, :], src[:, k, :], mv[:, k, 0:1], rstd[:, k:k + 1],
                    ALU.subtract, ALU.mult).then_inc(done, 1)

        def scores(g, k, st):
            dve.wait_ge(s["s_ps"], GT * g + k + 1)
            p3 = prob[:, k, :].rearrange("p (h j) -> p h j", h=H)
            st(tt(prob[:, k, :], bank[k][:, :], bias[:, :, :].rearrange("p h j -> p (h j)"), ALU.add))
            st(dve.tensor_reduce(negmax[:, k, :], p3, AX.X, ALU.max))
            tt(p3, p3, spread(negmax[:, k, :], [P, H, S]), ALU.subtract).then_inc(s["logit_ok"], 1)

        def head_out(g, k, st):
            dve.wait_ge(s["av_ps"], GT * g + k + 1)
            u = bank[k][:, 0:136].rearrange("p (h d) -> p h d", h=H)
            st(dve.reciprocal(rden[:, k, :], u[:, :, DV]))
            tt(o[:, :].rearrange("p (h d) -> p h d", h=H), u[:, :, 0:DV],
               spread(rden[:, k, :], [P, H, DV]), ALU.mult).then_inc(s["o_ok"], 1)

        def residual(g, k):
            dve.wait_ge(s["pr_ps"], GT * g + k + 1)
            tt(res[:, k, :], bank[k][:, 264:264 + D], tok[:, g * GT + k, :], ALU.add).then_inc(s["res_ok"], 1)
            dve.wait_ge(s["res_ok"], GT * g + k + 1 + GT)
            dve.bn_stats(stats[:, k, :], res[:, k, :]).then_inc(s["stat_ok"], 1)
            pause(dve, s["stat_ok"], GT * g + k + 1, s["passed_dve"])
            dve.bn_aggr(mv[:, k, :], stats[:, k, :]).then_inc(s["mv_ok"], 1)

        ast = Steps(dve, s["asteps"])
        A_STEPS = 3 * GT
        def x1_out(g):
            layernorm(g, s["mv_ok"], s["rstd_ok"], res, tok[:, g4(g * GT), :], s["x1_ok"])

        def group_a(g, first):
            ast.start(g * A_STEPS)
            scores(g, 0, ast)
            scores(g, 1, ast)
            if not first:
                x1_out(g - 1)
                dve.wait_ge(s["x1_ok"], GT * g)
            scores(g, 2, ast)
            head_out(g, 0, ast)
            scores(g, 3, ast)
            for k in range(1, GT):
                head_out(g, k, ast)
                residual(g, k - 1)
            residual(g, GT - 1)
            assert ast.n == A_STEPS
        group_a(0, True)
        with dve.Fori(1, NG) as g:
            group_a(g, False)
        x1_out(NG - 1)
        dve.wait_ge(s["x1_ok"], NT)

        dve.wait_ge(s["const_p"], N_CONST)
        ist = Steps(dve, s["igsteps"])
        bst = Steps(dve, s["bsteps"])
        I_STEPS, B_STEPS = 4, 12

        def front(g, q):
            ist.start(g * I_STEPS)
            dve.wait_ge(s["flog_ok"], g + 1)
            ist(stt(logf[:, :], fpre[:, :], 0.0, flog[:, :], ALU.min, ALU.subtract))
            ist(dve.tensor_tensor_scan(cumf[:, :], one_s[:, :], logf[:, :], 0.0, ALU.mult, ALU.add))
            ist(tt(arow[:, :], ipre[:, :], cumf[:, :], ALU.subtract))
            if not (isinstance(g, int) and g < 2):
                dve.wait_ge(s["dd_ps"], GT * (g - 1))
            dve.tensor_copy(al[q][GR:2 * GR, :], arow[:, :]).then_inc(s["al_ok"], 1)
            if not (isinstance(g, int) and g < 1):
                dve.wait_ge(s["rh_ok"], g)
            ist(dve.tensor_tensor_scan(amax[:, :], zero_s[:, :], arow[:, :], -BIG, ALU.add, ALU.max))
            tt(mrow[:, :], cumf[:, :], amax[:, :], ALU.add).then_inc(s["mrow_ok"], 1)
            assert ist.n == I_STEPS

        def score(g, k):
            dve.wait_ge(s["decay_ok"], GT * g + k + 1)
            stt(cmat[:, k % 2, :], bank[3 + k % 2][:, 0:256], DH ** -0.5, decay[:, k % 2, :],
                ALU.mult, ALU.mult).then_inc(s["c_ok"], 1)

        def cell(g, q, j):
            dve.wait_ge(s["u_ps"], GT * g + 2 * j + 2)
            dve.wait_ge(s["floor_ok"], 2 * g + 2)
            u = bank[5 + j][:, 0:264].rearrange("p (n d) -> p n d", d=DH + 1)
            nv = nrm[:, 2 * j:2 * j + 2, :].rearrange("p k h -> p (k h)")
            bst(dve.tensor_reduce(nv, u[:, :, DH:DH + 1], AX.X, ALU.max, apply_absolute_value=True))
            bst(tt(nv, nv, floor[q][:, 2 * j:2 * j + 2, :].rearrange("p k h -> p (k h)"), ALU.max))
            bst(tsc(nv, nv, 1e-6, None, ALU.add))
            bst(dve.reciprocal(nv, nv))
            m = tt(hst[:, 8 * j:8 * j + 8, :], u[:, :, 0:DH], spread(nv, [P, 8, DH]), ALU.mult)
            if j == 1:
                bst(m)

        def logits_out(g):
            pause(dve, s["lg_ps"], g + 1, s["passed_dve"])
            dve.tensor_copy(lg[:, g4(g * GT), :], bank[1][:, 0:GT * E].rearrange("p (k e) -> p k e", k=GT)).then_inc(s["lg_ok"], 1)

        def group_b(g, q, before, after):
            bst.start(g * B_STEPS)
            if before:
                logits_out(g - 1)
            score(g, 0)
            score(g, 1)
            if after:
                front(g + 1, 1 - q)
            score(g, 2)
            cell(g, q, 0)
            score(g, 3)
            cell(g, q, 1)
            bst(dve.tensor_reduce(hmu[:, :], hst[:, :, :], AX.X, ALU.add))
            bst(tsc(hmu[:, :], hmu[:, :], 1.0 / DH, None, ALU.mult))
            tt(hst[:, :, :], hst[:, :, :], spread(hmu[:, :], [P, GT * NH, DH]), ALU.subtract).then_inc(s["h_ok"], 1)
            dve.wait_ge(s["hsq_ok"], g + 1)
            dve.tensor_reduce(hva[:, :], hsq[:, :, :], AX.X, ALU.add).then_inc(s["hva_ok"], 1)
            dve.wait_ge(s["hrs_ok"], g + 1)
            dve.wait_ge(s["hlw_ok"], g + 1)
            bst(tt(hst[:, :, :], hlw[:, :, :], spread(hrs[:, :], [P, GT * NH, DH]), ALU.mult))
            h3 = hst[:, :, :].rearrange("p (k h) d -> p k (h d)", k=GT)
            tt(res[:, :, :], h3, tok[:, g4(g * GT), :], ALU.add).then_inc(s["res1_ok"], 1)
            dve.wait_ge(s["res1_ok"], g + 1)
            for k in range(GT):
                m = dve.bn_stats(stats[:, k, :], res[:, k, :])
            pause_after(m, g)
            for k in range(GT):
                dve.bn_aggr(mv[:, k, :], stats[:, k, :]).then_inc(s["mv1_ok"], 1)
            assert bst.n == B_STEPS, bst.n
            if before:
                dve.wait_ge(s["x2T_ps"], g)
                dve.wait_ge(s["tk_ok"], 16 * g)
            layernorm(g, s["mv1_ok"], s["rstd1_ok"], res, x2s, s["x2_ok"])
            dve.wait_ge(s["x2_ok"], GT * g + GT)

        def pause_after(m, g):
            m.then_inc(s["lnd_ok"], 1)
            pause(dve, s["lnd_ok"], g + 1, s["passed_dve"])
        front(0, 0)
        group_b(0, 0, False, True)
        with dve.Fori(0, (NG - 2) // 2) as i:
            for n in range(2):
                group_b(2 * i + 1 + n, 1 - n, True, True)
        group_b(NG - 1, 1, True, False)
        logits_out(NG - 1)

        r = Steps(dve, s["rsteps"])
        dve.wait_ge(s["const_p"], N_TABLES)
        dve.wait_ge(s["lg_ok"], NG)
        full = [P, NT, E]
        r(dve.tensor_reduce(m8[:, :], lg[:, :, :], AX.X, ALU.max))
        tt(lg[:, :, :], lg[:, :, :], spread(m8[:, :], full), ALU.subtract).then_inc(s["lmax_ok"], 1)
        dve.wait_ge(s["lexp_ok"], 1)
        r(dve.tensor_reduce(m8[:, :], lg[:, :, :], AX.X, ALU.add))
        r(dve.reciprocal(m8[:, :], m8[:, :]))
        r(tt(lg[:, :, :], lg[:, :, :], spread(m8[:, :], full), ALU.mult))
        for k in range(2):
            r(dve.tensor_reduce(gate[k][:, :], lg[:, :, :], AX.X, ALU.max))
            r(tt(cand[:, :, :], lg[:, :, :], spread(gate[k][:, :], full), ALU.is_equal))
            r(tt(cand[:, :, :], cand[:, :, :], io_e[:, :].unsqueeze(1).broadcast_to(full), ALU.mult))
            r(dve.tensor_reduce(m8[:, :], cand[:, :, :], AX.X, ALU.max))
            r(tt(hot[k][:, :, :], cand[:, :, :], spread(m8[:, :], full), ALU.is_equal))
            if k == 0:
                r(stt(lg[:, :, :], hot[0][:, :, :], -2.0, lg[:, :, :], ALU.mult, ALU.add))
        tt(hotb[:, :, :], hot[0][:, :, :], hot[1][:, :, :], ALU.add).then_inc(s["hotb_ok"], 1)
        dve.wait_ge(s["rank_ps"], 1)
        r(dve.tensor_copy(tote[:, :, :], bank[6][:, 256:512].rearrange("p (t e) -> p e t", e=E)))
        fl = lambda a: a[:, :, :].rearrange("p e t -> p (e t)")
        r(dve.tensor_tensor_scan(fl(cume), fl(segm), fl(tote), 0.0, ALU.mult, ALU.add))
        r(tt(gt[:, :, :], spread(cume[:, :, NT - 1], [P, E, NT]), io_128[:, :].unsqueeze(1).broadcast_to([P, E, NT]), ALU.is_gt))
        r(dve.tensor_reduce(ntile[:, :], gt[:, :, :], AX.X, ALU.add))
        r(dve.tensor_tensor_scan(ctile[:, :], one8[:, :], ntile[:, :], 0.0, ALU.mult, ALU.add))
        r(tt(cume[:, :, :], cume[:, :, :], tote[:, :, :], ALU.subtract))
        r(tt(sl[:, :, :], bank[6][:, 0:256].rearrange("p (t e) -> p t e", e=E), cume[:, :, :].rearrange("p e t -> p t e"), ALU.add))
        r(tt(ntile[:, :], ctile[:, :], ntile[:, :], ALU.subtract))
        r(stt(sl[:, :, :], ntile[:, :].unsqueeze(1).broadcast_to(full), float(P), sl[:, :, :], ALU.mult, ALU.add))
        for k in range(2):
            r(tt(cand[:, :, :], sl[:, :, :], hot[k][:, :, :], ALU.mult))
            r(dve.tensor_reduce(slotf[:, :], cand[:, :, :], AX.X, ALU.add))
            r(dve.tensor_copy(slot[k][:, :], slotf[:, :]))
        r(tt(tcmp[:, :, :], ctile[0:1, :].unsqueeze(1).broadcast_to([1, SLOT_TILES, E]),
             spread(io_tau[:, :], [1, SLOT_TILES, E]), ALU.is_le))
        r(dve.tensor_reduce(texp[:, :], tcmp[:, :, :], AX.X, ALU.add))
        r(tsc(texp[:, :], texp[:, :], float(E - 1), None, ALU.min))
        dve.tensor_copy(texpi[:, :], texp[:, :]).then_inc(s["texp_ok"], 1)

        def stage(i, n, t, k, first):
            if not first:
                pause(dve, scat[n], 16 * i, s["passed_dve"])
            dve.tensor_copy(stg[n][:, 0:D], tok[:, t, :])
            dve.tensor_copy(stg[n][:, GATE:GATE + 1], gate[k][:, bass.ds(t, 1)])
            dve.tensor_copy(stg[n][:, :].bitcast(I32)[:, DEST:DEST + 1], dest[:, k, bass.ds(t, 1)])
            dve.tensor_copy(idx[n][:, :], slot[k][:, bass.ds(t, 1)]).then_inc(s["stage_ok"], 1)

        def two_groups(i, first):
            for a in range(2):
                g = 2 * i + a
                for n in range(2 * GT):
                    stage(2 * g + n // 4, n % 4, g * GT + n // 2, n % 2, first and a == 0 and n < 4)
                dve.wait_ge(s["shd_ps"], g + 1)
                dve.wait_ge(s["stage_ok"], 2 * GT * (g + 1))
                tg = tok[:, g4(g * GT), :]
                stt(tg, tg, 2.0, bank[4 + a][:, :].rearrange("p (k d) -> p k d", k=GT),
                    ALU.mult, ALU.add).then_inc(s["base_ok"], 1)
        dve.wait_ge(s["tk_ok"], 16 * NG)
        two_groups(0, True)
        with dve.Fori(1, NG // 2) as i:
            two_groups(i, False)

        def x_out(t, n):
            dve.wait_ge(s["xr_ps"], t + 1)
            dve.tensor_copy(xrT[:, n % 2, :], bank[n % 2][:, 0:P]).then_inc(s["xrT_ok"], 1)

        def h_out(t, n):
            dve.wait_ge(s["hT_ps"], t + 1)
            dve.tensor_copy(hT[:, n % 2, :], bank[4 + n % 2][:, :]).then_inc(s["hT_ok"], 1)

        def y_out(t, n, times):
            dve.wait_ge(s["y_ps"], t + 1)
            if not (isinstance(t, int) and t < 4):
                dve.wait_ge(sc_y[n % 4], 16 * times)
            tsc(yr[n % 4][:, :], bank[6 + n % 2][:, 0:D], xr[n % NX][:, GATE:GATE + 1], None,
                ALU.mult).then_inc(s["y_ok"], 1)

        def step(t, n, i):
            known = isinstance(t, int)
            if not known or t < SLOT_TILES:
                x_out(t, n)
            if not known or (t >= 2 and t - 2 < SLOT_TILES):
                h_out(t - 2, n - 2)
            if not known or (t >= 3 and t - 3 < SLOT_TILES):
                y_out(t - 3, n - 3, (t - 3) // 4 if known else 2 * i + (n - 3) // 4)
        for t in range(NX):
            step(t, t, 0)
        with dve.Fori(1, SLOT_TILES // NX) as i:
            for n in range(NX):
                step(i * NX + n, n, i)
        for t in range(SLOT_TILES, SLOT_TILES + 3):
            step(t, t, 0)

        def totals(g, n, i, first):
            dve.wait_ge(ld_y1[n], 16 * (i + 1))
            dve.wait_ge(s["presum_ok"], g + 1)
            if not first:
                dve.wait_ge(s["fin_ok"], g - 1)
            tt(resf[n], sumf[n], y1[:, n], ALU.add).then_inc(s["res1_ok"], 1)
            dve.wait_ge(s["res1_ok"], NG + g + 1)
            for k in range(GT):
                m = dve.bn_stats(stats[:, k, :], resf[n][:, k, :])
            m.then_inc(s["stat_ok"], 1)
            pause(dve, s["stat_ok"], NT + g + 1, s["passed_dve"])
            for k in range(GT):
                dve.bn_aggr(mvf[n][:, k, :], stats[:, k, :]).then_inc(s["mv2_ok"], 1)

        def shifts(g, n):
            dve.wait_ge(s["rstd2_ok"], g + 1)
            dve.wait_ge(s["mv2_ok"], GT * g + GT)
            stt(shift[n][:, :], mvf[n][:, :, 0], -1.0, rstdf[n][:, :], ALU.mult, ALU.mult).then_inc(s["shift_ok"], 1)
        totals(0, 0, 0, True)
        totals(1, 1, 0, True)
        shifts(0, 0)
        with dve.Fori(1, NG // 2) as i:
            totals(2 * i, 0, i, False)
            shifts(2 * i - 1, 1)
            totals(2 * i + 1, 1, i, False)
            shifts(2 * i, 0)
        shifts(NG - 1, 1)

    es.close()


_INS = ['x', 'ctx_1024', 'L0_attn_W_qk', 'L0_attn_W_v', 'L0_attn_W_out', 'L0_attn_b_out', 'L0_attn_conv',
        'L0_xattn_w_igate', 'L0_xattn_b_igate', 'L0_xattn_w_fgate', 'L0_xattn_b_fgate', 'L0_xattn_ln_weight',
        'L0_ffn_shared_up', 'L0_ffn_shared_down', 'L0_ffn_routed_up', 'L0_ffn_routed_down', 'L0_ffn_router_w']


def kernel(**inputs):
    import numpy as _np
    import concourse.bacc as _bacc
    from concourse import mybir as _mybir
    from concourse.bass_utils import run_bass_kernel_spmd as _run

    nc = _bacc.Bacc("TRN2", target_bir_lowering=False, num_devices=1)
    arrays, args = {}, []
    for name in _INS:
        a = _np.ascontiguousarray(inputs[name])
        arrays[f"in_{name}"] = a
        args.append(nc.dram_tensor(f"in_{name}", a.shape, _mybir.dt.from_np(a.dtype), kind="ExternalInput").ap())
    out = nc.dram_tensor("out_x", (64, 64, 128), _mybir.dt.float32, kind="ExternalOutput").ap()
    decoder_layer(nc, *args, out)
    r = _run(nc, [arrays], core_ids=[0])
    return r.results[0]["out_x"]
```

```python
import concourse.bass as bass
from concourse import mybir
from contextlib import ExitStack

F32 = mybir.dt.float32
F32R = mybir.dt.float32r
BF16 = mybir.dt.bfloat16
I32 = mybir.dt.int32
ALU = mybir.AluOpType
ACT = mybir.ActivationFunctionType
AX = mybir.AxisListType

P = 128
B, S, D = 64, 64, 128
NT = B * S // P
GT = 4
NG = NT // GT
W = GT * P
H, DQ = 8, 64
DV = D // H
MAXPOS = 10
NH, DH = 4, 32
FF, E = 512, 8
FC = FF // P
SLOT_TILES = 2 * NT + E
ROW = D + 4
GATE, DEST = D, D + 1
DUMP = 9
BIG = 1e30
LN_EPS = 1e-5
N_CONST, N_TABLES = 14, 18


class Steps:

    def __init__(self, eng, sem):
        self.eng, self.sem, self.base, self.n = eng, sem, 0, 0

    def __call__(self, ins):
        self.n += 1
        ins.then_inc(self.sem, 1)
        self.eng.wait_ge(self.sem, self.base + self.n)

    def start(self, base):
        self.base, self.n = base, 0


def pause(eng, sem, value, passed):
    eng.wait_ge(sem, value)
    eng.sem_inc(passed, 1)


def spread(ap, shape):
    return ap.unsqueeze(len(shape) - 1).broadcast_to(shape)


def decoder_layer(nc, x, ctx_in, w_qk, w_v, w_out, b_out, conv, w_ig, b_ig, w_fg, b_fg, ln_w,
                  sh_up, sh_down, ro_up, ro_down, router_w, out):
    es = ExitStack()

    def sb(name, shape, dt=F32):
        return es.enter_context(nc.sbuf_tensor(name, shape, dt))

    def sem(name):
        return es.enter_context(nc.semaphore(name))

    bank = [es.enter_context(nc.psum_tensor(f"bank{n}", [P, 512], F32)) for n in range(8)]

    x_tok = x.rearrange("(t a) s d -> (a s) t d", a=2)
    ctx_tok = ctx_in.rearrange("(t a) s d -> (a s) t d", a=2)
    out_tok = out.rearrange("(t a) s d -> (a s) t d", a=2)
    conv_pad = nc.dram_tensor("conv_pad", (H, S, P), F32, kind="Internal").ap()
    slots = nc.dram_tensor("slots", (SLOT_TILES * P, ROW), F32, kind="Internal").ap()
    routed = nc.dram_tensor("routed", (2 * B * S + DUMP * P, D), F32, kind="Internal").ap()

    tok = sb("tok", [P, NT, D])
    x2T = sb("x2T", [P, NT * P])
    wup = sb("wup", [P, E * FF])
    wdn = sb("wdn", [P, E * FC * D])
    sup = sb("sup", [P, FF])
    sdn = sb("sdn", [P, FC, D])
    ident = sb("ident", [P, P])
    identb = sb("identb", [P, P], BF16)
    onesb = sb("onesb", [P, P], BF16)
    trib = sb("trib", [P, P], BF16)
    causal = sb("causal", [P, NH * S], BF16)
    eps = sb("eps", [P, 1])
    bout = sb("bout", [P, D])
    wv = sb("wv", [P, D])
    wo = sb("wo", [P, D])
    pairw_hi = sb("pairw_hi", [P, H, D], F32R)
    pairw_lo = sb("pairw_lo", [P, H, D], F32R)
    xT_hi = sb("xT_hi", [P, W], F32R)
    xT_lo = sb("xT_lo", [P, W], F32R)
    cpad = sb("cpad", [H, P])
    cin = sb("cin", [H, 2 * MAXPOS + 1])
    bias = sb("bias", [P, H, S])
    gw = sb("gw", [2 * NH, 3 * D])
    gwT = sb("gwT", [P, 3, 2 * NH])
    GR = 2 * GT * NH
    wg = [sb(f"wg{n}", [P, 2 * GT, 2 * GR]) for n in range(2)]
    bi = sb("bi", [GR, 1])
    bf = sb("bf", [GR, 1])
    lnw = sb("lnw", [P, D])
    rw = sb("rw", [P, E])
    xs = sb("xs", [P, GT, D])
    xT = sb("xT", [P, W])
    z = sb("z", [P, H, W])
    prob = sb("prob", [P, GT, H * S])
    wqk = prob[:, 0:2, :].rearrange("p a b -> p (a b)")
    wqkT = prob[:, 2:4, :].rearrange("p a (b c) -> p (a b) c", c=P)
    negmax = sb("negmax", [P, GT, H])
    probT = sb("probT", [P, GT * P])
    vblk = sb("vblk", [P, GT * 8, 2, DV + 1])
    rden = sb("rden", [P, GT, H])
    o = sb("o", [P, D])
    oT = sb("oT", [P, P])
    res = sb("res", [P, GT, D])
    stats = sb("stats", [P, GT, 6])
    mv = sb("mv", [P, GT, 2])
    lnv = sb("lnv", [P, GT])
    rstd = sb("rstd", [P, GT])
    cs = sb("cs", [P, GT, D])
    x1T = sb("x1T", [P, W])
    xTp = [xT, x1T]
    cT = [sb(f"cT{n}", [P, W]) for n in range(2)]
    qblk = [sb(f"qblk{n}", [P, 2 * GT, NH, S]) for n in range(2)]
    vals = [sb(f"vals{n}", [P, GT, NH, DH + 1]) for n in range(2)]
    fpre = sb("fpre", [GR, S])
    ipre = sb("ipre", [GR, S])
    flog = sb("flog", [GR, S])
    logf = sb("logf", [GR, S])
    cumf = sb("cumf", [GR, S])
    arow = sb("arow", [GR, S])
    amax = sb("amax", [GR, S])
    one_s = sb("one_s", [GR, S])
    zero_s = sb("zero_s", [GR, S])
    emx = sb("emx", [GR, S])
    mrow = sb("mrow", [GR, S])
    al = [sb(f"al{n}", [2 * GR, S]) for n in range(2)]
    rh = [sb(f"rh{n}", [2 * GR, 2 * GT, NH, S]) for n in range(2)]
    nhot = sb("nhot", [GR, GR])
    decay = sb("decay", [P, 2, NH * S])
    cmat = sb("cmat", [P, 2, NH * S])
    floor = [sb(f"floor{n}", [P, GT, NH]) for n in range(2)]
    nrm = sb("nrm", [P, GT, NH])
    hst = sb("hst", [P, GT * NH, DH])
    hmu = sb("hmu", [P, GT * NH])
    hsq = sb("hsq", [P, GT * NH, DH])
    hlw = sb("hlw", [P, GT * NH, DH])
    x2s = sb("x2s", [P, GT, D])
    hva = sb("hva", [P, GT * NH])
    hln = sb("hln", [P, GT * NH])
    hrs = sb("hrs", [P, GT * NH])
    mvf = [sb(f"mvf{n}", [P, GT, 2]) for n in range(4)]
    rstdf = [sb(f"rstdf{n}", [P, GT]) for n in range(4)]
    shift = [sb(f"shift{n}", [P, GT]) for n in range(4)]
    lg = sb("lg", [P, NT, E])
    m8 = sb("m8", [P, NT])
    cand = sb("cand", [P, NT, E])
    hot = [sb(f"hot{k}", [P, NT, E]) for k in range(2)]
    hotb = sb("hotb", [P, NT, E], BF16)
    gate = [sb(f"gate{k}", [P, NT]) for k in range(2)]
    io_e = sb("io_e", [P, E])
    io_128 = sb("io_128", [P, NT])
    io_tau = sb("io_tau", [1, SLOT_TILES])
    tote = sb("tote", [P, E, NT])
    cume = sb("cume", [P, E, NT])
    segm = sb("segm", [P, E, NT])
    one8 = sb("one8", [P, E])
    ntile = sb("ntile", [P, E])
    ctile = sb("ctile", [P, E])
    gt = sb("gt", [P, E, NT])
    sl = sb("sl", [P, NT, E])
    slot = [sb(f"slot{k}", [P, NT], I32) for k in range(2)]
    slotf = sb("slotf", [P, NT])
    dest = sb("dest", [P, 2, NT], I32)
    tcmp = sb("tcmp", [1, SLOT_TILES, E])
    texp = sb("texp", [1, SLOT_TILES])
    texpi = sb("texpi", [1, SLOT_TILES], I32)
    prefill = x2T[:, 0:DUMP * ROW].rearrange("p (b r) -> p b r", r=ROW)
    stg = [sb(f"stg{n}", [P, ROW]) for n in range(4)]
    idx = [sb(f"idx{n}", [P, 1], I32) for n in range(4)]
    shT = z[:, :, :].rearrange("p (a c) w -> p a c w", a=2)
    NX = 8
    qflat = qblk[0][:, :, :, :].rearrange("p n h s -> p (n h s)")
    xr = [qflat[:, n * ROW:(n + 1) * ROW] for n in range(NX)]
    yr = [qflat[:, NX * ROW + n * D:NX * ROW + (n + 1) * D] for n in range(4)]
    xrT = cT[0][:, 0:2 * P].rearrange("p (a d) -> p a d", a=2)
    wst = prob[:, 0:2, :]
    hT = prob[:, 2:4, :]
    y0, y1, fin = (a[:, :].rearrange("p (t d) -> p t d", d=D) for a in (wup, wdn, x2T))

    names = """ld_tok ld_wqk ld_conv ld_bias ld_attn ld_small ld_gw ld_wup ld_wdn ld_sh st_cpad cpad_ok
    const_p const_v wqkT_ps wqkT_ok pw_ps pw_ok gwT_ps gw_ok vsteps xs_ok xT_ps xT_ok xhi_ok xlo_ok
    pwlo_ok z_ps z_ok s_ps v_ps v_ok logit_ok exp_ok pT_ps pT_ok av_ps o_ok oT_ps oT_ok pr_ps
    res_ok stat_ok mv_ok lnv_ok rstd_ok x1_ok asteps xs1_ok cs_ok x1T_ps x1T_ok cT_ps cT_ok g_ps
    fpre_ok ipre_ok fabs_ok fexp_ok flog_ok igsteps al_ok rh_ok mrow_ok emx_ok floor_ok qblk_ok
    vals_ok dd_ps decay_ok c_ok u_ps h_ok hsq_ok hva_ok hn_ok hln_ok hrs_ok res1_ok mv1_ok lnv1_ok
    rstd1_ok x2_ok bsteps x2T_ps x2Ts_ok lg_ps lg_ok lmax_ok lexp_ok tokb_ok lnd_ok fl_ps hlw_ok
    tk_ok x2e_ok presum_ok shift_ok rsteps hotb_ok rank_ps texp_ok stage_ok scat0 scat1 scat2 scat3
    pre_ok shu_ps sh_ok shd_ps base_ok xr_ps xrT_ok up_ps wst_ok hT_ok y_ps y_ok passed_pool
    passed_dve passed_act passed_pe mv2_ok lnv2_ok rstd2_ok fin_ok st_out""".split()
    s = {n: sem(n) for n in names}
    ld_xr = [sem(f"ld_xr{n}") for n in range(NX)]
    sc_y = [sem(f"sc_y{n}") for n in range(4)]
    NY = 4
    ld_y0 = [sem(f"ld_y0_{n}") for n in range(NY)]
    ld_y1 = [sem(f"ld_y1_{n}") for n in range(NY)]
    scat = [s[f"scat{n}"] for n in range(4)]
    st_o = [sem(f"st_o{n}") for n in range(NY)]

    def g4(t):
        return bass.ds(t, GT)

    block = es.enter_context(nc.Block())

    @block.sync
    def _(sp):
        sp.dma_start(wqk, w_qk).then_inc(s["ld_wqk"], 16)
        sp.dma_start(xs[:, :, :], x_tok[:, 0:GT, :]).then_inc(s["xs_ok"], 16)
        sp.dma_start(cin[:, :], conv).then_inc(s["ld_conv"], 16)
        sp.dma_start(gw[0:NH, :], w_ig).then_inc(s["ld_gw"], 16)
        sp.dma_start(gw[NH:2 * NH, :], w_fg).then_inc(s["ld_gw"], 16)
        for dst, src in ((bi[:, :], bass.AP(tensor=b_ig.tensor, offset=0, ap=[[0, 2 * GT], [1, NH], [1, 1]])),
                         (bf[:, :], bass.AP(tensor=b_fg.tensor, offset=0, ap=[[0, 2 * GT], [1, NH], [1, 1]])),
                         (rw[:, :], router_w),
                         (lnw[:, :], bass.AP(tensor=ln_w.tensor, offset=0, ap=[[0, P], [1, D]]))):
            sp.dma_start(dst, src).then_inc(s["ld_small"], 16)
        sp.wait_ge(s["cpad_ok"], 3)
        sp.dma_start(conv_pad, cpad[:, :].unsqueeze(1).broadcast_to([H, S, P])).then_inc(s["st_cpad"], 16)
        sp.wait_ge(s["st_cpad"], 16)
        for a in range(2):
            src = bass.AP(tensor=conv_pad.tensor, offset=S - 1, ap=[[P - 1, S], [S * P, H], [1, S]])
            sp.dma_start(bias[a * S:(a + 1) * S, :, :], src).then_inc(s["ld_bias"], 16)
        sp.dma_start(tok[:, :, :], x_tok).then_inc(s["ld_tok"], 16)
        with sp.Fori(1, NG) as g:
            sp.wait_ge(s["xT_ps"], g)
            sp.dma_start(xs[:, :, :], x_tok[:, g4(g * GT), :]).then_inc(s["xs_ok"], 16)
        sp.wait_ge(s["pre_ok"], 1)
        for n in range(SLOT_TILES // DUMP):
            sp.dma_start(slots[n * DUMP * P:(n + 1) * DUMP * P, :].rearrange("(b p) r -> p b r", p=P),
                         prefill[:, :, :]).then_inc(s["st_out"], 16)
        sp.dma_start(sup[:, :], sh_up[0]).then_inc(s["ld_sh"], 16)
        sp.dma_start(sdn[:, :, :], sh_down[0].rearrange("(c p) h -> p c h", p=P)).then_inc(s["ld_sh"], 16)
        sp.dma_start(wup[:, :].rearrange("p (e f) -> p e f", e=E), ro_up.rearrange("e h f -> h e f")).then_inc(s["ld_wup"], 16)
        sp.dma_start(wdn[:, :].rearrange("p (e c h) -> p e c h", e=E, c=FC),
                     ro_down.rearrange("e (c p) h -> p e c h", p=P)).then_inc(s["ld_wdn"], 16)

        def stage_b(g, first=False):
            if not first:
                sp.wait_ge(s["x1T_ps"], g)
            sp.wait_ge(s["x1_ok"], GT * g + GT)
            sp.dma_start(xs[:, :, :], tok[:, g4(g * GT), :]).then_inc(s["xs1_ok"], 16)
            if not first:
                sp.wait_ge(s["cT_ps"], g)
                sp.wait_ge(s["vals_ok"], g)
            sp.dma_start(cs[:, :, :], ctx_tok[:, g4(g * GT), :]).then_inc(s["cs_ok"], 16)

        def keep_x2(g):
            sp.wait_ge(s["x2_ok"], GT * g + GT)
            sp.dma_start(tok[:, g4(g * GT), :], x2s[:, :, :]).then_inc(s["tk_ok"], 16)
        sp.wait_ge(s["xT_ps"], NG)
        stage_b(0, True)
        stage_b(1)
        stage_b(2)
        with sp.Fori(3, NG) as g:
            stage_b(g)
            keep_x2(g - 3)
        for g in range(NG - 3, NG):
            keep_x2(g)
        for n in range(4):
            sp.wait_ge(scat[n], 16 * 2 * NT // 4)
        def load_slots(t, n):
            sp.dma_start(xr[n][:, :], slots[bass.ds(t * P, P), :]).then_inc(ld_xr[n], 16)
        for n in range(NX):
            load_slots(n, n)
        with sp.Fori(1, SLOT_TILES // NX) as i:
            for n in range(NX):
                sp.wait_ge(sc_y[n % 4], 16 * (2 * i - 1 + n // 4))
                load_slots(i * NX + n, n)
        for n in range(4):
            sp.wait_ge(sc_y[n], 16 * SLOT_TILES // 4)
        def final(g, n, first=False):
            for y, ld, first_row, summed in ((y0, ld_y0, 0, "presum_ok"), (y1, ld_y1, B * S, "res1_ok")):
                if not first:
                    sp.wait_ge(s[summed], g - NY + 1 + (NG if summed == "res1_ok" else 0))
                sp.dma_start(y[:, g4(g * GT), :],
                             routed[bass.ds(g * W + first_row, W), :].rearrange("(t p) d -> p t d", p=P)).then_inc(ld[n], 16)
        for n in range(NY):
            final(n, n, True)
        with sp.Fori(1, NG // NY) as i:
            for n in range(NY):
                final(NY * i + n, n)

    @block.gpsimd
    def _(pool):
        st = Steps(pool, s["const_p"])

        def x_lo(g, q):
            pool.wait_ge(s["xhi_ok"], g + 1)
            if not (isinstance(g, int) and g == 0):
                pool.wait_ge(s["z_ps"], H * g)
            pool.wait_ge(s["xT_ok"], g + 1)
            pool.tensor_tensor(xT_lo[:, :], xTp[q][:, :], xT_hi[:, :], ALU.subtract).then_inc(s["xlo_ok"], 1)

        st(pool.memset(ident[:, :], 0.0))
        st(pool.affine_select(out=ident[:, :], in_=ident[:, :], compare_op=ALU.not_equal, fill=1.0,
                              base=0, pattern=[[-1, P]], channel_multiplier=1))
        st(pool.tensor_copy(identb[:, :], ident[:, :]))
        st(pool.memset(causal[:, :], 0.0))
        for a in range(2):
            v = causal[a * S:(a + 1) * S, :].rearrange("p (h s) -> p h s", h=NH)
            st(pool.affine_select(out=v, in_=v, compare_op=ALU.is_ge, fill=-BIG, base=0,
                                  pattern=[[0, NH], [1, S]], channel_multiplier=-1))
        st(pool.memset(trib[:, :], 1.0))
        st(pool.affine_select(out=trib[:, :], in_=trib[:, :], compare_op=ALU.is_gt, fill=0.0, base=0,
                              pattern=[[1, P]], channel_multiplier=-1))
        for q in range(2):
            v = rh[q][GR:2 * GR, :, :, :]
            st(pool.memset(v, 1.0))
            st(pool.affine_select(out=v, in_=v, compare_op=ALU.is_equal, fill=0.0, base=0,
                                  pattern=[[NH, 2 * GT], [1, NH], [0, S]], channel_multiplier=-1))
            if q == 0:
                x_lo(0, 0)
                pool.wait_ge(s["xlo_ok"], 1)
        st(pool.memset(nhot[:, :], -1.0))
        st(pool.affine_select(out=nhot[:, :], in_=nhot[:, :], compare_op=ALU.is_equal, fill=0.0,
                              base=0, pattern=[[1, GR]], channel_multiplier=-1))
        st(pool.iota(io_e[:, :], [[-1, E]], base=E, channel_multiplier=0, allow_small_or_imprecise_dtypes=True))
        st(pool.iota(io_128[:, :], [[P, NT]], base=0, channel_multiplier=0, allow_small_or_imprecise_dtypes=True))
        st(pool.iota(io_tau[:, :], [[1, SLOT_TILES]], base=0, channel_multiplier=0, allow_small_or_imprecise_dtypes=True))
        st(pool.iota(dest[:, :, :], [[B * S, 2], [P, NT]], base=0, channel_multiplier=1))
        st(pool.memset(prefill[:, :, :], 0.0))
        pool.iota(prefill[:, :, :].bitcast(I32)[:, :, DEST], [[P, DUMP]], base=2 * B * S,
                  channel_multiplier=1).then_inc(s["pre_ok"], 1)
        pool.wait_ge(s["ld_tok"], 16)
        pool.wait_ge(s["ld_attn"], 16 * 3)
        def bias_in(n):
            half = tok[:, n * NT // 2:(n + 1) * NT // 2, :]
            pool.tensor_tensor(half, half, bout[:, :].unsqueeze(1).broadcast_to([P, NT // 2, D]), ALU.add)\
                .then_inc(s["tokb_ok"], 1)
        bias_in(0)
        x_lo(1, 1)
        bias_in(1)
        with pool.Fori(1, NG // 2) as i:
            for n in range(2):
                x_lo(2 * i + n, n)

        def maxima(g, q):
            if not (isinstance(g, int) and g < 2):
                pool.wait_ge(s["dd_ps"], GT * (g - 1))
            pool.wait_ge(s["mrow_ok"], g + 1)
            for n in range(2):
                c = slice(n * GR // 2, (n + 1) * GR // 2)
                pool.tensor_tensor(rh[q][0:GR, :, :, :].rearrange("r j h s -> r (j h) s")[:, c, :],
                                   spread(nhot[:, c], [GR, GR // 2, S]),
                                   amax[:, :].unsqueeze(1).broadcast_to([GR, GR // 2, S]), ALU.mult).then_inc(s["rh_ok"], 1)

        def weighted(g):
            pool.wait_ge(s["h_ok"], g + 1)
            pool.tensor_tensor(hlw[:, :, :].rearrange("p (k h) d -> p k (h d)", k=GT),
                               hst[:, :, :].rearrange("p (k h) d -> p k (h d)", k=GT),
                               lnw[:, :].unsqueeze(1).broadcast_to([P, GT, D]), ALU.mult).then_inc(s["hlw_ok"], 1)
        maxima(0, 0)
        maxima(1, 1)
        with pool.Fori(0, (NG - 2) // 2) as i:
            for n in range(2):
                weighted(2 * i + n)
                maxima(2 * i + 2 + n, n)
        weighted(NG - 2)
        weighted(NG - 1)
        pool.wait_ge(s["st_out"], 16 * (SLOT_TILES // DUMP))
        with pool.Fori(0, NT // 2) as i:
            for n in range(4):
                pause(pool, s["stage_ok"], 4 * i + n + 1, s["passed_pool"])
                pool.indirect_dma_start(slots, bass.IndirectOffsetOnAxis(ap=idx[n][:, 0:1], axis=0),
                                        stg[n][:, :], None).then_inc(scat[n], 16)
        with pool.Fori(0, SLOT_TILES // NX) as i:
            for n in range(NX):
                pause(pool, s["y_ok"], NX * i + n + 1, s["passed_pool"])
                pool.indirect_dma_start(routed, bass.IndirectOffsetOnAxis(ap=xr[n][:, :].bitcast(I32)[:, DEST:DEST + 1], axis=0),
                                        yr[n % 4][:, :], None).then_inc(sc_y[n % 4], 16)

        def presum(g, n, i):
            pool.wait_ge(ld_y0[n], 16 * (i + 1))
            pool.tensor_tensor(y0[:, g4(g * GT), :], y0[:, g4(g * GT), :], tok[:, g4(g * GT), :], ALU.add)\
                .then_inc(s["presum_ok"], 1)
        with pool.Fori(0, NG // NY) as i:
            for n in range(NY):
                presum(NY * i + n, n, i)

    @block.scalar
    def _(act):
        def x_hi(g):
            act.wait_ge(s["xT_ps"], g + 1)
            if not (isinstance(g, int) and g == 0):
                act.wait_ge(s["z_ps"], H * g)
            act.activation(xT_hi[:, :], bank[7][:, :], ACT.Copy).then_inc(s["xhi_ok"], 1)

        def x_evac(g, q):
            act.activation(xTp[q][:, :], bank[7][:, :], ACT.Copy).then_inc(s["xT_ok"], 1)

        def z_evac(g, h):
            act.wait_ge(s["z_ps"], H * g + h + 1)
            if h == 0 and not (isinstance(g, int) and g == 0):
                act.wait_ge(s["s_ps"], GT * g)
            act.activation(z[:, h, :], bank[4 + h % 2][:, :], ACT.Copy).then_inc(s["z_ok"], 1)

        def exps(g, k):
            act.wait_ge(s["logit_ok"], GT * g + k + 1)
            act.activation(prob[:, k, :], prob[:, k, :], ACT.Exp).then_inc(s["exp_ok"], 1)

        def pT_evac(g, k):
            act.wait_ge(s["pT_ps"], GT * g + k + 1)
            act.activation(probT[:, :], bank[6][:, :], ACT.Copy).then_inc(s["pT_ok"], 1)

        def oT_evac(g, k):
            act.wait_ge(s["oT_ps"], GT * g + k + 1)
            act.activation(oT[:, :], bank[k][:, 136:136 + P], ACT.Copy).then_inc(s["oT_ok"], 1)

        def rsqrt(mv_sem, need, src, ln_out, ln_sem, r_out, r_sem, count, scale=1.0):
            act.wait_ge(mv_sem, need)
            act.activation(ln_out, src, ACT.Ln, bias=eps[:, 0:1], scale=scale).then_inc(ln_sem, 1)
            act.wait_ge(ln_sem, count)
            act.activation(r_out, ln_out, ACT.Exp, scale=-0.5).then_inc(r_sem, 1)

        def v_evac(g, first):
            act.wait_ge(s["v_ps"], g + 1)
            if not first:
                act.wait_ge(s["av_ps"], GT * g)
            for half in range(2):
                r = slice(half * S, half * S + S)
                act.activation(vblk[r, :, half, 0:DV], bank[7][r, :].rearrange("p (n d) -> p n d", d=DV),
                               ACT.Copy).then_inc(s["v_ok"], 1)

        def group_a(g, q, more, first=False):
            v_evac(g, first)
            if not first:
                oT_evac(g - 1, GT - 1)
            if more:
                x_hi(g + 1)
                x_evac(g + 1, 1 - q)
            exps(g, 0)
            if not first:
                rsqrt_a(g - 1)
            pT_evac(g, 0)
            if more:
                z_evac(g + 1, 0)
            exps(g, 1)
            if more:
                z_evac(g + 1, 1)
            pT_evac(g, 1)
            if more:
                z_evac(g + 1, 2)
            oT_evac(g, 0)
            exps(g, 2)
            if more:
                z_evac(g + 1, 3)
            pT_evac(g, 2)
            if more:
                z_evac(g + 1, 4)
            oT_evac(g, 1)
            exps(g, 3)
            if more:
                z_evac(g + 1, 5)
            pT_evac(g, 3)
            if more:
                z_evac(g + 1, 6)
            oT_evac(g, 2)
            if more:
                z_evac(g + 1, 7)

        def rsqrt_a(g):
            rsqrt(s["mv_ok"], GT * g + GT, mv[:, :, 1], lnv[:, :], s["lnv_ok"], rstd[:, :], s["rstd_ok"], g + 1)

        act.preload_act_table_set("natural_log_exp_and_others")
        act.dma_start(wv[:, :], w_v).then_inc(s["ld_attn"], 16)
        act.dma_start(wo[:, :], w_out).then_inc(s["ld_attn"], 16)
        act.dma_start(bout[:, :], bass.AP(tensor=b_out.tensor, offset=0, ap=[[0, P], [1, D]])).then_inc(s["ld_attn"], 16)
        act.wait_ge(s["wqkT_ps"], 1)
        act.activation(wqkT[:, 0:4, :], bank[0][:, :].rearrange("p (a b) -> p a b", a=4), ACT.Copy).then_inc(s["wqkT_ok"], 1)
        act.activation(wqkT[:, 4:8, :], bank[1][:, :].rearrange("p (a b) -> p a b", a=4), ACT.Copy).then_inc(s["wqkT_ok"], 1)
        x_hi(0)
        x_evac(0, 0)
        act.wait_ge(s["pw_ps"], 1)
        for a in range(2):
            act.activation(pairw_hi[:, a:H:2, :], bank[2 + a][:, :].rearrange("p (a b) -> p a b", a=4),
                           ACT.Copy, scale=DQ ** -0.5).then_inc(s["pw_ok"], 1)
        for h in range(H):
            z_evac(0, h)
        act.wait_ge(s["const_v"], 1)
        group_a(0, 0, True, True)
        with act.Fori(0, (NG - 2) // 2) as i:
            for n in range(2):
                group_a(2 * i + 1 + n, 1 - n, True)
        group_a(NG - 1, 1, False)
        oT_evac(NG - 1, GT - 1)
        rsqrt_a(NG - 1)

        def x2_evac(g):
            act.wait_ge(s["x2T_ps"], g + 1)
            act.activation(xT[:, :], bank[2][:, :], ACT.Copy).then_inc(s["x2Ts_ok"], 1)

        def x2_keep(g):
            act.activation(x2T[:, bass.ds(g * W, W)], bank[2][:, :], ACT.Copy).then_inc(s["x2e_ok"], 1)

        def front_turn(g, q):
            act.wait_ge(s["x1T_ps"], g + 1)
            act.activation(x1T[:, :], bank[0][:, :], ACT.Copy).then_inc(s["x1T_ok"], 1)
            act.wait_ge(s["cT_ps"], g + 1)
            act.activation(cT[q][:, :], bank[1][:, :], ACT.Copy).then_inc(s["cT_ok"], 1)

        def front_queries(g, q):
            for h in range(NH):
                r = slice(h * DH, (h + 1) * DH)
                act.activation(qblk[q][r, :, h, :], bank[0][r, :].rearrange("p (n s) -> p n s", s=S),
                               ACT.Copy).then_inc(s["qblk_ok"], 1)

        def front_values(g, q):
            act.wait_ge(s["cs_ok"], 16 * (g + 1))
            act.activation(vals[q][:, :, :, 0:DH], cs[:, :, :].rearrange("p k (h d) -> p k h d", h=NH),
                           ACT.Copy).then_inc(s["vals_ok"], 1)

        def front_gates(g):
            act.wait_ge(s["g_ps"], g + 1)
            act.activation(fpre[:, :], bank[7][0:GR, 0:S], ACT.Identity, bias=bf[:, 0:1]).then_inc(s["fpre_ok"], 1)
            act.activation(ipre[:, :], bank[7][GR:2 * GR, 0:S], ACT.Identity, bias=bi[:, 0:1]).then_inc(s["ipre_ok"], 1)
            act.wait_ge(s["fpre_ok"], g + 1)
            act.activation(flog[:, :], fpre[:, :], ACT.Abs).then_inc(s["fabs_ok"], 1)
            act.wait_ge(s["fabs_ok"], g + 1)
            act.activation(flog[:, :], flog[:, :], ACT.Exp, scale=-1.0).then_inc(s["fexp_ok"], 1)
            act.wait_ge(s["fexp_ok"], g + 1)
            act.activation(flog[:, :], flog[:, :], ACT.Ln, bias=1.0).then_inc(s["flog_ok"], 1)

        def front_floor(g, q):
            act.wait_ge(s["fl_ps"], g + 1)
            for a in range(2):
                r = slice(a * S, (a + 1) * S)
                act.activation(floor[q][r, :, :], bank[7][r, S:S + GR].rearrange("p (k a h) -> p a k h", a=2, h=NH)[:, a],
                               ACT.Copy).then_inc(s["floor_ok"], 1)

        def front_emx(g):
            act.wait_ge(s["mrow_ok"], g + 1)
            act.activation(emx[:, :], mrow[:, :], ACT.Exp, scale=-1.0).then_inc(s["emx_ok"], 1)

        def decays(g, k):
            act.wait_ge(s["dd_ps"], GT * g + k + 1)
            act.activation(decay[:, k % 2, :], bank[3 + k % 2][:, 256:512], ACT.Exp).then_inc(s["decay_ok"], 1)

        def squares(g):
            act.wait_ge(s["h_ok"], g + 1)
            act.activation(hsq[:, :, :], hst[:, :, :], ACT.Square).then_inc(s["hsq_ok"], 1)

        def rsqrt_h(g):
            rsqrt(s["hva_ok"], g + 1, hva[:, :], hln[:, :], s["hln_ok"], hrs[:, :], s["hrs_ok"], g + 1, scale=1.0 / DH)

        def rsqrt_x(g):
            rsqrt(s["mv1_ok"], GT * g + GT, mv[:, :, 1], lnv[:, :], s["lnv1_ok"], rstd[:, :], s["rstd1_ok"], g + 1)

        def group_b(g, q, before, after, late=True):
            if after:
                front_turn(g + 1, 1 - q)
            decays(g, 0)
            if before:
                squares(g - 1)
            decays(g, 1)
            if late:
                x2_evac(g - 2)
            if after:
                front_gates(g + 1)
                front_queries(g + 1, 1 - q)
            decays(g, 2)
            if after:
                front_values(g + 1, 1 - q)
            decays(g, 3)
            if before:
                rsqrt_h(g - 1)
            if late:
                x2_keep(g - 2)
            if after:
                front_emx(g + 1)
                front_floor(g + 1, 1 - q)
            if before:
                rsqrt_x(g - 1)
        act.wait_ge(s["st_out"], 16 * (SLOT_TILES // DUMP))
        front_turn(0, 0)
        front_queries(0, 0)
        front_values(0, 0)
        front_gates(0)
        front_emx(0)
        front_floor(0, 0)
        group_b(0, 0, False, True, False)
        group_b(1, 1, True, True, False)
        with act.Fori(0, (NG - 4) // 2) as i:
            for n in range(2):
                group_b(2 * i + 2 + n, n, True, True)
        group_b(NG - 2, 0, True, True)
        group_b(NG - 1, 1, True, False)
        squares(NG - 1)
        rsqrt_h(NG - 1)
        x2_evac(NG - 2)
        x2_keep(NG - 2)
        rsqrt_x(NG - 1)
        x2_evac(NG - 1)
        x2_keep(NG - 1)
        act.wait_ge(s["lmax_ok"], 1)
        act.activation(lg[:, :, :], lg[:, :, :], ACT.Exp).then_inc(s["lexp_ok"], 1)
        with act.Fori(0, NG // 2) as i:
            for a in range(2):
                g = 2 * i + a
                for c in range(FC):
                    act.wait_ge(s["shu_ps"], FC * g + c + 1)
                    act.activation(shT[:, a, c, :], bank[c % 2][:, :], ACT.Gelu).then_inc(s["sh_ok"], 1)
        def gelu(t, n):
            act.wait_ge(s["up_ps"], t + 1)
            act.activation(hT[:, n % 2, :], bank[2 + n % 2][:, :], ACT.Gelu).then_inc(s["hT_ok"], 1)
        with act.Fori(0, SLOT_TILES // 2) as i:
            for n in range(2):
                gelu(2 * i + n, n)
        act.preload_act_table_set("natural_log_exp_and_others")
        def last_a(g, n, i, first=False):
            if not (isinstance(g, int) and g == NG - 1):
                last_rstd(g + 1, (n + 1) % NY)
            pause(act, s["shift_ok"], g + 1, s["passed_act"])
            for k in range(GT):
                t = bass.ds(g * GT + k, 1)
                m = act.activation(fin[:, t, :], y1[:, t, :], ACT.Identity, scale=rstdf[n][:, k:k + 1],
                                   bias=shift[n][:, k:k + 1])
            m.then_inc(s["fin_ok"], 1)
            act.wait_ge(s["fin_ok"], g + 1)
            if not first:
                act.wait_ge(st_o[n], 16 * i)
            act.dma_start(out_tok[:, g4(g * GT), :], fin[:, g4(g * GT), :]).then_inc(st_o[n], 16)

        def last_rstd(g, n):
            act.wait_ge(s["mv2_ok"], GT * g + GT)
            if not (isinstance(g, int) and g == 0):
                act.wait_ge(s["rstd2_ok"], g)
            act.activation(lnv[:, :], mvf[n][:, :, 1], ACT.Ln, bias=eps[:, 0:1]).then_inc(s["lnv2_ok"], 1)
            act.wait_ge(s["lnv2_ok"], g + 1)
            act.activation(rstdf[n][:, :], lnv[:, :], ACT.Exp, scale=-0.5).then_inc(s["rstd2_ok"], 1)
        last_rstd(0, 0)
        for n in range(NY):
            last_a(n, n, 0, True)
        for n in range(NY):
            last_a(NY + n, n, 1)
        for n in range(NY):
            act.wait_ge(st_o[n], 16 * NG // NY)

    @block.tensor
    def _(pe):
        mm = pe.matmul
        pe.wait_ge(s["const_p"], 3)
        pe.wait_ge(s["ld_wqk"], 16)
        for c in range(H):
            m = pe.transpose(bank[c // 4][:, (c % 4) * P:(c % 4 + 1) * P], wqk[:, c * P:(c + 1) * P], ident[:, :])
        m.then_inc(s["wqkT_ps"], 1)
        pe.wait_ge(s["ld_gw"], 32)
        for c in range(3):
            m = pe.transpose(bank[6][:, 8 * c:8 * c + 8], gw[:, c * D:(c + 1) * D], ident[0:8, 0:8])
        m.then_inc(s["gwT_ps"], 1)

        def x_turn(g):
            pe.wait_ge(s["xs_ok"], 16 * (g + 1))
            if not (isinstance(g, int) and g == 0):
                pe.wait_ge(s["v_ok"], 2 * g)
            for k in range(GT):
                m = pe.transpose(bank[7][:, k * P:(k + 1) * P], xs[:, k, :], ident[:, :])
            m.then_inc(s["xT_ps"], 1)
        x_turn(0)
        pe.wait_ge(s["wqkT_ok"], 2)
        for a in range(2):
            for j in range(4):
                r = slice(a * DQ, (a + 1) * DQ)
                m = mm(bank[2 + a][:, j * P:(j + 1) * P], wqkT[r, 4 + j, :], wqkT[r, j, :], start=True, stop=True)
        m.then_inc(s["pw_ps"], 1)
        pe.wait_ge(s["pwlo_ok"], 2)
        pe.wait_ge(s["xlo_ok"], 1)

        def z_mm(g, h, early=False):
            if h == 0 and not (isinstance(g, int) and g == 0):
                pe.wait_ge(s["xlo_ok"], g + 1)
            if not (early and h < 2):
                pe.wait_ge(s["z_ok"], H * g + h - 1)
            mm(bank[4 + h % 2][:, :], pairw_hi[:, h, :], xT_hi[:, :], start=True, stop=False)
            mm(bank[4 + h % 2][:, :], pairw_lo[:, h, :], xT_hi[:, :], start=False, stop=False)
            mm(bank[4 + h % 2][:, :], pairw_hi[:, h, :], xT_lo[:, :], start=False, stop=True).then_inc(s["z_ps"], 1)
        for h in range(H):
            z_mm(0, h, True)
        pe.wait_ge(s["ld_attn"], 16 * 3)
        pe.wait_ge(s["const_v"], 1)

        def proj(g, k):
            pe.wait_ge(s["oT_ok"], GT * g + k + 1)
            mm(bank[k][:, 264:264 + D], oT[:, :], wo[:, :], start=True, stop=True).then_inc(s["pr_ps"], 1)

        def out_turn(g, k):
            pe.wait_ge(s["o_ok"], GT * g + k + 1)
            pe.transpose(bank[k][:, 136:136 + P], o[:, :], ident[:, :]).then_inc(s["oT_ps"], 1)

        def scores(g, q, k):
            pe.wait_ge(s["res_ok"], GT * g + k + 1)
            for a in range(2):
                c = slice(k * P + a * S, k * P + a * S + S)
                m = mm(bank[k][a * S:(a + 1) * S, :], xTp[q][:, c], z[:, :, c], start=True, stop=True)
            m.then_inc(s["s_ps"], 1)

        def values(g, q):
            for k in range(GT):
                for a in range(2):
                    for half in range(2):
                        m = mm(bank[7][half * S:(half + 1) * S, k * P + a * 64:k * P + a * 64 + 64],
                               xTp[q][:, k * P + a * S:k * P + a * S + S],
                               wv[:, :].rearrange("p (j e d) -> p e j d", e=2, d=DV)[:, half],
                               start=True, stop=True)
            m.then_inc(s["v_ps"], 1)

        def prob_turn(g, k):
            pe.wait_ge(s["exp_ok"], GT * g + k + 1)
            pe.wait_ge(s["pT_ok"], GT * g + k + 1)
            for j in range(4):
                m = pe.transpose(bank[6][:, j * P:(j + 1) * P], prob[:, k, j * P:(j + 1) * P], ident[:, :])
            m.then_inc(s["pT_ps"], 1)

        def heads(g, k):
            pe.wait_ge(s["pT_ok"], GT * g + k + 2)
            if k == 0:
                pe.wait_ge(s["v_ok"], 2 * g + 2)
            for j in range(4):
                for a in range(2):
                    m = mm(bank[k][a * S:(a + 1) * S, j * 34:j * 34 + 34],
                           probT[:, j * P + a * S:j * P + a * S + S],
                           vblk[:, k * 8 + a * 4 + j, :, :], start=True, stop=True)
            m.then_inc(s["av_ps"], 1)

        def group_a(g, q, more, first=False):
            pe.wait_ge(s["z_ok"], H * g + H)
            scores(g, q, 0)
            if not first:
                out_turn(g - 1, GT - 1)
            if more:
                x_turn(g + 1)
            scores(g, q, 1)
            if not first:
                proj(g - 1, GT - 1)
            scores(g, q, 2)
            scores(g, q, 3)
            prob_turn(g, 0)
            if more:
                z_mm(g + 1, 0)
            heads(g, 0)
            if more:
                z_mm(g + 1, 1)
            prob_turn(g, 1)
            if more:
                z_mm(g + 1, 2)
            out_turn(g, 0)
            heads(g, 1)
            if more:
                z_mm(g + 1, 3)
            proj(g, 0)
            prob_turn(g, 2)
            if more:
                z_mm(g + 1, 4)
            out_turn(g, 1)
            heads(g, 2)
            if more:
                z_mm(g + 1, 5)
            proj(g, 1)
            prob_turn(g, 3)
            if more:
                z_mm(g + 1, 6)
            out_turn(g, 2)
            heads(g, 3)
            if more:
                z_mm(g + 1, 7)
            proj(g, 2)
            if more:
                values(g + 1, 1 - q)
        pe.wait_ge(s["xT_ok"], 1)
        values(0, 0)
        group_a(0, 0, True, True)
        with pe.Fori(0, (NG - 2) // 2) as i:
            for n in range(2):
                group_a(2 * i + 1 + n, 1 - n, True)
        group_a(NG - 1, 1, False)
        out_turn(NG - 1, GT - 1)
        proj(NG - 1, GT - 1)
        pe.wait_ge(s["res_ok"], NT + GT)

        def front_turn(g):
            pe.wait_ge(s["xs1_ok"], 16 * (g + 1))
            if not (isinstance(g, int) and g == 0):
                pe.wait_ge(s["qblk_ok"], NH * g)
                pe.wait_ge(s["cT_ok"], g)
            for k in range(GT):
                m = pe.transpose(bank[0][:, k * P:(k + 1) * P], xs[:, k, :], ident[:, :])
            m.then_inc(s["x1T_ps"], 1)
            pe.wait_ge(s["cs_ok"], 16 * (g + 1))
            for k in range(GT):
                m = pe.transpose(bank[1][:, k * P:(k + 1) * P], cs[:, k, :], ident[:, :])
            m.then_inc(s["cT_ps"], 1)

        def front_gates(g, q):
            pe.wait_ge(s["x1T_ok"], g + 1)
            pe.wait_ge(s["cT_ok"], g + 1)
            if not (isinstance(g, int) and g == 0):
                pe.wait_ge(s["floor_ok"], 2 * g)
            if not (isinstance(g, int) and g < 4):
                pe.wait_ge(s["lg_ok"], g - 3)
            for j in range(2 * GT):
                for n, src in enumerate((x1T, cT[q])):
                    m = mm(bank[7][0:2 * GR, 0:S], wg[n][:, j, :], src[:, j * S:(j + 1) * S],
                           start=(j == 0 and n == 0), stop=(j == 2 * GT - 1 and n == 1))
            m.then_inc(s["g_ps"], 1)

        def front_floor(g):
            if not (isinstance(g, int) and g < 3):
                pe.wait_ge(s["lg_ok"], g - 2)
            pause(pe, s["emx_ok"], g + 1, s["passed_pe"])
            for a in range(2):
                m = mm(bank[7][a * S:(a + 1) * S, S:S + GR], emx[:, :], ident[0:GR, 0:GR], start=True, stop=True)
            m.then_inc(s["fl_ps"], 1)

        def qk(g, q, k, first):
            t = GT * g + k
            if not (first and k < 2):
                pe.wait_ge(s["c_ok"], t - 1)
            if k == 0:
                pe.wait_ge(s["qblk_ok"], NH * g + NH)
                pe.wait_ge(s["al_ok"], g + 1)
            if k in (0, 2):
                pe.wait_ge(s["rh_ok"], 2 * g + 1 + k // 2)
            bk = bank[3 + k % 2]
            for a in range(2):
                mm(bk[a * S:(a + 1) * S, 0:256], cT[q][:, k * P + a * S:k * P + a * S + S],
                   qblk[q][:, 2 * k + a, :, :], start=True, stop=True)
            for a in range(2):
                mm(bk[a * S:(a + 1) * S, 256:512], al[q][:, :], rh[q][:, 2 * k + a, :, :],
                   start=True, stop=False, skip_group_check=True)
            mm(bk[:, 256:512], identb[:, :], causal[:, :], start=False, stop=True,
               skip_group_check=True).then_inc(s["dd_ps"], 1)

        def av(g, q, k, first):
            if k == 0:
                pe.wait_ge(s["vals_ok"], g + 1)
                if not first:
                    pe.wait_ge(s["h_ok"], g)
            pause(pe, s["c_ok"], GT * g + k + 1, s["passed_pe"])
            for h in range(NH):
                for a in range(2):
                    r = slice(a * S, (a + 1) * S)
                    c = (k % 2) * 132 + h * 33
                    m = mm(bank[5 + k // 2][r, c:c + 33], cmat[r, k % 2, h * S:(h + 1) * S],
                           vals[q][r, k, h, :], start=True, stop=True)
            m.then_inc(s["u_ps"], 1)

        def x2_turn(g):
            if not (isinstance(g, int) and g == 0):
                pe.wait_ge(s["x2e_ok"], g)
            pe.wait_ge(s["x2_ok"], GT * g + GT)
            for k in range(GT):
                m = pe.transpose(bank[2][:, k * P:(k + 1) * P], x2s[:, k, :], ident[:, :])
            m.then_inc(s["x2T_ps"], 1)

        def router(g):
            pe.wait_ge(s["x2Ts_ok"], g + 1)
            pe.wait_ge(s["ipre_ok"], min(g + 4, NG) if isinstance(g, int) else g + 4)
            pe.wait_ge(s["floor_ok"], 2 * min(g + 3, NG) if isinstance(g, int) else 2 * (g + 3))
            for k in range(GT):
                m = mm(bank[7][:, 64 + k * E:64 + (k + 1) * E], xT[:, k * P:(k + 1) * P], rw[:, :], start=True, stop=True)
            m.then_inc(s["lg_ps"], 1)

        def group_b(g, q, after, first=False, late=True):
            if after:
                front_turn(g + 1)
            qk(g, q, 0, first)
            qk(g, q, 1, first)
            if after:
                front_gates(g + 1, 1 - q)
            if late:
                x2_turn(g - 2)
            av(g, q, 0, first)
            av(g, q, 1, first)
            qk(g, q, 2, first)
            if late:
                router(g - 2)
            qk(g, q, 3, first)
            av(g, q, 3, first)
            if after:
                front_floor(g + 1)
            av(g, q, 2, first)
        pe.wait_ge(s["const_p"], N_CONST)
        pe.wait_ge(s["gw_ok"], 1)
        front_turn(0)
        front_gates(0, 0)
        front_floor(0)
        group_b(0, 0, True, True, False)
        group_b(1, 1, True, False, False)
        for n in range(2):
            group_b(2 + n, n, True)
        with pe.Fori(1, (NG - 4) // 2) as i:
            for n in range(2):
                group_b(2 * i + 2 + n, n, True)
        group_b(NG - 2, 0, True)
        group_b(NG - 1, 1, False)
        x2_turn(NG - 2)
        router(NG - 2)
        pe.wait_ge(s["x2e_ok"], NG - 1)
        x2_turn(NG - 1)
        pe.wait_ge(s["lg_ok"], NG - 1)
        router(NG - 1)
        pe.wait_ge(s["lg_ok"], NG)
        pe.wait_ge(s["x2e_ok"], NG)
        def ranks():
            pe.wait_ge(s["hotb_ok"], 1)
            hb = hotb[:, :, :].rearrange("p t e -> p (t e)")
            mm(bank[6][:, 0:256], trib[:, :], hb, start=True, stop=True)
            mm(bank[6][:, 256:512], onesb[:, :], hb, start=True, stop=True).then_inc(s["rank_ps"], 1)
        pe.wait_ge(s["ld_sh"], 32)

        def sh_up_mm(g, first=False):
            for c in range(FC):
                if not (first and c < 2):
                    pe.wait_ge(s["sh_ok"], FC * g + c - 1)
                mm(bank[c % 2][:, :], sup[:, c * P:(c + 1) * P], x2T[:, bass.ds(g * W, W)],
                   start=True, stop=True).then_inc(s["shu_ps"], 1)

        def sh_down_mm(g, a, first=False):
            pe.wait_ge(s["sh_ok"], FC * g + FC)
            if not first:
                pe.wait_ge(s["base_ok"], g)
            for k in range(GT):
                for c in range(FC):
                    m = mm(bank[4 + a][:, k * D:(k + 1) * D], shT[:, a, c, k * P:(k + 1) * P], sdn[:, c, :],
                           start=(c == 0), stop=(c == FC - 1))
            m.then_inc(s["shd_ps"], 1)
        sh_up_mm(0, True)
        ranks()
        sh_up_mm(1)
        sh_down_mm(0, 0, True)
        with pe.Fori(1, NG // 2) as i:
            sh_up_mm(2 * i)
            sh_down_mm(2 * i - 1, 1)
            sh_up_mm(2 * i + 1)
            sh_down_mm(2 * i, 0)
        sh_down_mm(NG - 1, 1)
        pe.wait_ge(s["base_ok"], NG + 1)
        pe.wait_ge(s["texp_ok"], 1)
        pe.wait_ge(s["ld_wup"], 16)
        pe.wait_ge(s["ld_wdn"], 16)
        pe.wait_ge(s["rsteps"], 1)

        def expert(t):
            return pe.value_load(texpi[0:1, bass.ds(t, 1)], min_val=0, max_val=E - 1)

        def turn(t, n, i):
            pe.wait_ge(ld_xr[n % NX], 16 * (i + 1))
            if not (isinstance(t, int) and t < 2):
                pe.wait_ge(s["xrT_ok"], t - 1)
            pe.transpose(bank[n % 2][:, 0:P], xr[n % NX][:, 0:D], ident[:, :]).then_inc(s["xr_ps"], 1)

        def up(t, n):
            pe.wait_ge(s["wst_ok"], t + 1)
            pe.wait_ge(s["xrT_ok"], t + 1)
            if not (isinstance(t, int) and t < 2):
                pe.wait_ge(s["hT_ok"], t - 1)
            for c in range(FC):
                m = mm(bank[2 + n % 2][:, c * P:(c + 1) * P], wst[:, n % 2, c * P:(c + 1) * P], xrT[:, n % 2, :],
                       start=True, stop=True)
            m.then_inc(s["up_ps"], 1)

        def down(t, n):
            e = expert(t)
            pe.wait_ge(s["hT_ok"], t + 1)
            if not (isinstance(t, int) and t < 2):
                pe.wait_ge(s["y_ok"], t - 1)
            for c in range(FC):
                m = mm(bank[6 + n % 2][:, 0:D], hT[:, n % 2, c * P:(c + 1) * P],
                       wdn[:, bass.ds(e * (FC * D) + c * D, D)], start=(c == 0), stop=(c == FC - 1))
            m.then_inc(s["y_ps"], 1)

        def step(t, n, i, lo=True, hi=True):
            if hi:
                turn(t, n, i)
            if (not isinstance(t, int)) or (t >= 1 and t - 1 < SLOT_TILES):
                up(t - 1, n - 1)
            if (not isinstance(t, int)) or (t >= 2 and t - 2 < SLOT_TILES):
                down(t - 2, n - 2)
        for t in range(NX):
            step(t, t, 0)
        with pe.Fori(1, SLOT_TILES // NX) as i:
            for n in range(NX):
                step(i * NX + n, n, i)
        for t in range(SLOT_TILES, SLOT_TILES + 2):
            step(t, t, 0, hi=False)

    @block.vector
    def _(dve):
        tt, tsc, stt = dve.tensor_tensor, dve.tensor_scalar, dve.scalar_tensor_tensor
        dve.sem_inc(s["res_ok"], GT)
        dve.sem_inc(s["pT_ok"], 1)
        dve.sem_inc(s["base_ok"], 1)
        st = Steps(dve, s["vsteps"])
        dve.wait_ge(s["ld_conv"], 16)
        lo = S - 1 - MAXPOS
        nn = 2 * MAXPOS + 1
        dve.tensor_copy(cpad[:, lo:lo + nn], cin[:, :]).then_inc(s["cpad_ok"], 1)
        dve.tensor_copy(cpad[:, 0:lo], cin[:, 0:1].broadcast_to([H, lo])).then_inc(s["cpad_ok"], 1)
        dve.tensor_copy(cpad[:, lo + nn:P], cin[:, nn - 1:nn].broadcast_to([H, P - lo - nn])).then_inc(s["cpad_ok"], 1)
        st(dve.memset(eps[:, :], LN_EPS))
        st(dve.memset(onesb[:, :], 1.0))
        st(dve.memset(one8[:, :], 1.0))
        st(dve.memset(vblk[:, :, :, :], 0.0))
        st(dve.memset(vblk[0:S, :, 0, DV:DV + 1], 1.0))
        st(dve.memset(vblk[S:P, :, 1, DV:DV + 1], 1.0))
        for a in range(2):
            dve.wait_ge(s["pw_ok"], a + 1)
            stt(pairw_lo[:, a:H:2, :], bank[2 + a][:, :].rearrange("p (a b) -> p a b", a=4), DQ ** -0.5,
                pairw_hi[:, a:H:2, :], ALU.mult, ALU.subtract).then_inc(s["pwlo_ok"], 1)
        for q in range(2):
            st(dve.memset(qblk[q][:, :, :, :], 0.0))
            st(dve.memset(vals[q][:, :, :, DH:DH + 1], 1.0))
            st(dve.memset(al[q][0:GR, :], 1.0))
        st(dve.memset(one_s[:, :], 1.0))
        st(dve.memset(zero_s[:, :], 0.0))
        st(dve.memset(segm[:, :, :], 1.0))
        st(dve.memset(segm[:, :, 0], 0.0))
        for n in range(4):
            st(dve.memset(stg[n][:, :], 0.0))
        for n in range(2):
            st(dve.memset(wg[n][:, :, :], 0.0))
        dve.sem_inc(s["const_v"], 1)
        dve.wait_ge(s["ld_small"], 16 * 4)
        st(tsc(lnw[:, :], lnw[:, :], 1.0, None, ALU.add))
        dve.wait_ge(s["gwT_ps"], 1)
        st(dve.tensor_copy(gwT[:, :, :], bank[6][:, 0:24].rearrange("p (a b) -> p a b", a=3)))
        st(tt(gwT[:, 1, :], gwT[:, 1, :], gwT[:, 2, :], ALU.add))
        for n in range(2):
            for rows, cols in ((0, NH), (GR, 0)):
                w0 = wg[n][:, 0, rows:rows + NH]
                dst = bass.AP(tensor=w0.tensor, offset=w0.offset, ap=[list(w0.ap[0]), [2 * GR + NH, 2 * GT], [1, NH]])
                st(dve.tensor_copy(dst, gwT[:, n, cols:cols + NH].unsqueeze(1).broadcast_to([P, 2 * GT, NH])))
        dve.sem_inc(s["gw_ok"], 1)
        dve.wait_ge(s["ld_bias"], 32)

        def layernorm(g, mv_sem, rstd_sem, src, dst, done):
            dve.wait_ge(rstd_sem, g + 1)
            for k in range(GT):
                tsc(dst[:, k, :], src[:, k, :], mv[:, k, 0:1], rstd[:, k:k + 1],
                    ALU.subtract, ALU.mult).then_inc(done, 1)

        def scores(g, k, st):
            dve.wait_ge(s["s_ps"], GT * g + k + 1)
            p3 = prob[:, k, :].rearrange("p (h j) -> p h j", h=H)
            st(tt(prob[:, k, :], bank[k][:, :], bias[:, :, :].rearrange("p h j -> p (h j)"), ALU.add))
            st(dve.tensor_reduce(negmax[:, k, :], p3, AX.X, ALU.max))
            tt(p3, p3, spread(negmax[:, k, :], [P, H, S]), ALU.subtract).then_inc(s["logit_ok"], 1)

        def head_out(g, k, st):
            dve.wait_ge(s["av_ps"], GT * g + k + 1)
            u = bank[k][:, 0:136].rearrange("p (h d) -> p h d", h=H)
            st(dve.reciprocal(rden[:, k, :], u[:, :, DV]))
            tt(o[:, :].rearrange("p (h d) -> p h d", h=H), u[:, :, 0:DV],
               spread(rden[:, k, :], [P, H, DV]), ALU.mult).then_inc(s["o_ok"], 1)

        def residual(g, k):
            dve.wait_ge(s["pr_ps"], GT * g + k + 1)
            if isinstance(g, int) and g == 0:
                dve.wait_ge(s["tokb_ok"], 1)
            tt(res[:, k, :], bank[k][:, 264:264 + D], tok[:, g * GT + k, :], ALU.add).then_inc(s["res_ok"], 1)
            dve.wait_ge(s["res_ok"], GT * g + k + 1 + GT)
            dve.bn_stats(stats[:, k, :], res[:, k, :]).then_inc(s["stat_ok"], 1)
            pause(dve, s["stat_ok"], GT * g + k + 1, s["passed_dve"])
            dve.bn_aggr(mv[:, k, :], stats[:, k, :]).then_inc(s["mv_ok"], 1)

        ast = Steps(dve, s["asteps"])
        A_STEPS = 3 * GT
        def x1_out(g):
            layernorm(g, s["mv_ok"], s["rstd_ok"], res, tok[:, g4(g * GT), :], s["x1_ok"])
            dve.wait_ge(s["x1_ok"], GT * g + GT)

        def group_a(g, first, more=True):
            ast.start(g * A_STEPS)
            scores(g, 0, ast)
            if not first:
                residual(g - 1, GT - 1)
            scores(g, 1, ast)
            scores(g, 2, ast)
            head_out(g, 0, ast)
            if not first:
                x1_out(g - 1)
            head_out(g, 1, ast)
            scores(g, 3, ast)
            residual(g, 0)
            head_out(g, 2, ast)
            residual(g, 1)
            head_out(g, 3, ast)
            residual(g, 2)
            assert ast.n == A_STEPS
        group_a(0, True)
        dve.wait_ge(s["tokb_ok"], 2)
        with dve.Fori(1, NG - 1) as g:
            group_a(g, False)
        group_a(NG - 1, False, False)
        residual(NG - 1, GT - 1)
        x1_out(NG - 1)

        dve.wait_ge(s["const_p"], N_CONST)
        ist = Steps(dve, s["igsteps"])
        bst = Steps(dve, s["bsteps"])
        I_STEPS, B_STEPS = 4, 11

        def front(g, q):
            ist.start(g * I_STEPS)
            dve.wait_ge(s["flog_ok"], g + 1)
            ist(stt(logf[:, :], fpre[:, :], 0.0, flog[:, :], ALU.min, ALU.subtract))
            ist(dve.tensor_tensor_scan(cumf[:, :], one_s[:, :], logf[:, :], 0.0, ALU.mult, ALU.add))
            ist(tt(arow[:, :], ipre[:, :], cumf[:, :], ALU.subtract))
            if not (isinstance(g, int) and g < 2):
                dve.wait_ge(s["dd_ps"], GT * (g - 1))
            dve.tensor_copy(al[q][GR:2 * GR, :], arow[:, :]).then_inc(s["al_ok"], 1)
            if not (isinstance(g, int) and g < 1):
                dve.wait_ge(s["rh_ok"], 2 * g)
            ist(dve.tensor_tensor_scan(amax[:, :], zero_s[:, :], arow[:, :], -BIG, ALU.add, ALU.max))
            tt(mrow[:, :], cumf[:, :], amax[:, :], ALU.add).then_inc(s["mrow_ok"], 1)
            assert ist.n == I_STEPS

        def score(g, k):
            dve.wait_ge(s["decay_ok"], GT * g + k + 1)
            stt(cmat[:, k % 2, :], bank[3 + k % 2][:, 0:256], DH ** -0.5, decay[:, k % 2, :],
                ALU.mult, ALU.mult).then_inc(s["c_ok"], 1)

        def cell(g, q, j):
            dve.wait_ge(s["u_ps"], GT * g + 2 * j + 2)
            dve.wait_ge(s["floor_ok"], 2 * g + 2)
            u = bank[5 + j][:, 0:264].rearrange("p (n d) -> p n d", d=DH + 1)
            nv = nrm[:, 2 * j:2 * j + 2, :].rearrange("p k h -> p (k h)")
            bst(dve.tensor_reduce(nv, u[:, :, DH:DH + 1], AX.X, ALU.max, apply_absolute_value=True))
            bst(tt(nv, nv, floor[q][:, 2 * j:2 * j + 2, :].rearrange("p k h -> p (k h)"), ALU.max))
            bst(tsc(nv, nv, 1e-6, None, ALU.add))
            bst(dve.reciprocal(nv, nv))
            m = tt(hst[:, 8 * j:8 * j + 8, :], u[:, :, 0:DH], spread(nv, [P, 8, DH]), ALU.mult)
            if j == 1:
                bst(m)

        def logits_out(g):
            pause(dve, s["lg_ps"], g + 1, s["passed_dve"])
            dve.tensor_copy(lg[:, g4(g * GT), :], bank[7][:, 64:64 + GT * E].rearrange("p (k e) -> p k e", k=GT)).then_inc(s["lg_ok"], 1)

        def centre(g):
            bst(dve.tensor_reduce(hmu[:, :], hst[:, :, :], AX.X, ALU.add))
            bst(tsc(hmu[:, :], hmu[:, :], 1.0 / DH, None, ALU.mult))
            tt(hst[:, :, :], hst[:, :, :], spread(hmu[:, :], [P, GT * NH, DH]), ALU.subtract).then_inc(s["h_ok"], 1)

        def variance(g):
            dve.wait_ge(s["hsq_ok"], g + 1)
            dve.tensor_reduce(hva[:, :], hsq[:, :, :], AX.X, ALU.add).then_inc(s["hva_ok"], 1)

        def residual_b(g):
            dve.wait_ge(s["hrs_ok"], g + 1)
            dve.wait_ge(s["hlw_ok"], g + 1)
            tt(hlw[:, :, :], hlw[:, :, :], spread(hrs[:, :], [P, GT * NH, DH]), ALU.mult).then_inc(s["hn_ok"], 1)
            dve.wait_ge(s["hn_ok"], g + 1)
            h3 = hlw[:, :, :].rearrange("p (k h) d -> p k (h d)", k=GT)
            tt(res[:, :, :], h3, tok[:, g4(g * GT), :], ALU.add).then_inc(s["res1_ok"], 1)
            dve.wait_ge(s["res1_ok"], g + 1)
            for k in range(GT):
                m = dve.bn_stats(stats[:, k, :], res[:, k, :])
            m.then_inc(s["lnd_ok"], 1)
            pause(dve, s["lnd_ok"], g + 1, s["passed_dve"])
            for k in range(GT):
                dve.bn_aggr(mv[:, k, :], stats[:, k, :]).then_inc(s["mv1_ok"], 1)

        def x2_out(g, first=False):
            if not first:
                dve.wait_ge(s["x2T_ps"], g)
                dve.wait_ge(s["tk_ok"], 16 * g)
            layernorm(g, s["mv1_ok"], s["rstd1_ok"], res, x2s, s["x2_ok"])

        def group_b(g, q, before, after, second=False):
            bst.start(g * B_STEPS)
            score(g, 0)
            score(g, 1)
            if after:
                front(g + 1, 1 - q)
            if before and not second:
                logits_out(g - 2)
            if before:
                variance(g - 1)
            score(g, 2)
            score(g, 3)
            if before:
                residual_b(g - 1)
            cell(g, q, 0)
            cell(g, q, 1)
            centre(g)
            if before:
                x2_out(g - 1, second)
            assert bst.n == B_STEPS, bst.n

        front(0, 0)
        group_b(0, 0, False, True)
        group_b(1, 1, True, True, True)
        with dve.Fori(0, (NG - 4) // 2) as i:
            for n in range(2):
                group_b(2 * i + 2 + n, n, True, True)
        group_b(NG - 2, 0, True, True)
        group_b(NG - 1, 1, True, False)
        variance(NG - 1)
        residual_b(NG - 1)
        logits_out(NG - 2)
        x2_out(NG - 1)
        logits_out(NG - 1)

        r = Steps(dve, s["rsteps"])
        dve.wait_ge(s["const_p"], N_TABLES)
        dve.wait_ge(s["lg_ok"], NG)
        full = [P, NT, E]
        r(dve.tensor_reduce(m8[:, :], lg[:, :, :], AX.X, ALU.max))
        tt(lg[:, :, :], lg[:, :, :], spread(m8[:, :], full), ALU.subtract).then_inc(s["lmax_ok"], 1)
        dve.wait_ge(s["lexp_ok"], 1)
        first_expert = io_e[:, :].unsqueeze(1).broadcast_to(full)
        r(stt(cand[:, :, :], lg[:, :, :], 1.0, first_expert, ALU.is_equal, ALU.mult))
        for k in range(2):
            if k == 1:
                r(dve.tensor_reduce(gate[1][:, :], lg[:, :, :], AX.X, ALU.max))
                r(tt(cand[:, :, :], lg[:, :, :], spread(gate[1][:, :], full), ALU.is_equal))
                r(tt(cand[:, :, :], cand[:, :, :], first_expert, ALU.mult))
            r(dve.tensor_reduce(m8[:, :], cand[:, :, :], AX.X, ALU.max))
            r(tt(hot[k][:, :, :], cand[:, :, :], spread(m8[:, :], full), ALU.is_equal))
            if k == 0:
                r(dve.tensor_reduce(gate[0][:, :], lg[:, :, :], AX.X, ALU.add))
                r(stt(lg[:, :, :], hot[0][:, :, :], -2.0, lg[:, :, :], ALU.mult, ALU.add))
        tt(hotb[:, :, :], hot[0][:, :, :], hot[1][:, :, :], ALU.add).then_inc(s["hotb_ok"], 1)
        r(dve.reciprocal(gate[0][:, :], gate[0][:, :]))
        r(tt(gate[1][:, :], gate[1][:, :], gate[0][:, :], ALU.mult))
        dve.wait_ge(s["rank_ps"], 1)
        r(dve.tensor_copy(tote[:, :, :], bank[6][:, 256:512].rearrange("p (t e) -> p e t", e=E)))
        fl = lambda a: a[:, :, :].rearrange("p e t -> p (e t)")
        r(dve.tensor_tensor_scan(fl(cume), fl(segm), fl(tote), 0.0, ALU.mult, ALU.add))
        r(tt(gt[:, :, :], spread(cume[:, :, NT - 1], [P, E, NT]), io_128[:, :].unsqueeze(1).broadcast_to([P, E, NT]), ALU.is_gt))
        r(dve.tensor_reduce(ntile[:, :], gt[:, :, :], AX.X, ALU.add))
        r(dve.tensor_tensor_scan(ctile[:, :], one8[:, :], ntile[:, :], 0.0, ALU.mult, ALU.add))
        r(tt(cume[:, :, :], cume[:, :, :], tote[:, :, :], ALU.subtract))
        r(tt(sl[:, :, :], bank[6][:, 0:256].rearrange("p (t e) -> p t e", e=E), cume[:, :, :].rearrange("p e t -> p t e"), ALU.add))
        r(tt(ntile[:, :], ctile[:, :], ntile[:, :], ALU.subtract))
        r(stt(sl[:, :, :], ntile[:, :].unsqueeze(1).broadcast_to(full), float(P), sl[:, :, :], ALU.mult, ALU.add))
        for k in range(2):
            r(tt(cand[:, :, :], sl[:, :, :], hot[k][:, :, :], ALU.mult))
            r(dve.tensor_reduce(slotf[:, :], cand[:, :, :], AX.X, ALU.add))
            r(dve.tensor_copy(slot[k][:, :], slotf[:, :]))

        def stage(i, n, t, k, first):
            if not first:
                pause(dve, scat[n], 16 * i, s["passed_dve"])
            dve.tensor_copy(stg[n][:, 0:D], tok[:, t, :])
            dve.tensor_copy(stg[n][:, GATE:GATE + 1], gate[k][:, bass.ds(t, 1)])
            dve.tensor_copy(stg[n][:, :].bitcast(I32)[:, DEST:DEST + 1], dest[:, k, bass.ds(t, 1)])
            dve.tensor_copy(idx[n][:, :], slot[k][:, bass.ds(t, 1)]).then_inc(s["stage_ok"], 1)

        def two_groups(i, first):
            for a in range(2):
                g = 2 * i + a
                for n in range(2 * GT):
                    stage(2 * g + n // 4, n % 4, g * GT + n // 2, n % 2, first and a == 0 and n < 4)
                dve.wait_ge(s["shd_ps"], g + 1)
                dve.wait_ge(s["stage_ok"], 2 * GT * (g + 1))
                tg = tok[:, g4(g * GT), :]
                stt(tg, tg, 2.0, bank[4 + a][:, :].rearrange("p (k d) -> p k d", k=GT),
                    ALU.mult, ALU.add).then_inc(s["base_ok"], 1)
        dve.wait_ge(s["tk_ok"], 16 * NG)
        two_groups(0, True)
        with dve.Fori(1, NG // 2) as i:
            two_groups(i, False)
        r(tt(tcmp[:, :, :], ctile[0:1, :].unsqueeze(1).broadcast_to([1, SLOT_TILES, E]),
             spread(io_tau[:, :], [1, SLOT_TILES, E]), ALU.is_le))
        r(dve.tensor_reduce(texp[:, :], tcmp[:, :, :], AX.X, ALU.add))
        r(tsc(texp[:, :], texp[:, :], float(E - 1), None, ALU.min))
        dve.tensor_copy(texpi[:, :], texp[:, :]).then_inc(s["texp_ok"], 1)

        def x_out(t, n):
            dve.wait_ge(s["xr_ps"], t + 1)
            dve.tensor_copy(xrT[:, n % 2, :], bank[n % 2][:, 0:P]).then_inc(s["xrT_ok"], 1)

        def w_out(t, n):
            e = dve.value_load(texpi[0:1, bass.ds(t, 1)], min_val=0, max_val=E - 1)
            if not (isinstance(t, int) and t < 2):
                pause(dve, s["up_ps"], t - 1, s["passed_dve"])
            dve.tensor_copy(wst[:, n % 2, :], wup[:, bass.ds(e * FF, FF)]).then_inc(s["wst_ok"], 1)

        def y_out(t, n, times):
            dve.wait_ge(s["y_ps"], t + 1)
            if not (isinstance(t, int) and t < 4):
                dve.wait_ge(sc_y[n % 4], 16 * times)
            tsc(yr[n % 4][:, :], bank[6 + n % 2][:, 0:D], xr[n % NX][:, GATE:GATE + 1], None,
                ALU.mult).then_inc(s["y_ok"], 1)

        def step(t, n, i):
            known = isinstance(t, int)
            if not known or t < SLOT_TILES:
                w_out(t, n)
                x_out(t, n)
            if not known or (t >= 2 and t - 2 < SLOT_TILES):
                y_out(t - 2, n - 2, (t - 2) // 4 if known else 2 * i + (n - 2) // 4)
        dve.wait_ge(s["ld_wup"], 16)
        dve.wait_ge(s["texp_ok"], 1)
        for t in range(NX):
            step(t, t, 0)
        with dve.Fori(1, SLOT_TILES // NX) as i:
            for n in range(NX):
                step(i * NX + n, n, i)
        for t in range(SLOT_TILES, SLOT_TILES + 2):
            step(t, t, 0)

        def totals(g, n, i):
            dve.wait_ge(ld_y1[n], 16 * (i + 1))
            dve.wait_ge(s["presum_ok"], g + 1)
            yg = y1[:, g4(g * GT), :]
            tt(yg, yg, y0[:, g4(g * GT), :], ALU.add).then_inc(s["res1_ok"], 1)
            dve.wait_ge(s["res1_ok"], NG + g + 1)
            for k in range(GT):
                m = dve.bn_stats(stats[:, k, :], y1[:, g * GT + k, :])
            m.then_inc(s["stat_ok"], 1)
            if not (isinstance(g, int) and g < NY):
                dve.wait_ge(s["fin_ok"], g - NY + 1)
            pause(dve, s["stat_ok"], NT + g + 1, s["passed_dve"])
            for k in range(GT):
                dve.bn_aggr(mvf[n][:, k, :], stats[:, k, :]).then_inc(s["mv2_ok"], 1)

        def shifts(g, n):
            dve.wait_ge(s["rstd2_ok"], g + 1)
            dve.wait_ge(s["mv2_ok"], GT * g + GT)
            stt(shift[n][:, :], mvf[n][:, :, 0], -1.0, rstdf[n][:, :], ALU.mult, ALU.mult).then_inc(s["shift_ok"], 1)
        totals(0, 0, 0)
        for n in range(1, NY):
            totals(n, n, 0)
            shifts(n - 1, (n - 1) % NY)
        with dve.Fori(1, NG // NY) as i:
            for n in range(NY):
                totals(NY * i + n, n, i)
                shifts(NY * i + n - 1, (n - 1) % NY)
        shifts(NG - 1, NY - 1)

    es.close()


_INS = ['x', 'ctx_1024', 'L0_attn_W_qk', 'L0_attn_W_v', 'L0_attn_W_out', 'L0_attn_b_out', 'L0_attn_conv',
        'L0_xattn_w_igate', 'L0_xattn_b_igate', 'L0_xattn_w_fgate', 'L0_xattn_b_fgate', 'L0_xattn_ln_weight',
        'L0_ffn_shared_up', 'L0_ffn_shared_down', 'L0_ffn_routed_up', 'L0_ffn_routed_down', 'L0_ffn_router_w']


def kernel(**inputs):
    import numpy as _np
    import concourse.bacc as _bacc
    from concourse import mybir as _mybir
    from concourse.bass_utils import run_bass_kernel_spmd as _run

    nc = _bacc.Bacc("TRN2", target_bir_lowering=False, num_devices=1)
    arrays, args = {}, []
    for name in _INS:
        a = _np.ascontiguousarray(inputs[name])
        arrays[f"in_{name}"] = a
        args.append(nc.dram_tensor(f"in_{name}", a.shape, _mybir.dt.from_np(a.dtype), kind="ExternalInput").ap())
    out = nc.dram_tensor("out_x", (64, 64, 128), _mybir.dt.float32, kind="ExternalOutput").ap()
    decoder_layer(nc, *args, out)
    r = _run(nc, [arrays], core_ids=[0])
    return r.results[0]["out_x"]
```
